# Optimizing a Trainium2 kernel written in Bass

```python
import numpy as np
import jax
import jax.numpy as jnp

def _softmax(x, axis=-1):
    return jax.nn.softmax(x, axis=axis)

def _gelu(x):
    return jax.nn.gelu(x, approximate=True)

def _silu(x):
    return jax.nn.silu(x)

def _sigmoid(x):
    return jax.nn.sigmoid(x)

def _layernorm(x, axis=-1, eps=1e-05):
    m = jnp.mean(x, axis=axis, keepdims=True)
    v = jnp.var(x, axis=axis, keepdims=True)
    return (x - m) / jnp.sqrt(v + eps)

def _scatter_add(tgt, idx, src, axis=0):
    return tgt.at[idx].add(src)

def _segment_sum(src, seg, n):
    return jax.ops.segment_sum(src, seg, n)
kernel_name = 'mk_xattn_ffn_d2_seqx_r4_a03c29'

def setup_inputs(seed: int=0):
    np.random.seed(seed)
    _w = jnp.asarray

    def _rec_inputs():
        import jax
        import jax.numpy as jnp
        _rk = jax.random.key(seed)
        x = -0.0005207 + 1.001 * jax.random.normal(jax.random.fold_in(_rk, 1), (32, 128, 256), jnp.float32)
        _lenS = 128 - jax.random.randint(jax.random.fold_in(_rk, 7), (32,), 0, max(1, 128 // 4) + 1, jnp.int32)
        _lenS2 = 128 - jax.random.randint(jax.random.fold_in(_rk, 8), (32,), 0, max(1, 128 // 4) + 1, jnp.int32)
        _ctx_1024P = jax.random.normal(jax.random.fold_in(_rk, 11), (32, 16, 256), jnp.float32)
        _ctx_1024c = jax.random.dirichlet(jax.random.fold_in(_rk, 511), 0.3 * jnp.ones((16,), jnp.float32), (32, 128))
        _ctx_1024t = jnp.einsum('bsk,bkd->bsd', _ctx_1024c, _ctx_1024P)
        _ctx_1024t = _ctx_1024t * jax.lax.rsqrt(jnp.mean(jnp.square(_ctx_1024t)) + 1e-12) * 0.953939
        ctx_1024 = -0.000514642 + 1.00011 * (_ctx_1024t + 0.3 * jax.random.normal(jax.random.fold_in(_rk, 611), (32, 128, 256), jnp.float32))
        _validS = jnp.arange(128)[None, :] < _lenS[:, None]
        _validS2 = jnp.arange(128)[None, :] < _lenS2[:, None]
        _causal = jnp.tril(jnp.ones((128, 128), dtype=bool))
        mask_1x1xSxS2_ik1 = jnp.where(jnp.broadcast_to(_validS2[0:1, None, None, :], (1, 1, 128, 128)), 1, 0).astype(jnp.int32)
        return (x, ctx_1024, mask_1x1xSxS2_ik1)
    x, ctx_1024, mask_1x1xSxS2_ik1 = _rec_inputs()

    def _L0_xattn_setup():
        import jax, jax.numpy as jnp
        import numpy as np
        D_MODEL = 256
        FFN = 1024
        E = 8
        K = 2
        B, S = (4, 128)
        key = jax.random.key(seed)
        ks = jax.random.split(key, 8)
        scale_in = 1.0 / np.sqrt(D_MODEL)
        scale_ffn = 1.0 / np.sqrt(FFN)
        return {'x': jax.random.normal(ks[0], (B, S, D_MODEL), jnp.float32), 'context': jax.random.normal(ks[1], (B, S, D_MODEL), jnp.float32), 'Wg': jax.random.normal(ks[2], (D_MODEL, E), jnp.float32) * scale_in, 'bg': jnp.zeros((E,), jnp.float32), 'W1': jax.random.normal(ks[3], (E, D_MODEL, FFN), jnp.float32) * scale_in, 'b1': jnp.zeros((E, FFN), jnp.float32), 'W2': jax.random.normal(ks[4], (E, FFN, D_MODEL), jnp.float32) * scale_ffn, 'b2': jnp.zeros((E, D_MODEL), jnp.float32)}
    _L0_xattn_all = _L0_xattn_setup()
    _L0_xattn_in = {k: v for k, v in _L0_xattn_all.items() if k in ('Wg', 'bg', 'W1', 'b1', 'W2', 'b2')}
    del _L0_xattn_all

    def _L0_ffn_setup():
        import jax, jax.numpy as jnp
        import numpy as np
        key = jax.random.key(seed)
        ks = jax.random.split(key, 5)
        B, Sq, M, E, H = (4, 512, 256, 8, 1024)
        x = jax.random.normal(ks[0], (B, Sq, M), dtype=jnp.float32)
        wg = jax.random.normal(ks[1], (M, E), dtype=jnp.float32) * (1.0 / np.sqrt(M))
        w1 = jax.random.normal(ks[2], (E, M, H), dtype=jnp.float32) * (1.0 / np.sqrt(M))
        b1 = jnp.zeros((E, H), dtype=jnp.float32)
        w2 = jax.random.normal(ks[3], (E, H, M), dtype=jnp.float32) * (1.0 / np.sqrt(H))
        b2 = jnp.zeros((E, M), dtype=jnp.float32)
        return {'x': x, 'wg': wg, 'w1': w1, 'b1': b1, 'w2': w2, 'b2': b2}
    _L0_ffn_all = _L0_ffn_setup()
    _L0_ffn_in = {k: v for k, v in _L0_ffn_all.items() if k in ('wg', 'w1', 'b1', 'w2', 'b2')}
    del _L0_ffn_all

    def _L1_xattn_setup():
        import jax, jax.numpy as jnp
        import numpy as np
        D_MODEL = 256
        H = 16
        D_K = D_MODEL // H
        key = jax.random.key(seed)
        ks = jax.random.split(key, 12)
        B, S = (2, 512)
        inp = {'q': jax.random.normal(ks[0], (B, S, D_MODEL), jnp.float32), 'k': jax.random.normal(ks[1], (B, S, D_MODEL), jnp.float32), 'v': jax.random.normal(ks[2], (B, S, D_MODEL), jnp.float32), 'mask': jax.random.randint(ks[3], (1, 1, S, S), 0, 2, jnp.int32)}
        s = 1.0 / np.sqrt(D_MODEL)
        inp['wq_w'] = jax.random.normal(ks[4], (D_MODEL, D_MODEL), jnp.float32) * s
        inp['wq_b'] = jnp.zeros((D_MODEL,), jnp.float32)
        inp['wk_w'] = jax.random.normal(ks[5], (D_MODEL, D_MODEL), jnp.float32) * s
        inp['wk_b'] = jnp.zeros((D_MODEL,), jnp.float32)
        inp['wv_w'] = jax.random.normal(ks[6], (D_MODEL, D_MODEL), jnp.float32) * s
        inp['wv_b'] = jnp.zeros((D_MODEL,), jnp.float32)
        inp['wo_w'] = jax.random.normal(ks[7], (D_MODEL, D_MODEL), jnp.float32) * s
        inp['wo_b'] = jnp.zeros((D_MODEL,), jnp.float32)
        return inp
    _L1_xattn_all = _L1_xattn_setup()
    _L1_xattn_in = {k: v for k, v in _L1_xattn_all.items() if k in ('wq_w', 'wq_b', 'wk_w', 'wk_b', 'wv_w', 'wv_b', 'wo_w', 'wo_b')}
    del _L1_xattn_all

    def _L1_ffn_setup():
        import jax, jax.numpy as jnp
        import numpy as np
        BLOCK = 32
        W_BITS = 4
        ACT_BITS = 16

        def act_qdq(x):
            qmax = 2.0 ** (ACT_BITS - 1) - 1.0
            scale = jnp.maximum(jnp.max(jnp.abs(x)) / qmax, 1e-12)
            return jnp.clip(jnp.round(x / scale), -qmax - 1.0, qmax) * scale

        def fixed_qdq_u16(x):
            scale = 1.0 / 65536.0
            return jnp.clip(jnp.round(x / scale), 0.0, 65535.0) * scale

        def lpbq_dequant(w):
            O, I = w.shape
            qmax = 2.0 ** (W_BITS - 1) - 1.0
            wb = w.reshape(O, I // BLOCK, BLOCK)
            s = jnp.maximum(jnp.max(jnp.abs(wb), axis=-1, keepdims=True) / qmax, 1e-12)
            wq = jnp.clip(jnp.round(wb / s), -qmax - 1.0, qmax) * s
            return wq.reshape(O, I)
        key = jax.random.key(seed)
        k1, k2, k3, k4 = jax.random.split(key, 4)
        B, S, H, I = (2, 1024, 256, 768)
        x = jax.random.normal(k1, (B, S, H), jnp.float32)
        w_gate = jax.random.normal(k2, (I, H), jnp.float32) * 0.02
        w_up = jax.random.normal(k3, (I, H), jnp.float32) * 0.02
        w_down = jax.random.normal(k4, (H, I), jnp.float32) * 0.02
        return {'x': x, 'w_gate': w_gate, 'w_up': w_up, 'w_down': w_down}
    _L1_ffn_all = _L1_ffn_setup()
    _L1_ffn_in = {k: v for k, v in _L1_ffn_all.items() if k in ('w_gate', 'w_up', 'w_down')}
    del _L1_ffn_all
    return {'x': x, 'ctx_1024': ctx_1024, 'mask_1x1xSxS2_ik1': mask_1x1xSxS2_ik1, 'L0_xattn_Wg': _L0_xattn_in['Wg'], 'L0_xattn_bg': _L0_xattn_in['bg'], 'L0_xattn_W1': _L0_xattn_in['W1'], 'L0_xattn_b1': _L0_xattn_in['b1'], 'L0_xattn_W2': _L0_xattn_in['W2'], 'L0_xattn_b2': _L0_xattn_in['b2'], 'L0_ffn_wg': _L0_ffn_in['wg'], 'L0_ffn_w1': _L0_ffn_in['w1'], 'L0_ffn_b1': _L0_ffn_in['b1'], 'L0_ffn_w2': _L0_ffn_in['w2'], 'L0_ffn_b2': _L0_ffn_in['b2'], 'L1_xattn_wq_w': _L1_xattn_in['wq_w'], 'L1_xattn_wq_b': _L1_xattn_in['wq_b'], 'L1_xattn_wk_w': _L1_xattn_in['wk_w'], 'L1_xattn_wk_b': _L1_xattn_in['wk_b'], 'L1_xattn_wv_w': _L1_xattn_in['wv_w'], 'L1_xattn_wv_b': _L1_xattn_in['wv_b'], 'L1_xattn_wo_w': _L1_xattn_in['wo_w'], 'L1_xattn_wo_b': _L1_xattn_in['wo_b'], 'L1_ffn_w_gate': _L1_ffn_in['w_gate'], 'L1_ffn_w_up': _L1_ffn_in['w_up'], 'L1_ffn_w_down': _L1_ffn_in['w_down']}

def reference(x, ctx_1024, mask_1x1xSxS2_ik1, L0_xattn_Wg, L0_xattn_bg, L0_xattn_W1, L0_xattn_b1, L0_xattn_W2, L0_xattn_b2, L0_ffn_wg, L0_ffn_w1, L0_ffn_b1, L0_ffn_w2, L0_ffn_b2, L1_xattn_wq_w, L1_xattn_wq_b, L1_xattn_wk_w, L1_xattn_wk_b, L1_xattn_wv_w, L1_xattn_wv_b, L1_xattn_wo_w, L1_xattn_wo_b, L1_ffn_w_gate, L1_ffn_w_up, L1_ffn_w_down):
    import jax
    import jax.numpy as jnp

    def _L0_xattn_ref(x, context, Wg, bg, W1, b1, W2, b2):
        import jax, jax.numpy as jnp
        import numpy as np
        D_MODEL = 256
        FFN = 1024
        E = 8
        K = 2
        B, S = (4, 128)
        logits = jnp.einsum('bsd,de->bse', context, Wg) + bg
        scores_topk, idx_topk = jax.lax.top_k(logits, K)
        weights = jax.nn.softmax(scores_topk, axis=-1)
        combine = jnp.sum(jax.nn.one_hot(idx_topk, E, dtype=weights.dtype) * weights[..., None], axis=-2)
        h = jax.nn.relu(jnp.einsum('bsd,edf->bsef', x, W1) + b1)
        y = jnp.einsum('bsef,efd->bsed', h, W2) + b2
        out = jnp.einsum('bsed,bse->bsd', y, combine)
        return out

    def _L0_ffn_ref(x, wg, w1, b1, w2, b2):
        import jax, jax.numpy as jnp
        import numpy as np
        B, Sq, M = x.shape
        E = wg.shape[1]
        S = B * Sq
        C = S // E
        xt = x.reshape(S, M)
        gates = jax.nn.softmax(xt @ wg, axis=-1)
        expert_idx = jnp.argmax(gates, axis=-1)
        mask1 = jax.nn.one_hot(expert_idx, E, dtype=xt.dtype)
        locations = jnp.cumsum(mask1, axis=0) - 1.0
        pos = jnp.sum(locations * mask1, axis=1).astype(jnp.int32)
        keep = (pos < C).astype(xt.dtype)
        gate_val = jnp.sum(gates * mask1, axis=1) * keep
        slot = expert_idx.astype(jnp.int32) * C + jnp.clip(pos, 0, C - 1)
        disp = jnp.zeros((E * C, M), dtype=xt.dtype).at[slot].add(xt * keep[:, None])
        disp = disp.reshape(E, C, M)
        h = jax.nn.relu(jnp.einsum('ecm,emh->ech', disp, w1) + b1[:, None, :])
        eo = jnp.einsum('ech,ehm->ecm', h, w2) + b2[:, None, :]
        out = eo.reshape(E * C, M)[slot] * gate_val[:, None]
        return out.reshape(B, Sq, M)

    def _L1_xattn_ref(q, k, v, mask, wq_w, wq_b, wk_w, wk_b, wv_w, wv_b, wo_w, wo_b):
        import jax, jax.numpy as jnp
        import numpy as np
        D_MODEL = 256
        H = 16
        D_K = D_MODEL // H
        B, S, _ = q.shape

        def proj(x, w, b):
            y = x @ w.T + b
            return y.reshape(B, S, H, D_K).transpose(0, 2, 1, 3)
        Q = proj(q, wq_w, wq_b)
        K = proj(k, wk_w, wk_b)
        V = proj(v, wv_w, wv_b)
        scores = jnp.einsum('bhqd,bhkd->bhqk', Q, K) / jnp.sqrt(jnp.float32(D_K))
        scores = jnp.where(mask == 0, jnp.float32(1e-09), scores)
        attn = jax.nn.softmax(scores, axis=-1)
        out = jnp.einsum('bhqk,bhkd->bhqd', attn, V)
        out = out.transpose(0, 2, 1, 3).reshape(B, S, H * D_K)
        return out @ wo_w.T + wo_b

    def _L1_ffn_ref(x, w_gate, w_up, w_down):
        import jax, jax.numpy as jnp
        import numpy as np
        BLOCK = 32
        W_BITS = 4
        ACT_BITS = 16

        def act_qdq(x):
            qmax = 2.0 ** (ACT_BITS - 1) - 1.0
            scale = jnp.maximum(jnp.max(jnp.abs(x)) / qmax, 1e-12)
            return jnp.clip(jnp.round(x / scale), -qmax - 1.0, qmax) * scale

        def fixed_qdq_u16(x):
            scale = 1.0 / 65536.0
            return jnp.clip(jnp.round(x / scale), 0.0, 65535.0) * scale

        def lpbq_dequant(w):
            O, I = w.shape
            qmax = 2.0 ** (W_BITS - 1) - 1.0
            wb = w.reshape(O, I // BLOCK, BLOCK)
            s = jnp.maximum(jnp.max(jnp.abs(wb), axis=-1, keepdims=True) / qmax, 1e-12)
            wq = jnp.clip(jnp.round(wb / s), -qmax - 1.0, qmax) * s
            return wq.reshape(O, I)
        x = act_qdq(x)
        up = act_qdq(x @ lpbq_dequant(w_up).T)
        gate = act_qdq(x @ lpbq_dequant(w_gate).T)
        sig = fixed_qdq_u16(jax.nn.sigmoid(gate))
        gate = act_qdq(gate * sig)
        o = act_qdq(gate * up)
        return o @ lpbq_dequant(w_down).T
    x = x + _L0_xattn_ref(_layernorm(x, axis=-1), ctx_1024, L0_xattn_Wg, L0_xattn_bg, L0_xattn_W1, L0_xattn_b1, L0_xattn_W2, L0_xattn_b2)
    x = x + _L0_ffn_ref(_layernorm(x, axis=-1), L0_ffn_wg, L0_ffn_w1, L0_ffn_b1, L0_ffn_w2, L0_ffn_b2)
    x = x + _L1_xattn_ref(_layernorm(x, axis=-1), ctx_1024, ctx_1024, mask_1x1xSxS2_ik1, L1_xattn_wq_w, L1_xattn_wq_b, L1_xattn_wk_w, L1_xattn_wk_b, L1_xattn_wv_w, L1_xattn_wv_b, L1_xattn_wo_w, L1_xattn_wo_b)
    x = x + _L1_ffn_ref(_layernorm(x, axis=-1), L1_ffn_w_gate, L1_ffn_w_up, L1_ffn_w_down)
    return x

_drawn_inputs = setup_inputs


def setup_inputs(seed=0):
    import zlib

    import numpy as np

    out = dict(_drawn_inputs(seed))
    spreads = {'L0_xattn_bg': (0.0, 0.1),
     'L0_xattn_b1': (0.0, 0.1),
     'L0_xattn_b2': (0.0, 0.1),
     'L0_ffn_b1': (0.0, 0.372),
     'L0_ffn_b2': (0.0, 0.267),
     'L1_xattn_wq_b': (0.0, 0.405),
     'L1_xattn_wk_b': (0.0, 0.8),
     'L1_xattn_wv_b': (0.0, 0.1),
     'L1_xattn_wo_b': (0.0, 0.1)}
    factors = {}
    for name, (base, spread) in spreads.items():
        noise = np.random.default_rng([zlib.crc32(name.encode()), seed]).standard_normal(out[name].shape)
        drawn = base * np.exp(spread * noise) if base else spread * noise
        out[name] = jnp.asarray(drawn.astype(out[name].dtype))
    for name, factor in factors.items():
        out[name] = (out[name] * factor).astype(out[name].dtype)
    return out
```

```python
import concourse.bass as bass
from concourse import mybir
from contextlib import ExitStack, contextmanager

F32 = mybir.dt.float32
F16 = mybir.dt.float16
I32 = mybir.dt.int32
ALU = mybir.AluOpType
ACT = mybir.ActivationFunctionType
AX_X = mybir.AxisListType.X
P = 128
WEIGHT_SCALE = 64.0
ROUND = 1.5 * 2.0**23
EPS = 1e-05


@contextmanager
def stage_semaphores(nc, name):
    held = []

    def sem(n):
        held.append(nc.alloc_semaphore(name=f"{name}_{n}"))
        return held[-1]

    yield sem
    nc.clear_and_free_semaphores(held)
    nc.all_engine_barrier()


class Order:

    def __init__(self, engine, semaphore):
        self.engine, self.semaphore, self.count = engine, semaphore, 0

    def __call__(self, instruction):
        instruction.then_inc(self.semaphore, 1)
        self.count = self.count + 1
        self.engine.wait_ge(self.semaphore, self.count)

    def tick(self, instruction):
        instruction.then_inc(self.semaphore, 1)
        self.count = self.count + 1

    def wait(self):
        self.engine.wait_ge(self.semaphore, self.count)


def free(engine, semaphore, value):
    if not (isinstance(value, int) and value <= 0):
        engine.wait_ge(semaphore, value)


def each(engine, n, body):
    body(0)
    with engine.Fori(1, n) as m:
        body(m)


def layernorm_scales(dve, order, x_all, stats, mean_var, var, rstd, rtmp, s_var, s_root):
    V = dve
    T = x_all.shape[1]
    for t in range(T):
        order.tick(V.bn_stats(stats[:, t, :], x_all[:, t, :]))
    order.wait()
    for t in range(T):
        order.tick(V.bn_aggr(mean_var[:, t, :], stats[:, t, :]))
    order.wait()
    V.tensor_scalar(var[:], mean_var[:, :, 1], EPS, None, ALU.add).then_inc(s_var, 1)
    dve.wait_ge(s_root, 1)
    order(V.reciprocal(rstd[:], rstd[:]))
    order(V.tensor_tensor(rtmp[:], rstd[:], rstd[:], ALU.mult))
    order(V.tensor_tensor(rtmp[:], rtmp[:], var[:], ALU.mult))
    order(V.tensor_scalar(rtmp[:], rtmp[:], -0.5, 1.5, ALU.mult, ALU.add))
    order(V.tensor_tensor(rstd[:], rstd[:], rtmp[:], ALU.mult))


def broadcast_rows(ap, rows, n):
    return bass.AP(tensor=ap.tensor, offset=ap.offset, ap=[[0, rows], [1, n]])


def experts(nc, name, x, gate_source, wg, bg, w1, b1, w2, b2, x_sum, normed, choices, capacity):
    tokens, D = x.shape
    E = wg.shape[1]
    F = w1.shape[2]
    T, DC, FC = tokens // P, D // P, F // P
    if capacity is None:
        NS = (choices * tokens + E * (P - 1)) // P
        NS += -NS % 2
    else:
        NS = E * capacity // P
    CHUNK = 1024
    CPE = 2 * DC * F // CHUNK
    assert DC * F == FC * D and CPE == 4 and DC == 2 and FC == 8
    GC = 2

    with ExitStack() as ctx:
        sem = ctx.enter_context(stage_semaphores(nc, name))

        def sb(n, shape, dt):
            return ctx.enter_context(nc.sbuf_tensor(f"{name}_{n}", shape, dt))

        def pb(n, shape, dt):
            return ctx.enter_context(nc.psum_tensor(f"{name}_{n}", shape, dt))


        w_hi = sb("w_hi", [P, E, CPE, CHUNK], F16)
        w_lo = sb("w_lo", [P, E, CPE, CHUNK], F16)
        staged = [sb(f"staged{c}", [P, CHUNK], F32) for c in range(CPE)]
        x_all = sb("x_all", [P, T, D], F32)
        flat = x_all[:].rearrange("p t d -> p (t d)")
        h32 = [flat[:, p * F:(p + 1) * F] for p in range(2)]
        halves = flat[:, 2 * F:4 * F].bitcast(F16)
        h_hi = [halves[:, p * F:(p + 1) * F].rearrange("p (c t) -> p c t", c=FC) for p in range(2)]
        h_lo = [halves[:, (2 + p) * F:(3 + p) * F].rearrange("p (c t) -> p c t", c=FC) for p in range(2)]
        xg = [flat[:, 4 * F + p * D:4 * F + (p + 1) * D] for p in range(2)]
        y = [flat[:, 4 * F + (2 + p) * D:4 * F + (3 + p) * D] for p in range(2)]
        xT_hi = [sb(f"xT_hi{p}", [P, DC, P], F16) for p in range(2)]
        xT_lo = [sb(f"xT_lo{p}", [P, DC, P], F16) for p in range(2)]
        gate_in = [sb(f"gate_in{p}", [P, GC, D], F32) for p in range(2)]
        gateT = [sb(f"gateT{p}", [P, DC, P], F32) for p in range(2)]
        b1_rows = sb("b1_rows", [E * FC, P], F32)
        b1T = sb("b1T", [P, E * FC], F32)
        b2_all = sb("b2_all", [P, E, D], F32)
        wg_sb = sb("wg_sb", [P, DC, E], F32)
        bg_sb = sb("bg_sb", [P, E], F32)
        ident = sb("ident", [P, P], F32)
        before = sb("before", [P, P], F16)
        ones = sb("ones", [P, P], F16)
        expert_no = sb("expert_no", [P, E], F32)
        lane_no = sb("lane_no", [P, P], F32)
        pad_row = sb("pad_row", [P, 1], F32)
        token_1 = sb("token_1", [P, T], F32)
        stats = sb("stats", [P, T, 6], F32)
        mean_var = sb("mean_var", [P, T, 2], F32)
        rstd = sb("rstd", [P, T], F32)
        rtmp = sb("rtmp", [P, T], F32)
        logits = sb("logits", [P, T, E], F32)
        work = sb("work", [P, T, E], F32)
        onehot = [sb(f"onehot{c}", [P, T, E], F32) for c in range(choices)]
        oh16 = sb("oh16", [P, T, E], F16)
        best = [sb(f"best{c}", [P, T], F32) for c in range(choices)]
        first = sb("first", [P, T], F32)
        weight = [sb(f"weight{c}", [P, T], F32) for c in range(choices)]
        total = sb("total", [P, E, T], F32)
        running = sb("running", [P, E, T], F32)
        one_t = sb("one_t", [P, T], F32)
        tiles_of = sb("tiles_of", [P, E], F32)
        start_of = sb("start_of", [P, E], F32)
        ends_of = sb("ends_of", [P, E], F32)
        slot_div = [sb(f"slot_div{c}", [P, T], F32) for c in range(choices)]
        slot_mod = [sb(f"slot_mod{c}", [P, T], F32) for c in range(choices)]
        pick_lane = [sb(f"pick_lane{p}", [P, P], F32) for p in range(2)]
        pick_tile = [sb(f"pick_tile{p}", [P, 2, NS], F32) for p in range(2)]
        row_f = sb("row_f", [P, NS], F32)
        pad_f = sb("pad_f", [P, NS], F32)
        row_of_slot = sb("row_of_slot", [P, NS], I32)
        weight_of_slot = sb("weight_of_slot", [P, NS], F32)
        expert_f = sb("expert_f", [P, NS], F32)
        expert_of_tile = sb("expert_of_tile", [P, NS], I32)
        rows_in = [sb(f"rows_in{p}", [P, 1], I32) for p in range(2)]
        rows_out = [sb(f"rows_out{p}", [P, 1], I32) for p in range(2)]

        xT_ps = [pb(f"xT_ps{p}", [P, 512], F32) for p in range(2)]
        h_ps = [pb(f"h_ps{p}", [P, 2, 512], F32) for p in range(2)]
        y_ps = [pb(f"y_ps{p}", [P, 512], F32) for p in range(2)]

        s_x = [sem(f"x_quarter{q}_loaded") for q in range(4)]; s_small = sem("small_loaded"); s_gate_in = [sem(f"gate_in{p}_loaded") for p in range(2)]
        s_staged = [sem(f"staged{c}_loaded") for c in range(CPE)]
        s_hi = sem("w_hi_done"); s_split = sem("w_split")
        s_const = sem("constants"); s_pool = sem("pool_order"); s_dve = sem("dve_order"); s_act = sem("act_order")
        s_var = sem("variances"); s_root = sem("roots"); s_normed = sem("normed"); s_stored = sem("normed_stored"); s_begun = sem("x_sum_begun")
        s_go = sem("pool_goes_on")
        s_b1 = sem("b1_transposed"); s_b1T = sem("b1T_ready")
        s_tr = [sem(f"gate_transposed{p}") for p in range(2)]; s_trc = [sem(f"gateT{p}_ready") for p in range(2)]
        s_lg = [sem(f"logits_from{p}") for p in range(2)]
        s_diff = sem("exp_in"); s_exp = sem("exp_out")
        s_oh = sem("onehots"); s_count = sem("counts")
        s_pick = [sem(f"picks{p}_ready") for p in range(2)]; s_picked = [sem(f"picks{p}_used") for p in range(2)]
        s_table = sem("tables_ready")
        s_rows_in = [sem(f"rows_in{p}_copied") for p in range(2)]; s_rows_out = [sem(f"rows_out{p}_copied") for p in range(2)]
        s_xg = [sem(f"xg{p}_gathered") for p in range(2)]; s_xt = [sem(f"xT{p}_transposed") for p in range(2)]
        s_xh = [sem(f"xT_hi{p}_ready") for p in range(2)]; s_xl = [sem(f"xT_lo{p}_ready") for p in range(2)]
        s_h = [sem(f"h{p}_banks") for p in range(2)]; s_h32 = [sem(f"h32_{p}_ready") for p in range(2)]
        s_hh = [sem(f"h_hi{p}_ready") for p in range(2)]; s_hl = [sem(f"h_lo{p}_ready") for p in range(2)]
        s_l2 = [sem(f"y_ps{p}_ready") for p in range(2)]; s_yb = [sem(f"y{p}_biased") for p in range(2)]; s_y = [sem(f"y{p}_ready") for p in range(2)]
        s_added = [sem(f"y{p}_added") for p in range(2)]

        M = NS // 2
        HEAD = 4
        block = ctx.enter_context(nc.Block())

        @block.sync
        def _(sp):
            x_tiles = x.rearrange("(t p) d -> p t d", p=P)
            for q in range(4):
                n = T // 4
                sp.dma_start(x_all[:, q * n:(q + 1) * n, :], x_tiles[:, q * n:(q + 1) * n, :]).then_inc(s_x[q], 16)
            sp.dma_start(wg_sb[:], wg.rearrange("(c p) e -> p c e", p=P)).then_inc(s_small, 16)
            if bg is not None:
                sp.dma_start(bg_sb[:], broadcast_rows(bg, P, E)).then_inc(s_small, 16)
            sp.dma_start(b1_rows[:], b1.rearrange("e (c f) -> (e c) f", f=P)).then_inc(s_small, 16)
            sp.dma_start(b2_all[:].rearrange("p e d -> p (e d)"), broadcast_rows(b2, P, E * D)).then_inc(s_small, 16)

            def load_expert(e):
                w1_e = w1[e].rearrange("(c p) f -> p c f", p=P)
                w2_e = w2[e].rearrange("(c p) d -> p c d", p=P)
                for c in range(CPE):
                    if not (isinstance(e, int) and e == 0):
                        sp.wait_ge(s_split, (e - 1) * CPE + c + 1)
                    if c < 2:
                        sp.dma_start(staged[c][:], w1_e[:, c, :]).then_inc(s_staged[c], 16)
                    else:
                        sp.dma_start(staged[c][:].rearrange("p (c d) -> p c d", d=D),
                                     w2_e[:, (c - 2) * 4:(c - 1) * 4, :]).then_inc(s_staged[c], 16)

            if gate_source is not None:
                g_tiles = gate_source.rearrange("(t p) d -> p t d", p=P)
                for p in range(2):
                    sp.dma_start(gate_in[p][:], g_tiles[:, p * GC:(p + 1) * GC, :]).then_inc(s_gate_in[p], 16)
                load_expert(0)
                with sp.Fori(1, T // GC // 2) as m:
                    for p in range(2):
                        for k in range(GC):
                            sp.wait_ge(s_tr[k], 2 * m - 1 + p)
                        sp.dma_start(gate_in[p][:], g_tiles[:, bass.ds((2 * m + p) * GC, GC), :]).then_inc(s_gate_in[p], 16)
            else:
                load_expert(0)
            sp.wait_ge(s_normed, 1)
            n_tiles = normed[0:tokens].rearrange("(t p) d -> p t d", p=P)
            sp.dma_start(n_tiles, x_all[:]).then_inc(s_stored, 16)
            sp.dma_start(normed[tokens:tokens + P], x_all[:, 0, :]).then_inc(s_stored, 16)
            with sp.Fori(1, E) as e:
                load_expert(e)
            for p in range(2):
                sp.wait_ge(s_added[p], 16 * M)

        @block.gpsimd
        def _(pool):
            order = Order(pool, s_pool)
            order(nc.gpsimd.memset(ident[:], 0.0))
            order(nc.gpsimd.memset(before[:], 1.0))
            nc.gpsimd.memset(ones[:], 1.0).then_inc(s_const, 1)
            nc.gpsimd.memset(one_t[:], 1.0).then_inc(s_const, 1)
            nc.gpsimd.affine_select(out=ident[:], in_=ident[:], compare_op=ALU.not_equal, fill=1.0, base=0,
                                    pattern=[[-1, P]], channel_multiplier=1).then_inc(s_const, 1)
            nc.gpsimd.affine_select(out=before[:], in_=before[:], compare_op=ALU.is_gt, fill=0.0, base=0,
                                    pattern=[[1, P]], channel_multiplier=-1).then_inc(s_const, 1)
            kw = dict(allow_small_or_imprecise_dtypes=True)
            nc.gpsimd.iota(expert_no[:], pattern=[[1, E]], base=0, channel_multiplier=0, **kw).then_inc(s_const, 1)
            nc.gpsimd.iota(lane_no[:], pattern=[[1, P]], base=0, channel_multiplier=0, **kw).then_inc(s_const, 1)
            nc.gpsimd.iota(pad_row[:], pattern=[[1, 1]], base=tokens + 1, channel_multiplier=1, **kw).then_inc(s_const, 1)
            nc.gpsimd.iota(token_1[:], pattern=[[P, T]], base=1, channel_multiplier=1, **kw).then_inc(s_const, 1)

            def gather(m, p, i):
                free(pool, s_xt[p], m)
                nc.gpsimd.tensor_copy(rows_in[p][:], row_of_slot[:, bass.ds(i, 1)]).then_inc(s_rows_in[p], 1)
                pool.wait_ge(s_rows_in[p], m + 1)
                pool.sem_inc(s_go)
                nc.gpsimd.indirect_dma_start(out=xg[p], out_offset=None, in_=normed,
                                             in_offset=bass.IndirectOffsetOnAxis(ap=rows_in[p][:, 0:1], axis=0)
                                             ).then_inc(s_xg[p], 16)

            def add(m, p, i):
                if p == 1:
                    pool.wait_ge(s_added[0], 16 * (m + 1))
                else:
                    free(pool, s_added[1], 16 * m)
                nc.gpsimd.tensor_copy(rows_out[p][:], row_of_slot[:, bass.ds(i, 1)]).then_inc(s_rows_out[p], 1)
                pool.wait_ge(s_rows_out[p], m + 1)
                pool.wait_ge(s_y[p], m + 1)
                pool.sem_inc(s_go)
                nc.gpsimd.indirect_dma_start(out=x_sum, out_offset=bass.IndirectOffsetOnAxis(ap=rows_out[p][:, 0:1], axis=0),
                                             in_=y[p], in_offset=None, compute_op=ALU.add).then_inc(s_added[p], 16)

            pool.wait_ge(s_table, 1)
            pool.wait_ge(s_stored, 32)
            gather(0, 0, 0)
            gather(0, 1, 1)
            gather(1, 0, 2)
            gather(1, 1, 3)
            if gate_source is not None:
                pool.wait_ge(s_begun, 32)
            add(0, 0, 0)
            with pool.Fori(2, M) as m:
                gather(m, 0, 2 * m)
                add(m - 2, 1, 2 * m - 3)
                gather(m, 1, 2 * m + 1)
                add(m - 1, 0, 2 * m - 2)
            add(M - 2, 1, NS - 3)
            add(M - 1, 0, NS - 2)
            add(M - 1, 1, NS - 1)

        def w1_at(w, e, dc, fc):
            return w[:, bass.ds(e, 1), dc, fc * P:(fc + 1) * P].rearrange("p a f -> p (a f)")

        def w2_at(w, e, fc):
            c, r = divmod(fc * D, CHUNK)
            return w[:, bass.ds(e, 1), 2 + c, r:r + D].rearrange("p a f -> p (a f)")

        @block.tensor
        def _(pe):
            pe.wait_ge(s_const, 8)
            pe.wait_ge(s_small, 48 + 16 * (bg is not None))
            nc.tensor.transpose(y_ps[0][:, 0:E * FC], b1_rows[:], ident[0:E * FC, 0:E * FC]).then_inc(s_b1, 1)
            lg = y_ps[1]
            if gate_source is None:
                pe.wait_ge(s_normed, 1)

            def gate_transpose(m, k, p):
                free(pe, s_trc[p], m * GC + k // 2)
                if gate_source is not None:
                    g = k // GC
                    if k % GC == 0:
                        pe.wait_ge(s_gate_in[g], 16 * (m + 1))
                    src = gate_in[g][:, k % GC, :]
                    for c in range(DC):
                        last = nc.tensor.transpose(xT_ps[p][:, c * P:(c + 1) * P], src[:, c * P:(c + 1) * P], ident[:])
                    last.then_inc(s_tr[p], 1)
                else:
                    for c in range(DC):
                        src = x_all[:, bass.ds(2 * GC * m + k, 1), c * P:(c + 1) * P].rearrange("p a d -> p (a d)") if not isinstance(m, int) else x_all[:, 2 * GC * m + k, c * P:(c + 1) * P]
                        last = nc.tensor.transpose(xT_ps[p][:, c * P:(c + 1) * P], src, ident[:])
                    last.then_inc(s_tr[p], 1)

            def gate_logits(m, k, p):
                pe.wait_ge(s_trc[p], m * GC + k // 2 + 1)
                t = 2 * GC * m + k
                for c in range(DC):
                    last = nc.tensor.matmul(lg[:, bass.ds(t * E, E)], gateT[p][:, c, :], wg_sb[:, c, :],
                                            start=(c == 0), stop=(c == DC - 1))
                last.then_inc(s_lg[p], 1)

            if gate_source is not None:
                def gate_tiles(m):
                    for k in range(2 * GC):
                        gate_transpose(m, k, k % 2)
                        if k % 2:
                            gate_logits(m, k - 1, 0)
                            gate_logits(m, k, 1)

                each(pe, T // GC // 2, gate_tiles)
            else:
                for m in range(T // GC // 2):
                    for k in range(2 * GC):
                        gate_transpose(m, k, k % 2)
                        if k % 2:
                            gate_logits(m, k - 1, 0)
                            gate_logits(m, k, 1)
            pe.wait_ge(s_oh, 1)
            pairs = oh16[:].rearrange("p t e -> p (t e)")
            nc.tensor.matmul(h_ps[0][:, 0, 0:T * E], before[:], pairs, start=True, stop=True)
            nc.tensor.matmul(h_ps[0][:, 1, 0:T * E], ones[:], pairs, start=True, stop=True).then_inc(s_count, 1)
            rounds = T * choices
            table = h_ps[1][:, 0, 0:2 * NS]

            def pick(m, p, start, stop):
                pe.wait_ge(s_pick[p], m + 1)
                nc.tensor.matmul(table, pick_lane[p][:], pick_tile[p][:].rearrange("p a n -> p (a n)"),
                                 start=start, stop=stop, skip_group_check=True).then_inc(s_picked[p], 1)

            pick(0, 0, True, False)
            pick(0, 1, False, False)
            with pe.Fori(1, rounds // 2 - 1) as m:
                for p in range(2):
                    pick(m, p, False, False)
            pick(rounds // 2 - 1, 0, False, False)
            pick(rounds // 2 - 1, 1, False, True)

            def transpose_in(m, p):
                pe.wait_ge(s_xg[p], 16 * (m + 1))
                if isinstance(m, int) and m == 0:
                    pe.wait_ge(s_table, 1)
                else:
                    pe.wait_ge(s_xl[p], m)
                for c in range(DC):
                    last = nc.tensor.transpose(xT_ps[p][:, c * P:(c + 1) * P], xg[p][:, c * P:(c + 1) * P], ident[:])
                last.then_inc(s_xt[p], 1)

            def layer1(m, p, i):
                e = pe.value_load(expert_of_tile[0:1, bass.ds(i, 1)], min_val=0, max_val=E - 1)
                pe.wait_ge(s_split, (e + 1) * CPE)
                pe.wait_ge(s_xl[p], m + 1)
                free(pe, s_h32[p], 2 * m)
                for b in range(2):
                    for q in range(4):
                        fc = 4 * b + q
                        out = h_ps[p][:, b, q * P:(q + 1) * P]
                        for c in range(DC):
                            hi, lo = w1_at(w_hi, e, c, fc), w1_at(w_lo, e, c, fc)
                            nc.tensor.matmul(out, hi, xT_hi[p][:, c, :], start=(c == 0), stop=False)
                            nc.tensor.matmul(out, hi, xT_lo[p][:, c, :], start=False, stop=False)
                            last = nc.tensor.matmul(out, lo, xT_hi[p][:, c, :], start=False, stop=(c == DC - 1))
                    last.then_inc(s_h[p], 1)

            def layer2(m, p, i):
                e = pe.value_load(expert_of_tile[0:1, bass.ds(i, 1)], min_val=0, max_val=E - 1)
                pe.wait_ge(s_hl[p], 2 * (m + 1))
                free(pe, s_yb[p], m)
                out = y_ps[p][:, 0:D]
                for fc in range(FC):
                    hi, lo = w2_at(w_hi, e, fc), w2_at(w_lo, e, fc)
                    nc.tensor.matmul(out, h_hi[p][:, fc, :], hi, start=(fc == 0), stop=False)
                    nc.tensor.matmul(out, h_hi[p][:, fc, :], lo, start=False, stop=False)
                    last = nc.tensor.matmul(out, h_lo[p][:, fc, :], hi, start=False, stop=(fc == FC - 1))
                last.then_inc(s_l2[p], 1)

            transpose_in(0, 0)
            transpose_in(0, 1)
            layer1(0, 0, 0)

            def pair(m):
                layer1(m, 1, 2 * m + 1)
                transpose_in(m + 1, 0)
                layer2(m, 0, 2 * m)
                layer1(m + 1, 0, 2 * m + 2)
                transpose_in(m + 1, 1)
                layer2(m, 1, 2 * m + 1)

            each(pe, M - 1, pair)
            layer1(M - 1, 1, NS - 1)
            layer2(M - 1, 0, NS - 2)
            layer2(M - 1, 1, NS - 1)

        def split_hi(act, e):
            for c in range(CPE):
                act.wait_ge(s_staged[c], 16 * (e + 1))
                nc.scalar.activation(w_hi[:, e, c, :], staged[c][:], ACT.Copy, scale=WEIGHT_SCALE).then_inc(s_hi, 1)

        @block.scalar
        def _(act):
            if gate_source is not None:
                act.dma_start(x_sum[0:tokens], x).then_inc(s_begun, 16)
                act.dma_start(x_sum[tokens:tokens + P], x[0:P]).then_inc(s_begun, 16)
            act.wait_ge(s_var, 1)
            nc.scalar.activation(rstd[:], rtmp[:], ACT.Sqrt).then_inc(s_root, 1)
            act.wait_ge(s_b1, 1)
            nc.scalar.activation(b1T[:], y_ps[0][:, 0:E * FC], ACT.Copy).then_inc(s_b1T, 1)
            split_hi(act, 0)

            def gate_copy(n, p):
                act.wait_ge(s_tr[p], n + 1)
                if not (isinstance(n, int) and n == 0):
                    act.wait_ge(s_lg[p], n)
                nc.scalar.activation(gateT[p][:].rearrange("p c t -> p (c t)"), xT_ps[p][:, 0:D], ACT.Copy).then_inc(s_trc[p], 1)

            gate_copy(0, 0)
            gate_copy(0, 1)
            with act.Fori(1, T // 2) as n:
                for p in range(2):
                    gate_copy(n, p)
            act.wait_ge(s_diff, 1)
            if choices == 2:
                nc.scalar.activation(weight[1][:], rtmp[:], ACT.Exp).then_inc(s_exp, 1)
            else:
                nc.scalar.activation(work[:], work[:], ACT.Exp).then_inc(s_exp, 1)

            def x_high(m, p):
                act.wait_ge(s_xt[p], m + 1)
                free(act, s_h[p], 2 * m)
                nc.scalar.activation(xT_hi[p][:].rearrange("p c t -> p (c t)"), xT_ps[p][:, 0:D], ACT.Copy).then_inc(s_xh[p], 1)

            def hidden(m, p, i):
                e = act.value_load(expert_of_tile[0:1, bass.ds(i, 1)], min_val=0, max_val=E - 1)
                for b in range(2):
                    act.wait_ge(s_h[p], 2 * m + b + 1)
                    free(act, s_hl[p], 2 * m)
                    for q in range(4):
                        fc = 4 * b + q
                        last = nc.scalar.activation(h32[p][:, fc * P:(fc + 1) * P], h_ps[p][:, b, q * P:(q + 1) * P],
                                                    ACT.Relu, bias=b1T[:, bass.ds(e * FC + fc, 1)], scale=1 / WEIGHT_SCALE)
                    last.then_inc(s_h32[p], 1)

            act.wait_ge(s_table, 1)
            x_high(0, 0)
            x_high(0, 1)
            hidden(0, 0, 0)
            for m in range(HEAD):
                split_hi(act, 2 * m + 1)
                hidden(m, 1, 2 * m + 1)
                x_high(m + 1, 0)
                if 2 * m + 2 < E:
                    split_hi(act, 2 * m + 2)
                hidden(m + 1, 0, 2 * m + 2)
                x_high(m + 1, 1)
            with act.Fori(HEAD, M - 1) as m:
                hidden(m, 1, 2 * m + 1)
                x_high(m + 1, 0)
                hidden(m + 1, 0, 2 * m + 2)
                x_high(m + 1, 1)
            hidden(M - 1, 1, NS - 1)

        def split_lo(dve, e):
            for c in range(CPE):
                dve.wait_ge(s_hi, e * CPE + c + 1)
                nc.vector.scalar_tensor_tensor(w_lo[:, e, c, :], staged[c][:], WEIGHT_SCALE, w_hi[:, e, c, :],
                                               ALU.mult, ALU.subtract).then_inc(s_split, 1)

        @block.vector
        def _(dve):
            V = nc.vector
            order = Order(dve, s_dve)
            for t in range(T):
                if t % (T // 4) == 0:
                    dve.wait_ge(s_x[t // (T // 4)], 16)
                order.tick(V.bn_stats(stats[:, t, :], x_all[:, t, :]))
            order.wait()
            for t in range(T):
                order.tick(V.bn_aggr(mean_var[:, t, :], stats[:, t, :]))
            order.wait()
            V.tensor_scalar(rtmp[:], mean_var[:, :, 1], EPS, None, ALU.add).then_inc(s_var, 1)
            dve.wait_ge(s_root, 1)
            order(V.reciprocal(rstd[:], rstd[:]))
            order(V.tensor_tensor(first[:], rstd[:], rstd[:], ALU.mult))
            order(V.tensor_tensor(first[:], first[:], rtmp[:], ALU.mult))
            order(V.tensor_scalar(first[:], first[:], -0.5, 1.5, ALU.mult, ALU.add))
            order(V.tensor_tensor(rstd[:], rstd[:], first[:], ALU.mult))
            for t in range(T):
                order.tick(V.tensor_scalar(x_all[:, t, :], x_all[:, t, :], mean_var[:, t, 0:1], rstd[:, t:t + 1],
                                           ALU.subtract, ALU.mult))
            order.wait()
            V.nop().then_inc(s_normed, 1)
            split_lo(dve, 0)

            def by_expert(ap):
                return ap.unsqueeze(2).to_broadcast([P, T, E])

            def of_expert(ap):
                return ap.unsqueeze(1).to_broadcast([P, T, E])

            dve.wait_ge(s_const, 8)
            for p in range(2):
                dve.wait_ge(s_lg[p], T // 2)
            lg = y_ps[1][:, 0:T * E].rearrange("p (t e) -> p t e", e=E)
            if bg is not None:
                order(V.tensor_tensor(logits[:], lg, of_expert(bg_sb[:]), ALU.add))
            else:
                order(V.tensor_copy(logits[:], lg))
            for c in range(choices):
                order(V.tensor_reduce(best[c][:], logits[:], AX_X, ALU.max))
                order(V.tensor_tensor(work[:], logits[:], by_expert(best[c][:]), ALU.is_lt))
                order(V.tensor_scalar(work[:], work[:], float(E), None, ALU.mult))
                order(V.tensor_tensor(work[:], work[:], of_expert(expert_no[:]), ALU.add))
                order(V.tensor_reduce(first[:], work[:], AX_X, ALU.min))
                order(V.tensor_tensor(onehot[c][:], of_expert(expert_no[:]), by_expert(first[:]), ALU.is_equal))
                if c + 1 < choices:
                    order(V.tensor_scalar(work[:], onehot[c][:], -3e38, None, ALU.mult))
                    order(V.tensor_tensor(logits[:], logits[:], work[:], ALU.add))
            if choices == 2:
                order(V.tensor_tensor(oh16[:], onehot[0][:], onehot[1][:], ALU.add))
                V.nop().then_inc(s_oh, 1)
                order(V.tensor_tensor(rtmp[:], best[1][:], best[0][:], ALU.subtract))
                V.nop().then_inc(s_diff, 1)
                dve.wait_ge(s_exp, 1)
                order(V.tensor_scalar(weight[0][:], weight[1][:], 1.0, None, ALU.add))
                order(V.reciprocal(weight[0][:], weight[0][:]))
                order(V.tensor_tensor(weight[1][:], weight[1][:], weight[0][:], ALU.mult))
            else:
                order(V.tensor_copy(oh16[:], onehot[0][:]))
                V.nop().then_inc(s_oh, 1)
                order(V.tensor_tensor(work[:], logits[:], by_expert(best[0][:]), ALU.subtract))
                V.nop().then_inc(s_diff, 1)
                dve.wait_ge(s_exp, 1)
                order(V.tensor_reduce(weight[0][:], work[:], AX_X, ALU.add))
                order(V.reciprocal(weight[0][:], weight[0][:]))

            dve.wait_ge(s_count, 1)
            order(V.tensor_copy(total[:].rearrange("p e t -> p t e"),
                                h_ps[0][:, 1, 0:T * E].rearrange("p (t e) -> p t e", e=E)))
            for e in range(E):
                order.tick(V.tensor_tensor_scan(running[:, e, :], one_t[:], total[:, e, :], 0.0, ALU.mult, ALU.add))
            order.wait()
            if capacity is None:
                order(V.tensor_scalar(tiles_of[:], running[:, :, T - 1], 1 / P, (P - 1) / P - 0.49609375, ALU.mult, ALU.add))
                order(V.tensor_scalar(tiles_of[:], tiles_of[:], ROUND, -ROUND, ALU.add, ALU.add))
                order(V.tensor_scalar(tiles_of[:], tiles_of[:], 1.0, None, ALU.max))
                order(V.tensor_tensor_scan(ends_of[:], one_t[:, 0:E], tiles_of[:], 0.0, ALU.mult, ALU.add))
                order(V.tensor_tensor(start_of[:], ends_of[:], tiles_of[:], ALU.subtract))
            else:
                order(V.tensor_scalar(start_of[:], expert_no[:], float(capacity // P), None, ALU.mult))
            order(V.tensor_tensor(running[:], running[:], total[:], ALU.subtract))
            order(V.tensor_tensor(work[:], running[:].rearrange("p e t -> p t e"),
                                  h_ps[0][:, 0, 0:T * E].rearrange("p (t e) -> p t e", e=E), ALU.add))
            if capacity is not None:
                order(V.tensor_scalar(logits[:], work[:], float(capacity), float(4 * tokens), ALU.is_ge, ALU.mult))
                order(V.tensor_tensor(work[:], work[:], logits[:], ALU.add))
            order(V.tensor_scalar(ends_of[:], start_of[:], float(P), None, ALU.mult))
            order(V.tensor_tensor(work[:], work[:], of_expert(ends_of[:]), ALU.add))
            for c in range(choices):
                order(V.tensor_tensor(logits[:], work[:], onehot[c][:], ALU.mult))
                order(V.tensor_reduce(first[:], logits[:], AX_X, ALU.add))
                order(V.tensor_scalar(slot_div[c][:], first[:], 1 / P, -0.49609375, ALU.mult, ALU.add))
                order(V.tensor_scalar(slot_div[c][:], slot_div[c][:], ROUND, -ROUND, ALU.add, ALU.add))
                order(V.scalar_tensor_tensor(slot_mod[c][:], slot_div[c][:], -float(P), first[:], ALU.mult, ALU.add))
            order(V.tensor_scalar(expert_f[:], lane_no[:, 0:NS], start_of[:, 1:2], None, ALU.is_ge))
            for e in range(2, E):
                order(V.scalar_tensor_tensor(expert_f[:], lane_no[:, 0:NS], start_of[:, e:e + 1], expert_f[:],
                                             ALU.is_ge, ALU.add))
            order(V.tensor_copy(expert_of_tile[:], expert_f[:]))

            def picks(m, p, c, t):
                free(dve, s_picked[p], m)
                V.tensor_scalar(pick_lane[p][:], lane_no[:], slot_mod[c][:, bass.ds(t, 1)], None, ALU.is_equal)
                V.tensor_scalar(pick_tile[p][:, 0, :], lane_no[:, 0:NS], slot_div[c][:, bass.ds(t, 1)],
                                token_1[:, bass.ds(t, 1)], ALU.is_equal, ALU.mult)
                V.tensor_scalar(pick_tile[p][:, 1, :], lane_no[:, 0:NS], slot_div[c][:, bass.ds(t, 1)],
                                weight[c][:, bass.ds(t, 1)], ALU.is_equal, ALU.mult).then_inc(s_pick[p], 1)

            if choices == 2:
                picks(0, 0, 0, 0)
                picks(0, 1, 1, 0)
                with dve.Fori(1, T) as t:
                    for c in range(2):
                        picks(t, c, c, t)
            else:
                picks(0, 0, 0, 0)
                picks(0, 1, 0, 1)
                with dve.Fori(1, T // 2) as m:
                    for p in range(2):
                        picks(m, p, 0, 2 * m + p)
            for p in range(2):
                dve.wait_ge(s_picked[p], T * choices // 2)
            table = h_ps[1][:, 0, 0:2 * NS]
            order(V.tensor_scalar(pad_f[:], table[:, 0:NS], 0.0, pad_row[:], ALU.is_equal, ALU.mult))
            order(V.scalar_tensor_tensor(row_f[:], table[:, 0:NS], -1.0, pad_f[:], ALU.add, ALU.add))
            order(V.tensor_copy(row_of_slot[:], row_f[:]))
            order(V.tensor_copy(weight_of_slot[:], table[:, NS:2 * NS]))
            V.nop().then_inc(s_table, 1)

            def x_low(m, p):
                dve.wait_ge(s_xh[p], m + 1)
                V.tensor_tensor(xT_lo[p][:].rearrange("p c t -> p (c t)"), xT_ps[p][:, 0:D],
                                xT_hi[p][:].rearrange("p c t -> p (c t)"), ALU.subtract).then_inc(s_xl[p], 1)

            def hidden_split(m, p):
                for b in range(2):
                    dve.wait_ge(s_h32[p], 2 * m + b + 1)
                    if b == 0 and not (isinstance(m, int) and m == 0):
                        dve.wait_ge(s_l2[p], m)
                    part = h32[p][:, b * 512:(b + 1) * 512]
                    hi = h_hi[p][:, 4 * b:4 * b + 4, :].rearrange("p c t -> p (c t)")
                    lo = h_lo[p][:, 4 * b:4 * b + 4, :].rearrange("p c t -> p (c t)")
                    V.tensor_copy(hi, part).then_inc(s_hh[p], 1)
                    dve.wait_ge(s_hh[p], 2 * m + b + 1)
                    V.tensor_tensor(lo, part, hi, ALU.subtract).then_inc(s_hl[p], 1)

            def result(m, p, i):
                e = dve.value_load(expert_of_tile[0:1, bass.ds(i, 1)], min_val=0, max_val=E - 1)
                dve.wait_ge(s_l2[p], m + 1)
                free(dve, s_added[p], 16 * m)
                V.scalar_tensor_tensor(y[p], y_ps[p][:, 0:D], 1 / WEIGHT_SCALE,
                                       b2_all[:, bass.ds(e, 1), :].rearrange("p a d -> p (a d)"), ALU.mult, ALU.add).then_inc(s_yb[p], 1)
                dve.wait_ge(s_yb[p], m + 1)
                V.tensor_scalar(y[p], y[p], weight_of_slot[:, bass.ds(i, 1)], None, ALU.mult).then_inc(s_y[p], 1)

            x_low(0, 0)
            x_low(0, 1)
            hidden_split(0, 0)
            for m in range(HEAD):
                split_lo(dve, 2 * m + 1)
                hidden_split(m, 1)
                x_low(m + 1, 0)
                result(m, 0, 2 * m)
                if 2 * m + 2 < E:
                    split_lo(dve, 2 * m + 2)
                hidden_split(m + 1, 0)
                x_low(m + 1, 1)
                result(m, 1, 2 * m + 1)
            with dve.Fori(HEAD, M - 1) as m:
                hidden_split(m, 1)
                x_low(m + 1, 0)
                result(m, 0, 2 * m)
                hidden_split(m + 1, 0)
                x_low(m + 1, 1)
                result(m, 1, 2 * m + 1)
            hidden_split(M - 1, 1)
            result(M - 1, 0, NS - 2)
            result(M - 1, 1, NS - 1)


def this(engine, semaphores, m, p):
    engine.wait_ge(semaphores[p], m + 1)


def last(engine, semaphores, m, p):
    free(engine, semaphores[1 - p], m + p)


def attention(nc, name, x_all, x_sum, context, mask, wq, bq, wk, bk, wv, bv, wo, bo):
    B = x_all.shape[1]
    D = x_all.shape[2]
    DC = D // P
    H = 16
    DK = D // H
    HC = H // 2
    V1 = DK + 1
    QS = WEIGHT_SCALE * float(DK) ** 0.5
    assert D == 2 * P and DK == 16

    with ExitStack() as ctx:
        sem = ctx.enter_context(stage_semaphores(nc, name))

        def sb(n, shape, dt):
            return ctx.enter_context(nc.sbuf_tensor(f"{name}_{n}", shape, dt))

        def pb(n, shape, dt):
            return ctx.enter_context(nc.psum_tensor(f"{name}_{n}", shape, dt))

        def two(n):
            return [sem(f"{n}_{p}") for p in range(2)]

        c_in = [sb(f"c_in{p}", [P, D], F32) for p in range(2)]
        w_rows = sb("w_rows", [P, 4, DC, D], F32)
        wT_hi = sb("wT_hi", [P, 4, DC, D], F16)
        wT_lo = sb("wT_lo", [P, 4, DC, D], F16)
        kvT_hi = sb("kvT_hi", [P, DC, 2 * D], F16)
        kvT_lo = sb("kvT_lo", [P, DC, 2 * D], F16)
        biases = sb("biases", [P, 4, D], F32)
        mask_sb = sb("mask_sb", [P, P], I32)
        masked = sb("masked", [P, P], I32)
        tiny = sb("tiny", [P, P], F32)
        ident = sb("ident", [P, P], F32)
        ident16 = sb("ident16", [P, P], F16)
        stats = sb("stats", [P, B, 6], F32)
        mean_var = sb("mean_var", [P, B, 2], F32)
        rstd = sb("rstd", [P, B], F32)
        var = sb("var", [P, B], F32)
        rtmp = sb("rtmp", [P, B], F32)
        xn = sb("xn", [P, D], F32)
        inT_hi = sb("inT_hi", [P, 4, P], F16)
        inT_lo = sb("inT_lo", [P, 4, P], F16)
        q32 = sb("q32", [P, D], F32)
        k32 = sb("k32", [P, D], F32)
        v32 = [sb(f"v32_{p}", [P, H, V1], F32) for p in range(2)]
        q_parts = sb("q_parts", [P, H, 4, DK], F16)
        k_parts = sb("k_parts", [P, H, 4, DK], F16)
        qT = sb("qT", [P, HC, P], F16)
        kT = sb("kT", [P, HC, P], F16)
        top = sb("top", [P, H], F32)
        prob = sb("prob", [P, H, P], F32)
        probT = sb("probT", [P, H, P], F32)
        rsum = sb("rsum", [P, H], F32)
        o32 = sb("o32", [P, D], F32)
        oT_hi = sb("oT_hi", [P, DC, P], F16)
        oT_lo = sb("oT_lo", [P, DC, P], F16)

        S = pb("S", [P, 2, HC, P], F32)
        front = [pb(f"front{i}", [P, 512], F32) for i in range(2)]
        out_ps = pb("out_ps", [P, 512], F32)
        oT_ps = pb("oT_ps", [P, 512], F32)

        s_x = sem("x_loaded"); s_c = two("context_loaded"); s_w = sem("weights_loaded")
        s_pool = sem("pool_order"); s_dve = sem("dve_order"); s_const = sem("constants")
        s_var = sem("variance"); s_root = sem("root"); s_prep = sem("dve_prepared")
        s_wt = two("weights_transposed"); s_wh = two("weights_hi"); s_wl = two("weights_lo")
        s_xn = two("xn_ready"); s_xb = two("x_biased")
        s_tp = two("inputs_transposed"); s_th = two("inT_hi_ready"); s_tl = two("inT_lo_ready")
        s_kv = two("kv_product"); s_q = two("q_product")
        s_k32 = two("k32_ready"); s_v32 = two("v32_ready"); s_q32 = two("q32_ready")
        s_qh = two("q_high"); s_kh = two("k_high"); s_ql = two("q_low"); s_kl = two("k_low")
        s_qt = two("q_transposed"); s_kt = two("k_transposed"); s_qT = two("qT_ready"); s_kT = two("kT_ready")
        s_s = [two(f"scores{r}") for r in range(2)]
        s_top = [two(f"top{r}") for r in range(2)]; s_mask = [two(f"masked{r}") for r in range(2)]
        s_sub = [two(f"shifted{r}") for r in range(2)]; s_exp = [two(f"exp{r}") for r in range(2)]
        s_pt = [two(f"prob_transposed{r}") for r in range(2)]; s_pT = [two(f"probT{r}_ready") for r in range(2)]
        s_pv = two("pv_product"); s_rs = two("rsum_ready"); s_o = two("o32_ready")
        s_ot = two("o_transposed"); s_oh = two("oT_hi_ready"); s_ol = two("oT_lo_ready")
        s_out = two("out_product"); s_done = two("batch_done")

        s_go = sem("dve_goes_on")

        M = B // 2
        block = ctx.enter_context(nc.Block())

        @block.sync
        def _(sp):
            sp.dma_start(x_all[:], x_sum.rearrange("(t p) d -> p t d", p=P)).then_inc(s_x, 16)
            for i, w in enumerate((wq, wk, wv, wo)):
                sp.dma_start(w_rows[:, i], w.rearrange("(c p) d -> p c d", p=P)).then_inc(s_w, 16)
            for i, b in enumerate((bq, bk, bv, bo)):
                sp.dma_start(biases[:, i, :], broadcast_rows(b, P, D)).then_inc(s_w, 16)
            sp.dma_start(mask_sb[:], mask.rearrange("a b q k -> (a b q) k")).then_inc(s_w, 16)

            def load(m):
                for p in range(2):
                    free(sp, s_tp[p], m)
                    sp.dma_start(c_in[p][:], context[bass.ds((2 * m + p) * P, P), :]).then_inc(s_c[p], 16)

            each(sp, M, load)

        @block.gpsimd
        def _(pool):
            order = Order(pool, s_pool)
            order(nc.gpsimd.memset(ident[:], 0.0))
            order(nc.gpsimd.memset(ident16[:], 0.0))
            for i in (ident, ident16):
                nc.gpsimd.affine_select(out=i[:], in_=i[:], compare_op=ALU.not_equal, fill=1.0, base=0,
                                        pattern=[[-1, P]], channel_multiplier=1).then_inc(s_const, 1)
            nc.gpsimd.memset(tiny[:], 1e-09).then_inc(s_const, 1)
            for p in range(2):
                nc.gpsimd.memset(v32[p][:, :, DK:V1], 1.0).then_inc(s_const, 1)
            pool.wait_ge(s_w, 16 * 9)

            def batch(m, p):
                b = 2 * m + p
                this(pool, s_xn, m, p)
                row = x_all[:, bass.ds(b, 1), :].rearrange("p a d -> p (a d)")
                nc.gpsimd.tensor_tensor(row, row, biases[:, 3, :], ALU.add).then_inc(s_xb[p], 1)
                this(pool, s_qh, m, p)
                q2 = q32[:].rearrange("p (h d) -> p h d", h=H).unsqueeze(2).to_broadcast([P, H, 2, DK])
                nc.gpsimd.tensor_tensor(q_parts[:, :, 2:4, :], q2, q_parts[:, :, 0:2, :], ALU.subtract).then_inc(s_ql[p], 1)
                this(pool, s_kh, m, p)
                k2 = k32[:].rearrange("p (h d) -> p h d", h=H).unsqueeze(2).to_broadcast([P, H, 2, DK])
                nc.gpsimd.tensor_tensor(k_parts[:, :, 1:4:2, :], k2, k_parts[:, :, 0:4:2, :], ALU.subtract).then_inc(s_kl[p], 1)

            def pair(m):
                for p in range(2):
                    batch(m, p)

            each(pool, M, pair)

        @block.tensor
        def _(pe):
            pe.wait_ge(s_const, 5)
            pe.wait_ge(s_w, 16 * 9)
            for i in range(4):
                p = i % 2
                if i >= 2:
                    pe.wait_ge(s_wl[p], i // 2)
                for r in range(DC):
                    for c in range(DC):
                        mm = nc.tensor.transpose(front[p][:, (c * DC + r) * P:(c * DC + r + 1) * P],
                                                 w_rows[:, i, r, c * P:(c + 1) * P], ident[:])
                mm.then_inc(s_wt[p], 1)
            pe.wait_ge(s_prep, 1)

            def front_in(m, p):
                this(pe, s_xn, m, p)
                pe.wait_ge(s_c[p], 16 * (m + 1))
                last(pe, s_qT, m, p)
                for c in range(DC):
                    nc.tensor.transpose(front[0][:, c * P:(c + 1) * P], xn[:, c * P:(c + 1) * P], ident[:])
                for c in range(DC):
                    mm = nc.tensor.transpose(front[0][:, (2 + c) * P:(3 + c) * P], c_in[p][:, c * P:(c + 1) * P], ident[:])
                mm.then_inc(s_tp[p], 1)

            def front_products(m, p):
                this(pe, s_tl, m, p)
                last(pe, s_kT, m, p)
                for c in range(DC):
                    a_hi, a_lo = inT_hi[:, 2 + c, :], inT_lo[:, 2 + c, :]
                    nc.tensor.matmul(front[1][:], a_hi, kvT_hi[:, c, :], start=(c == 0), stop=False)
                    nc.tensor.matmul(front[1][:], a_hi, kvT_lo[:, c, :], start=False, stop=False)
                    mm = nc.tensor.matmul(front[1][:], a_lo, kvT_hi[:, c, :], start=False, stop=(c == DC - 1))
                mm.then_inc(s_kv[p], 1)
                for c in range(DC):
                    a_hi, a_lo = inT_hi[:, c, :], inT_lo[:, c, :]
                    out = front[0][:, 0:D]
                    nc.tensor.matmul(out, a_hi, wT_hi[:, 0, c, :], start=(c == 0), stop=False)
                    nc.tensor.matmul(out, a_hi, wT_lo[:, 0, c, :], start=False, stop=False)
                    mm = nc.tensor.matmul(out, a_lo, wT_hi[:, 0, c, :], start=False, stop=(c == DC - 1))
                mm.then_inc(s_q[p], 1)

            def front_transposes(m, p):
                this(pe, s_ql, m, p)
                for c in range(HC):
                    mm = nc.tensor.transpose(front[0][:].bitcast(F16)[:, c * P:(c + 1) * P],
                                             q_parts[:, 2 * c:2 * c + 2].rearrange("p h k d -> p (h k d)"), ident16[:])
                mm.then_inc(s_qt[p], 1)
                this(pe, s_kl, m, p)
                this(pe, s_v32, m, p)
                for c in range(HC):
                    mm = nc.tensor.transpose(front[1][:].bitcast(F16)[:, c * P:(c + 1) * P],
                                             k_parts[:, 2 * c:2 * c + 2].rearrange("p h k d -> p (h k d)"), ident16[:])
                mm.then_inc(s_kt[p], 1)

            def scores(m, p):
                this(pe, s_qT, m, p)
                this(pe, s_kT, m, p)
                for r in range(2):
                    last(pe, s_pT[r], m, p)
                for c in range(HC):
                    for r in range(2):
                        rows = slice(64 * r, 64 * r + 64)
                        mm = nc.tensor.matmul(S[:, r, c, :], qT[rows, c, :], kT[rows, c, :], start=True, stop=True)
                        if c == HC - 1:
                            mm.then_inc(s_s[r][p], 1)

            def back_transposes(m, p):
                for r in range(2):
                    this(pe, s_exp[r], m, p)
                    for c in range(HC):
                        mm = nc.tensor.transpose(S[:, r, c, :], prob[:, r * HC + c, :], ident[:])
                    mm.then_inc(s_pt[r][p], 1)

            def back_products(m, p):
                last(pe, s_done, m, p)
                for r in range(2):
                    this(pe, s_pT[r], m, p)
                    for c in range(HC):
                        h = r * HC + c
                        mm = nc.tensor.matmul(out_ps[:, h * V1:(h + 1) * V1], probT[:, h, :], v32[p][:, 2 * c + r, :],
                                              start=True, stop=True)
                mm.then_inc(s_pv[p], 1)

            def back_out(m, p):
                this(pe, s_o, m, p)
                for c in range(DC):
                    mm = nc.tensor.transpose(oT_ps[:, c * P:(c + 1) * P], o32[:, c * P:(c + 1) * P], ident[:])
                mm.then_inc(s_ot[p], 1)
                this(pe, s_ol, m, p)
                for c in range(DC):
                    out = out_ps[:, 0:D]
                    nc.tensor.matmul(out, oT_hi[:, c, :], wT_hi[:, 3, c, :], start=(c == 0), stop=False)
                    nc.tensor.matmul(out, oT_hi[:, c, :], wT_lo[:, 3, c, :], start=False, stop=False)
                    mm = nc.tensor.matmul(out, oT_lo[:, c, :], wT_hi[:, 3, c, :], start=False, stop=(c == DC - 1))
                mm.then_inc(s_out[p], 1)

            def batch(m, p, more):
                n, q = (m, 1) if p == 0 else (m + 1, 0)
                scores(m, p)
                if more:
                    front_in(n, q)
                    front_products(n, q)
                back_transposes(m, p)
                if more:
                    front_transposes(n, q)
                back_products(m, p)
                back_out(m, p)

            front_in(0, 0)
            front_products(0, 0)
            front_transposes(0, 0)
            for p in range(2):
                batch(0, p, True)
            with pe.Fori(1, M - 1) as m:
                for p in range(2):
                    batch(m, p, True)
            batch(M - 1, 0, True)
            batch(M - 1, 1, False)

        @block.scalar
        def _(act):
            A = nc.scalar
            act.wait_ge(s_var, 1)
            A.activation(rstd[:], var[:], ACT.Sqrt).then_inc(s_root, 1)
            for i in range(4):
                p = i % 2
                act.wait_ge(s_wt[p], i // 2 + 1)
                A.activation(wT_hi[:, i].rearrange("p c d -> p (c d)"), front[p][:], ACT.Copy, scale=WEIGHT_SCALE).then_inc(s_wh[p], 1)

            def front_in(m, p):
                this(act, s_tp, m, p)
                A.activation(inT_hi[:].rearrange("p c t -> p (c t)"), front[0][:], ACT.Copy).then_inc(s_th[p], 1)

            def front_high(m, p):
                this(act, s_k32, m, p)
                k2 = k32[:].rearrange("p (h d) -> p h d", h=H).unsqueeze(2).to_broadcast([P, H, 2, DK])
                A.activation(k_parts[:, :, 0:4:2, :], k2, ACT.Copy).then_inc(s_kh[p], 1)
                this(act, s_q32, m, p)
                q2 = q32[:].rearrange("p (h d) -> p h d", h=H).unsqueeze(2).to_broadcast([P, H, 2, DK])
                A.activation(q_parts[:, :, 0:2, :], q2, ACT.Copy).then_inc(s_qh[p], 1)

            def front_copy(m, p):
                this(act, s_qt, m, p)
                for r in range(2):
                    last(act, s_s[r], m, p)
                A.activation(qT[:].rearrange("p c t -> p (c t)"), front[0][:].bitcast(F16), ACT.Copy).then_inc(s_qT[p], 1)

            def exps(m, p):
                for r in range(2):
                    this(act, s_sub[r], m, p)
                    part = prob[:, r * HC:(r + 1) * HC, :]
                    A.activation(part, part, ACT.Exp).then_inc(s_exp[r][p], 1)

            def prob_copy(m, p):
                last(act, s_pv, m, p)
                for r in range(2):
                    this(act, s_pt[r], m, p)
                    A.activation(probT[:, r * HC:(r + 1) * HC, :], S[:, r], ACT.Copy).then_inc(s_pT[r][p], 1)

            def out_high(m, p):
                this(act, s_ot, m, p)
                A.activation(oT_hi[:].rearrange("p c t -> p (c t)"), oT_ps[:, 0:D], ACT.Copy).then_inc(s_oh[p], 1)

            def batch(m, p, more):
                n, q = (m, 1) if p == 0 else (m + 1, 0)
                if more:
                    front_in(n, q)
                exps(m, p)
                if more:
                    front_high(n, q)
                prob_copy(m, p)
                if more:
                    front_copy(n, q)
                out_high(m, p)

            front_in(0, 0)
            front_high(0, 0)
            front_copy(0, 0)
            for p in range(2):
                batch(0, p, True)
            with act.Fori(1, M - 1) as m:
                for p in range(2):
                    batch(m, p, True)
            batch(M - 1, 0, True)
            batch(M - 1, 1, False)

        @block.vector
        def _(dve):
            V = nc.vector
            order = Order(dve, s_dve)
            dve.wait_ge(s_x, 16)
            layernorm_scales(dve, order, x_all, stats, mean_var, var, rstd, rtmp, s_var, s_root)
            dve.wait_ge(s_w, 16 * 9)
            for i in range(4):
                p = i % 2
                dve.wait_ge(s_wh[p], i // 2 + 1)
                V.scalar_tensor_tensor(wT_lo[:, i].rearrange("p c d -> p (c d)"), front[p][:], WEIGHT_SCALE,
                                       wT_hi[:, i].rearrange("p c d -> p (c d)"), ALU.mult, ALU.subtract).then_inc(s_wl[p], 1)
            for p in range(2):
                dve.wait_ge(s_wl[p], 2)
            for src, dst in ((wT_hi, kvT_hi), (wT_lo, kvT_lo)):
                for i in range(2):
                    order.tick(V.tensor_copy(dst[:, :, i * D:(i + 1) * D], src[:, 1 + i]))
            order.tick(V.tensor_scalar(biases[:, 0, :], biases[:, 0, :], 1 / float(DK) ** 0.5, None, ALU.mult))
            order(V.tensor_scalar(masked[:], mask_sb[:], 0, None, ALU.is_equal))
            V.nop().then_inc(s_prep, 1)
            dve.wait_ge(s_const, 5)

            def normalise(m, p):
                b = 2 * m + p
                last(dve, s_tp, m, p)
                V.tensor_scalar(xn[:], x_all[:, bass.ds(b, 1), :].rearrange("p a d -> p (a d)"),
                                mean_var[:, bass.ds(b, 1), 0], rstd[:, bass.ds(b, 1)], ALU.subtract, ALU.mult).then_inc(s_xn[p], 1)

            def front_low(m, p):
                this(dve, s_th, m, p)
                V.tensor_tensor(inT_lo[:].rearrange("p c t -> p (c t)"), front[0][:],
                                inT_hi[:].rearrange("p c t -> p (c t)"), ALU.subtract).then_inc(s_tl[p], 1)

            def front_bias(m, p):
                this(dve, s_kv, m, p)
                last(dve, s_kl, m, p)
                last(dve, s_ql, m, p)
                V.scalar_tensor_tensor(k32[:], front[1][:, 0:D], 1 / WEIGHT_SCALE, biases[:, 1, :], ALU.mult, ALU.add).then_inc(s_k32[p], 1)
                this(dve, s_q, m, p)
                V.scalar_tensor_tensor(q32[:], front[0][:, 0:D], 1 / QS, biases[:, 0, :], ALU.mult, ALU.add).then_inc(s_q32[p], 1)
                free(dve, s_pv[p], m)
                V.scalar_tensor_tensor(v32[p][:, :, 0:DK], front[1][:, D:2 * D].rearrange("p (h d) -> p h d", h=H), 1 / WEIGHT_SCALE,
                                       biases[:, 2, :].rearrange("p (h d) -> p h d", h=H), ALU.mult, ALU.add).then_inc(s_v32[p], 1)

            def front_copy(m, p):
                this(dve, s_kt, m, p)
                for r in range(2):
                    last(dve, s_s[r], m, p)
                V.tensor_copy(kT[:].rearrange("p c t -> p (c t)"), front[1][:].bitcast(F16)).then_inc(s_kT[p], 1)

            def softmax_shift(m, p):
                for r in range(2):
                    this(dve, s_s[r], m, p)
                    wide = [P, HC, P]
                    dve.sem_inc(s_go)
                    V.copy_predicated(S[:, r], masked[:].unsqueeze(1).to_broadcast(wide),
                                      tiny[:].unsqueeze(1).to_broadcast(wide)).then_inc(s_mask[r][p], 1)
                    this(dve, s_mask[r], m, p)
                    tops = top[:, r * HC:(r + 1) * HC]
                    V.tensor_reduce(tops, S[:, r], AX_X, ALU.max).then_inc(s_top[r][p], 1)
                    this(dve, s_top[r], m, p)
                    last(dve, s_pt[r], m, p)
                    V.tensor_tensor(prob[:, r * HC:(r + 1) * HC, :], S[:, r], tops.unsqueeze(2).to_broadcast(wide),
                                    ALU.subtract).then_inc(s_sub[r][p], 1)

            def divide(m, p):
                this(dve, s_pv, m, p)
                o = out_ps[:, 0:H * V1].rearrange("p (r c v) -> p r c v", r=2, v=V1)
                V.reciprocal(rsum[:].rearrange("p (r c) -> p r c", r=2), o[:, :, :, DK]).then_inc(s_rs[p], 1)
                this(dve, s_rs, m, p)
                last(dve, s_ot, m, p)
                V.tensor_tensor(o32[:].rearrange("p (c r d) -> p r c d", r=2, d=DK), o[:, :, :, 0:DK],
                                rsum[:].rearrange("p (r c) -> p r c", r=2).unsqueeze(3).to_broadcast([P, 2, HC, DK]),
                                ALU.mult).then_inc(s_o[p], 1)

            def out_low(m, p):
                this(dve, s_oh, m, p)
                V.tensor_tensor(oT_lo[:].rearrange("p c t -> p (c t)"), oT_ps[:, 0:D],
                                oT_hi[:].rearrange("p c t -> p (c t)"), ALU.subtract).then_inc(s_ol[p], 1)

            def finish(m, p):
                b = 2 * m + p
                this(dve, s_out, m, p)
                this(dve, s_xb, m, p)
                row = x_all[:, bass.ds(b, 1), :].rearrange("p a d -> p (a d)")
                V.scalar_tensor_tensor(row, out_ps[:, 0:D], 1 / WEIGHT_SCALE, row, ALU.mult, ALU.add).then_inc(s_done[p], 1)

            def batch(m, p, more):
                n, q = (m, 1) if p == 0 else (m + 1, 0)
                if more:
                    normalise(n, q)
                softmax_shift(m, p)
                if more:
                    front_low(n, q)
                    front_bias(n, q)
                divide_next = (m, p)
                if more:
                    front_copy(n, q)
                divide(*divide_next)
                out_low(m, p)
                finish(m, p)

            normalise(0, 0)
            front_low(0, 0)
            front_bias(0, 0)
            front_copy(0, 0)
            for p in range(2):
                batch(0, p, True)
            with dve.Fori(1, M - 1) as m:
                for p in range(2):
                    batch(m, p, True)
            batch(M - 1, 0, True)
            batch(M - 1, 1, False)
            for p in range(2):
                dve.wait_ge(s_done[p], M)


def gated_ffn(nc, name, x_all, w_gate, w_up, w_down, up_raw, out):
    T, D = x_all.shape[1], x_all.shape[2]
    tokens = T * P
    I = w_gate.shape[0]
    DC, IC = D // P, I // P
    BLOCK = 32
    WQMAX = 7.0
    QMAX = 2.0**15 - 1
    N = 512
    TG = tokens // N
    COLS = IC * tokens
    CB = 1024
    STEPS = COLS // CB
    NP = 2 * IC
    BANKS = 4

    with ExitStack() as ctx:
        sem = ctx.enter_context(stage_semaphores(nc, name))

        def sb(n, shape, dt):
            return ctx.enter_context(nc.sbuf_tensor(f"{name}_{n}", shape, dt))

        def pb(n, shape, dt):
            return ctx.enter_context(nc.psum_tensor(f"{name}_{n}", shape, dt))

        def two(n):
            return [sem(f"{n}_{p}") for p in range(2)]

        act_all = sb("act_all", [P, IC, tokens], F32)
        flat = act_all[:].rearrange("p c t -> p (c t)")
        y_all = flat[:, 0:T * D].rearrange("p (t d) -> p t d", d=D)
        W = IC * D
        rows = [flat[:, T * D + i * W:T * D + (i + 1) * W] for i in range(3)]
        scaled = [flat[:, T * D + (3 + i) * W:T * D + (4 + i) * W] for i in range(3)]
        yT_hi = sb("yT_hi", [P, DC, tokens], F16)
        yT_lo = sb("yT_lo", [P, DC, tokens], F16)
        guT_hi = sb("guT_hi", [P, 2, DC, I], F16)
        guT_lo = sb("guT_lo", [P, 2, DC, I], F16)
        dT_hi = sb("dT_hi", [P, IC, D], F16)
        dT_lo = sb("dT_lo", [P, IC, D], F16)
        ident = sb("ident", [P, P], F32)
        round_c = sb("round_c", [P, 1], F32)
        round_u = sb("round_u", [P, 1], F32)
        stats = sb("stats", [P, T, 6], F32)
        mean_var = sb("mean_var", [P, T, 2], F32)
        rstd = sb("rstd", [P, T], F32)
        var = sb("var", [P, T], F32)
        rtmp = sb("rtmp", [P, T], F32)
        NB = W // BLOCK
        b_scale = sb("b_scale", [P, 3, NB], F32)
        b_inv = sb("b_inv", [P, 3, NB], F32)
        maxes = sb("maxes", [P, NP, TG], F32)
        step_max = sb("step_max", [P, max(STEPS, T)], F32)
        largest = sb("largest", [P, 4, 2], F32)
        reduced = sb("reduced", [P, 4, 2], F32)
        scale = sb("scale", [P, 5], F32)
        to_int = sb("to_int", [P, 5], F32)
        tmp = sb("tmp", [P, 5], F32)
        unit = sb("unit", [P, 3], F32)
        u_out = [sb(f"u_out{p}", [P, N], F32) for p in range(2)]
        work = [[sb(f"work{i}{p}", [P, CB], F32) for p in range(2)] for i in range(2)]
        later = yT_hi[:].rearrange("p c t -> p (c t)").bitcast(F32)
        o_parts = yT_lo[:].rearrange("p c t -> p (c t)")

        ps = [pb(f"ps{i}", [P, N], F32) for i in range(8)]

        s_w = [sem(f"rows{i}_loaded") for i in range(3)]
        s_const = sem("constants"); s_pool = sem("pool_order"); s_dve = sem("dve_order")
        s_var = sem("variance"); s_root = sem("root")
        s_deq = sem("weights_dequantised"); s_wt = two("weights_transposed"); s_wh = two("weights_hi"); s_wl = two("weights_lo")
        s_big = sem("largest_ready"); s_red = sem("largest_reduced"); s_scale = sem("scales_ready")
        s_t = two("x_rounded"); s_q = two("x_quantised"); s_qt = two("x_transposed"); s_qh = two("yT_hi_ready"); s_ql = two("yT_lo_ready")
        s_pr = [sem(f"product_in_bank{i}") for i in range(BANKS)]; s_ev = [sem(f"bank{i}_copied") for i in range(BANKS)]
        s_mx = [sem(f"bank{i}_max_taken") for i in range(BANKS)]
        s_us = two("up_stored")
        s_2 = {k: two("sig_" + k) for k in ("t", "int", "sigmoid", "shift", "sig", "product", "max")}
        s_3 = {k: two("up_" + k) for k in ("loaded", "t", "int", "tu", "product", "max")}
        s_4 = {k: two("down_" + k) for k in ("t", "int", "hi", "lo", "product", "out", "stored")}

        def weight_groups(i):
            if i < 2:
                return [[c * D + d * P for c in range(c0, c0 + 2) for d in range(DC)] for c0 in range(0, IC, 2)]
            return [[r * I + c * P for c in range(c0, c0 + 2) for r in range(DC)] for c0 in range(0, IC, 2)]

        def weight_parts(i, j, w, d):
            if i < 2:
                return w[:, i, :, 2 * j * P:2 * (j + 1) * P].rearrange("p r (c q) -> p c r q", q=P)
            return d[:, 2 * j:2 * j + 2, :].rearrange("p c (r q) -> p c r q", q=P)

        def down_parts(p):
            n = IC * P
            return [o_parts[:, (2 * h + p) * n:(2 * h + p + 1) * n].rearrange("p (c t) -> p c t", c=IC) for h in range(2)]

        s_go = sem("act_goes_on")

        block = ctx.enter_context(nc.Block())

        @block.sync
        def _(sp):
            for i, w in enumerate((w_gate, w_up)):
                sp.dma_start(rows[i].rearrange("p (c d) -> p c d", d=D), w.rearrange("(c p) d -> p c d", p=P)).then_inc(s_w[i], 16)
            sp.dma_start(rows[2].rearrange("p (c i) -> p c i", i=I), w_down.rearrange("(c p) i -> p c i", p=P)).then_inc(s_w[2], 16)


            def up_out(g):
                for c in range(IC):
                    k = IC + c
                    sp.wait_ge(s_ev[k % BANKS], (NP // BANKS) * g + k // BANKS + 1)
                    sp.dma_start(up_raw[:, c, bass.ds(g * N, N)], u_out[c % 2][:]).then_inc(s_us[c % 2], 16)

            each(sp, TG, up_out)
            for p in range(2):
                sp.wait_ge(s_us[p], 16 * TG * IC // 2)
            up_flat = up_raw.rearrange("p c t -> p (c t)")

            def up_in(m):
                for p in range(2):
                    free(sp, s_3["tu"][p], m)
                    sp.dma_start(later[:, (2 + p) * CB:(3 + p) * CB], up_flat[:, bass.ds((2 * m + p) * CB, CB)]).then_inc(s_3["loaded"][p], 16)

            each(sp, STEPS // 2, up_in)

            def result_out(m):
                for p in range(2):
                    sp.wait_ge(s_4["out"][p], m + 1)
                    sp.dma_start(out[bass.ds((2 * m + p) * P, P), :], u_out[p][:, 0:D]).then_inc(s_4["stored"][p], 16)

            each(sp, T // 2, result_out)
            for p in range(2):
                sp.wait_ge(s_4["stored"][p], 16 * T // 2)

        @block.gpsimd
        def _(pool):
            order = Order(pool, s_pool)
            order(nc.gpsimd.memset(ident[:], 0.0))
            nc.gpsimd.affine_select(out=ident[:], in_=ident[:], compare_op=ALU.not_equal, fill=1.0, base=0,
                                    pattern=[[-1, P]], channel_multiplier=1).then_inc(s_const, 1)
            nc.gpsimd.memset(round_c[:], ROUND).then_inc(s_const, 1)
            nc.gpsimd.memset(round_u[:], 2.0**23).then_inc(s_const, 1)

            def all_max(n):
                pool.wait_ge(s_big, n + 1)
                nc.gpsimd.partition_all_reduce(reduced[:, n, :], largest[:, n, :], P, bass.bass_isa.ReduceOp.max).then_inc(s_red, 1)

            all_max(0)
            all_max(1)

            def multiply_sigmoid(m):
                for p in range(2):
                    this(pool, s_2["sig"], m, p)
                    part = flat[:, bass.ds((2 * m + p) * CB, CB)]
                    nc.gpsimd.tensor_tensor(part, part, work[1][p][:], ALU.mult).then_inc(s_2["product"][p], 1)

            each(pool, STEPS // 2, multiply_sigmoid)
            all_max(2)
            all_max(3)

        @block.tensor
        def _(pe):
            pe.wait_ge(s_const, 3)

            def weights(i, n, parts):
                p = n % 2
                if n >= 2:
                    pe.wait_ge(s_wl[p], n // 2)
                for j, part in enumerate(parts):
                    mm = nc.tensor.transpose(ps[p][:, j * P:(j + 1) * P], part, ident[:])
                mm.then_inc(s_wt[p], 1)

            n = 0
            for i in range(3):
                pe.wait_ge(s_deq, i + 1)
                for group in weight_groups(i):
                    weights(i, n, [scaled[i][:, a:a + P] for a in group])
                    n += 1

            def tokens_in(m, p):
                this(pe, s_q, m, p)
                free(pe, s_ql[p], m)
                for t in range(2):
                    for c in range(DC):
                        mm = nc.tensor.transpose(ps[2 + p][:, (2 * c + t) * P:(2 * c + t + 1) * P],
                                                 work[0][p][:, t * D + c * P:t * D + (c + 1) * P], ident[:])
                mm.then_inc(s_qt[p], 1)

            def tokens_group(m):
                for p in range(2):
                    tokens_in(m, p)

            each(pe, T // 4, tokens_group)
            for p in range(2):
                pe.wait_ge(s_ql[p], T // 4)
                pe.wait_ge(s_wl[p], (n + 1 - p) // 2)

            def products(g):
                y_at = [[y[:, c, bass.ds(g * N, N)] for c in range(DC)] for y in (yT_hi, yT_lo)]
                for k in range(NP):
                    b = k % BANKS
                    free(pe, s_ev[b], (NP // BANKS) * g + k // BANKS)
                    i, c0 = divmod(k, IC)
                    for c in range(DC):
                        hi, lo = (w[:, i, c, c0 * P:(c0 + 1) * P] for w in (guT_hi, guT_lo))
                        nc.tensor.matmul(ps[4 + b][:], hi, y_at[0][c], start=(c == 0), stop=False)
                        nc.tensor.matmul(ps[4 + b][:], hi, y_at[1][c], start=False, stop=False)
                        mm = nc.tensor.matmul(ps[4 + b][:], lo, y_at[0][c], start=False, stop=(c == DC - 1))
                    mm.then_inc(s_pr[b], 1)

            each(pe, TG, products)

            def down_products(m):
                for p in range(2):
                    this(pe, s_4["lo"], m, p)
                    free(pe, s_4["out"][p], m)
                    hi, lo = down_parts(p)
                    for c in range(IC):
                        nc.tensor.matmul(ps[p][:, 0:D], hi[:, c, :], dT_hi[:, c, :], start=(c == 0), stop=False)
                        nc.tensor.matmul(ps[p][:, 0:D], hi[:, c, :], dT_lo[:, c, :], start=False, stop=False)
                        mm = nc.tensor.matmul(ps[p][:, 0:D], lo[:, c, :], dT_hi[:, c, :], start=False, stop=(c == IC - 1))
                    mm.then_inc(s_4["product"][p], 1)

            each(pe, T // 2, down_products)

        @block.scalar
        def _(act):
            A = nc.scalar
            act.wait_ge(s_var, 1)
            A.activation(rstd[:], var[:], ACT.Sqrt).then_inc(s_root, 1)
            n = 0
            for i in range(3):
                for j in range(IC // 2):
                    p = n % 2
                    act.wait_ge(s_wt[p], n // 2 + 1)
                    bank = ps[p][:].rearrange("p (c r q) -> p c r q", c=2, r=DC)
                    A.activation(weight_parts(i, j, guT_hi, dT_hi), bank, ACT.Copy, scale=WEIGHT_SCALE).then_inc(s_wh[p], 1)
                    n += 1
            act.wait_ge(s_const, 3)
            act.wait_ge(s_scale, 1)

            def quantise_input(m):
                for p in range(2):
                    free(act, s_qt[p], m)
                    A.activation(work[0][p][:, 0:2 * D], flat[:, bass.ds((2 * m + p) * 2 * D, 2 * D)], ACT.Identity,
                                 bias=round_c[:], scale=to_int[:, 0:1]).then_inc(s_t[p], 1)
                    this(act, s_qt, m, p)
                    t0 = (2 * m + p) * 2 * P
                    A.activation(yT_hi[:, :, bass.ds(t0, 2 * P)], ps[2 + p][:].rearrange("p (c t) -> p c t", c=DC),
                                 ACT.Copy).then_inc(s_qh[p], 1)

            each(act, T // 4, quantise_input)

            def copy_products(g):
                for k in range(NP):
                    b = k % BANKS
                    act.wait_ge(s_pr[b], (NP // BANKS) * g + k // BANKS + 1)
                    if k < IC:
                        dst = act_all[:, k, bass.ds(g * N, N)]
                    else:
                        c = k - IC
                        free(act, s_us[c % 2], 16 * ((IC // 2) * g + c // 2))
                        if c >= 2:
                            act.wait_ge(s_mx[(k - 2) % BANKS], (NP // BANKS) * g + (k - 2) // BANKS + 1)
                        else:
                            k2 = NP - 2 + c
                            free(act, s_mx[k2 % BANKS], (NP // BANKS) * (g - 1) + k2 // BANKS + 1)
                        dst = u_out[c % 2][:]
                    A.activation(dst, ps[4 + b][:], ACT.Copy).then_inc(s_ev[b], 1)

            each(act, TG, copy_products)

            act.wait_ge(s_scale, 2)

            def sigmoid_steps(m):
                for p in range(2):
                    free(act, s_2["product"][p], m)
                    act.sem_inc(s_go)
                    part = flat[:, bass.ds((2 * m + p) * CB, CB)]
                    A.activation(work[0][p][:], part, ACT.Identity, bias=round_c[:], scale=to_int[:, 1:2]).then_inc(s_2["t"][p], 1)
                for p in range(2):
                    part = flat[:, bass.ds((2 * m + p) * CB, CB)]
                    this(act, s_2["int"], m, p)
                    act.sem_inc(s_go)
                    A.activation(work[1][p][:], part, ACT.Sigmoid, scale=scale[:, 1:2]).then_inc(s_2["sigmoid"][p], 1)
                    this(act, s_2["sigmoid"], m, p)
                    A.activation(work[0][p][:], work[1][p][:], ACT.Identity, bias=round_u[:], scale=2.0**16).then_inc(s_2["shift"][p], 1)

            each(act, STEPS // 2, sigmoid_steps)

            act.wait_ge(s_scale, 3)

            def scale_up_steps(m):
                for p in range(2):
                    part = flat[:, bass.ds((2 * m + p) * CB, CB)]
                    free(act, s_3["product"][p], m)
                    act.sem_inc(s_go)
                    A.activation(work[0][p][:], part, ACT.Identity, bias=round_c[:], scale=to_int[:, 3:4]).then_inc(s_3["t"][p], 1)
                    act.wait_ge(s_3["loaded"][p], 16 * (m + 1))
                    A.activation(work[1][p][:], later[:, (2 + p) * CB:(3 + p) * CB], ACT.Identity, bias=round_c[:],
                                 scale=to_int[:, 2:3]).then_inc(s_3["tu"][p], 1)

            each(act, STEPS // 2, scale_up_steps)

            act.wait_ge(s_scale, 4)

            def down_parts_steps(m):
                for p in range(2):
                    free(act, s_4["lo"][p], m)
                    act.sem_inc(s_go)
                    A.activation(work[0][p][:, 0:IC * P].rearrange("p (c t) -> p c t", c=IC), act_all[:, :, bass.ds((2 * m + p) * P, P)],
                                 ACT.Identity, bias=round_c[:], scale=to_int[:, 4:5]).then_inc(s_4["t"][p], 1)
                for p in range(2):
                    this(act, s_4["int"], m, p)
                    free(act, s_4["product"][p], m)
                    A.activation(down_parts(p)[0].rearrange("p c t -> p (c t)"), work[1][p][:, 0:IC * P], ACT.Copy).then_inc(s_4["hi"][p], 1)

            each(act, T // 2, down_parts_steps)

        @block.vector
        def _(dve):
            V = nc.vector
            order = Order(dve, s_dve)
            layernorm_scales(dve, order, x_all, stats, mean_var, var, rstd, rtmp, s_var, s_root)
            for t in range(T):
                order.tick(V.tensor_scalar(y_all[:, t, :], x_all[:, t, :], mean_var[:, t, 0:1], rstd[:, t:t + 1],
                                           ALU.subtract, ALU.mult))
            order.tick(V.memset(largest[:], 0.0))
            order.wait()
            order(V.tensor_reduce(step_max[:, 0:T], y_all, AX_X, ALU.max, apply_absolute_value=True))
            V.tensor_reduce(largest[:, 0, 0:1], step_max[:, 0:T], AX_X, ALU.max).then_inc(s_big, 1)

            for i in range(3):
                dve.wait_ge(s_w[i], 16)
                blocks = rows[i].rearrange("p (b k) -> p b k", k=BLOCK)
                to = scaled[i].rearrange("p (b k) -> p b k", k=BLOCK)
                s, inv = b_scale[:, i, :], b_inv[:, i, :]
                order(V.tensor_reduce(s, blocks, AX_X, ALU.max, apply_absolute_value=True))
                order(V.tensor_scalar(s, s, 1 / WQMAX, 1e-12, ALU.mult, ALU.max))
                order(V.reciprocal(inv, s))
                order(V.tensor_tensor(to, blocks, inv.unsqueeze(2).to_broadcast([P, NB, BLOCK]), ALU.mult))
                order(V.tensor_scalar(to, to, ROUND, -ROUND, ALU.add, ALU.add))
                V.tensor_tensor(to, to, s.unsqueeze(2).to_broadcast([P, NB, BLOCK]), ALU.mult).then_inc(s_deq, 1)
            n = 0
            for i in range(3):
                for j in range(IC // 2):
                    p = n % 2
                    dve.wait_ge(s_wh[p], n // 2 + 1)
                    bank = ps[p][:].rearrange("p (c r q) -> p c r q", c=2, r=DC)
                    for c in range(2):
                        ins = V.scalar_tensor_tensor(weight_parts(i, j, guT_lo, dT_lo)[:, c], bank[:, c], WEIGHT_SCALE,
                                                     weight_parts(i, j, guT_hi, dT_hi)[:, c], ALU.mult, ALU.subtract)
                    ins.then_inc(s_wl[p], 1)
                    n += 1

            def new_scale(n, col, unit):
                big = reduced[:, n, col:col + 1]
                c = {0: 0, 1: 1 + col, 2: 3, 3: 4}[n]
                if unit is not None:
                    order(V.tensor_scalar(tmp[:, c:c + 1], big, unit, None, ALU.mult))
                    big = tmp[:, c:c + 1]
                order(V.tensor_scalar(scale[:, c:c + 1], big, 1 / QMAX, 1e-12, ALU.mult, ALU.max))
                order(V.reciprocal(to_int[:, c:c + 1], scale[:, c:c + 1]))
                if unit is not None:
                    order(V.tensor_scalar(to_int[:, c:c + 1], to_int[:, c:c + 1], unit, None, ALU.mult))

            dve.wait_ge(s_red, 1)
            new_scale(0, 0, None)
            V.nop().then_inc(s_scale, 1)

            def input_steps(m):
                for p in range(2):
                    this(dve, s_t, m, p)
                    V.tensor_scalar(work[0][p][:, 0:2 * D], work[0][p][:, 0:2 * D], -ROUND, None, ALU.add).then_inc(s_q[p], 1)
                    this(dve, s_qh, m, p)
                    t0 = (2 * m + p) * 2 * P
                    V.tensor_tensor(yT_lo[:, :, bass.ds(t0, 2 * P)], ps[2 + p][:].rearrange("p (c t) -> p c t", c=DC),
                                    yT_hi[:, :, bass.ds(t0, 2 * P)], ALU.subtract).then_inc(s_ql[p], 1)

            each(dve, T // 4, input_steps)

            def product_maxima(g):
                for k in range(NP):
                    b = k % BANKS
                    dve.wait_ge(s_ev[b], (NP // BANKS) * g + k // BANKS + 1)
                    src = act_all[:, k, bass.ds(g * N, N)] if k < IC else u_out[k % 2][:]
                    V.tensor_reduce(maxes[:, k, bass.ds(g, 1)], src, AX_X, ALU.max, apply_absolute_value=True).then_inc(s_mx[b], 1)

            each(dve, TG, product_maxima)
            for b in range(BANKS):
                dve.wait_ge(s_mx[b], TG * NP // BANKS)
            order(V.tensor_scalar(unit[:, 0:1], scale[:, 0:1], 1 / WEIGHT_SCALE, None, ALU.mult))
            V.tensor_reduce(largest[:, 1, :], maxes[:].rearrange("p (i c) g -> p i (c g)", i=2), AX_X, ALU.max).then_inc(s_big, 1)
            dve.wait_ge(s_red, 2)
            new_scale(1, 0, unit[:, 0:1])
            new_scale(1, 1, unit[:, 0:1])
            V.nop().then_inc(s_scale, 1)

            def sigmoid_steps(m):
                for p in range(2):
                    this(dve, s_2["t"], m, p)
                    V.tensor_scalar(flat[:, bass.ds((2 * m + p) * CB, CB)], work[0][p][:], -ROUND, None, ALU.add).then_inc(s_2["int"][p], 1)
                for p in range(2):
                    this(dve, s_2["shift"], m, p)
                    V.tensor_scalar(work[1][p][:], work[0][p][:], 2.0**23 + 65535.0, -2.0**23, ALU.min, ALU.add).then_inc(s_2["sig"][p], 1)
                for p in range(2):
                    this(dve, s_2["product"], m, p)
                    V.tensor_reduce(step_max[:, bass.ds(2 * m + p, 1)], flat[:, bass.ds((2 * m + p) * CB, CB)], AX_X, ALU.max,
                                    apply_absolute_value=True).then_inc(s_2["max"][p], 1)

            each(dve, STEPS // 2, sigmoid_steps)
            for p in range(2):
                dve.wait_ge(s_2["max"][p], STEPS // 2)
            order(V.tensor_scalar(unit[:, 1:2], scale[:, 1:2], 2.0**-16, None, ALU.mult))
            V.tensor_reduce(largest[:, 2, 0:1], step_max[:, 0:STEPS], AX_X, ALU.max).then_inc(s_big, 1)
            dve.wait_ge(s_red, 3)
            new_scale(2, 0, unit[:, 1:2])
            V.nop().then_inc(s_scale, 1)

            def product_steps(m):
                for p in range(2):
                    part = flat[:, bass.ds((2 * m + p) * CB, CB)]
                    this(dve, s_3["t"], m, p)
                    V.tensor_scalar(part, work[0][p][:], -ROUND, None, ALU.add).then_inc(s_3["int"][p], 1)
                    this(dve, s_3["tu"], m, p)
                    this(dve, s_3["int"], m, p)
                    V.scalar_tensor_tensor(part, work[1][p][:], -ROUND, part, ALU.add, ALU.mult).then_inc(s_3["product"][p], 1)
                    this(dve, s_3["product"], m, p)
                    V.tensor_reduce(step_max[:, bass.ds(2 * m + p, 1)], part, AX_X, ALU.max, apply_absolute_value=True).then_inc(s_3["max"][p], 1)

            each(dve, STEPS // 2, product_steps)
            for p in range(2):
                dve.wait_ge(s_3["max"][p], STEPS // 2)
            order(V.tensor_tensor(unit[:, 2:3], scale[:, 2:3], scale[:, 3:4], ALU.mult))
            V.tensor_reduce(largest[:, 3, 0:1], step_max[:, 0:STEPS], AX_X, ALU.max).then_inc(s_big, 1)
            dve.wait_ge(s_red, 4)
            new_scale(3, 0, unit[:, 2:3])
            order(V.tensor_scalar(tmp[:, 4:5], scale[:, 4:5], 1 / WEIGHT_SCALE, None, ALU.mult))
            V.nop().then_inc(s_scale, 1)

            def down_steps(m):
                for p in range(2):
                    this(dve, s_4["t"], m, p)
                    V.tensor_scalar(work[1][p][:, 0:IC * P], work[0][p][:, 0:IC * P], -ROUND, None, ALU.add).then_inc(s_4["int"][p], 1)
                for p in range(2):
                    this(dve, s_4["hi"], m, p)
                    V.tensor_tensor(down_parts(p)[1].rearrange("p c t -> p (c t)"), work[1][p][:, 0:IC * P],
                                    down_parts(p)[0].rearrange("p c t -> p (c t)"), ALU.subtract).then_inc(s_4["lo"][p], 1)
                for p in range(2):
                    this(dve, s_4["product"], m, p)
                    free(dve, s_4["stored"][p], 16 * m)
                    V.scalar_tensor_tensor(u_out[p][:, 0:D], ps[p][:, 0:D], tmp[:, 4:5],
                                           x_all[:, bass.ds(2 * m + p, 1), :].rearrange("p a d -> p (a d)"), ALU.mult, ALU.add).then_inc(s_4["out"][p], 1)

            each(dve, T // 2, down_steps)


def two_layers(nc, x, context, mask, e2, e1, attn, ffn, out):
    tokens, D = x.shape
    E = e1["wg"].shape[1]
    I = ffn["w_gate"].shape[0]
    x_sum = nc.dram_tensor("x_sum", (tokens + P, D), F32, kind="Internal").ap()
    normed = nc.dram_tensor("normed", (tokens + P, D), F32, kind="Internal").ap()
    up_raw = nc.dram_tensor("up_raw", (P, I // P, tokens), F32, kind="Internal").ap()
    experts(nc, "top2", x, context, e2["wg"], e2["bg"], e2["w1"], e2["b1"], e2["w2"], e2["b2"], x_sum, normed, 2, None)
    experts(nc, "top1", x_sum[0:tokens], None, e1["wg"], None, e1["w1"], e1["b1"], e1["w2"], e1["b2"], x_sum, normed, 1,
            tokens // E)
    with nc.sbuf_tensor("x_held", [P, tokens // P, D], F32) as x_held:
        attention(nc, "attn", x_held, x_sum[0:tokens], context, mask, **attn)
        gated_ffn(nc, "ffn", x_held, ffn["w_gate"], ffn["w_up"], ffn["w_down"], up_raw, out)


NAMES = ["x", "ctx_1024", "mask_1x1xSxS2_ik1",
         "L0_xattn_Wg", "L0_xattn_bg", "L0_xattn_W1", "L0_xattn_b1", "L0_xattn_W2", "L0_xattn_b2",
         "L0_ffn_wg", "L0_ffn_w1", "L0_ffn_b1", "L0_ffn_w2", "L0_ffn_b2",
         "L1_xattn_wq_w", "L1_xattn_wq_b", "L1_xattn_wk_w", "L1_xattn_wk_b",
         "L1_xattn_wv_w", "L1_xattn_wv_b", "L1_xattn_wo_w", "L1_xattn_wo_b",
         "L1_ffn_w_gate", "L1_ffn_w_up", "L1_ffn_w_down"]


def kernel(**inputs):
    import numpy as np
    import concourse.bacc as bacc
    from concourse.bass_utils import run_bass_kernel_spmd

    nc = bacc.Bacc("TRN2", target_bir_lowering=False, num_devices=1)
    arrays, a = {}, {}
    for name in NAMES:
        array = np.ascontiguousarray(inputs[name])
        arrays[f"in_{name}"] = array
        a[name] = nc.dram_tensor(f"in_{name}", array.shape, mybir.dt.from_np(array.dtype), kind="ExternalInput").ap()
    shape = inputs["x"].shape
    out = nc.dram_tensor("out", shape, F32, kind="ExternalOutput").ap()
    rows = [t.rearrange("b s d -> (b s) d") for t in (a["x"], a["ctx_1024"], out)]
    two_layers(nc, rows[0], rows[1], a["mask_1x1xSxS2_ik1"],
               {k.lower(): a[f"L0_xattn_{k}"] for k in ("Wg", "bg", "W1", "b1", "W2", "b2")},
               {k: a[f"L0_ffn_{k}"] for k in ("wg", "w1", "b1", "w2", "b2")},
               {k[0:2] if k[3] == "w" else "b" + k[1]: a[f"L1_xattn_{k}"]
                for k in ("wq_w", "wq_b", "wk_w", "wk_b", "wv_w", "wv_b", "wo_w", "wo_b")},
               {k: a[f"L1_ffn_{k}"] for k in ("w_gate", "w_up", "w_down")},
               rows[2])
    result = run_bass_kernel_spmd(nc, [arrays], core_ids=[0])
    return result.results[0]["out"]
```

```python
import concourse.bass as bass
from concourse import mybir
from contextlib import ExitStack, contextmanager

F32 = mybir.dt.float32
F16 = mybir.dt.float16
I32 = mybir.dt.int32
ALU = mybir.AluOpType
ACT = mybir.ActivationFunctionType
AX_X = mybir.AxisListType.X
P = 128
WEIGHT_SCALE = 64.0
ROUND = 1.5 * 2.0**23
EPS = 1e-05


@contextmanager
def stage_semaphores(nc, name):
    held = []

    def sem(n):
        held.append(nc.alloc_semaphore(name=f"{name}_{n}"))
        return held[-1]

    yield sem
    nc.clear_and_free_semaphores(held)
    nc.all_engine_barrier()


class Order:

    def __init__(self, engine, semaphore):
        self.engine, self.semaphore, self.count = engine, semaphore, 0

    def __call__(self, instruction):
        instruction.then_inc(self.semaphore, 1)
        self.count = self.count + 1
        self.engine.wait_ge(self.semaphore, self.count)

    def tick(self, instruction):
        instruction.then_inc(self.semaphore, 1)
        self.count = self.count + 1

    def wait(self):
        self.engine.wait_ge(self.semaphore, self.count)


def free(engine, semaphore, value):
    if not (isinstance(value, int) and value <= 0):
        engine.wait_ge(semaphore, value)


def each(engine, n, body):
    body(0)
    with engine.Fori(1, n) as m:
        body(m)


def staggered(engine, count, *steps):
    ahead, behind = max(d for _, d in steps), -min(d for _, d in steps)

    def pair(m):
        for p in range(2):
            for step, distance in steps:
                j = p + distance
                if not isinstance(m, int) or 0 <= 2 * m + j < count:
                    step(m + j // 2, j % 2)

    start, end = 1 + (behind + 1) // 2, (count - ahead) // 2
    for m in range(-((ahead + 1) // 2), start):
        pair(m)
    with engine.Fori(start, end) as m:
        pair(m)
    for m in range(end, (count + behind + 1) // 2):
        pair(m)


def layernorm_scales(dve, order, x_all, stats, mean_var, var, rstd, rtmp, s_var, s_root):
    V = dve
    T = x_all.shape[1]
    for t in range(T):
        order.tick(V.bn_stats(stats[:, t, :], x_all[:, t, :]))
    order.wait()
    for t in range(T):
        order.tick(V.bn_aggr(mean_var[:, t, :], stats[:, t, :]))
    order.wait()
    V.tensor_scalar(var[:], mean_var[:, :, 1], EPS, None, ALU.add).then_inc(s_var, 1)
    dve.wait_ge(s_root, 1)
    order(V.reciprocal(rstd[:], rstd[:]))
    order(V.tensor_tensor(rtmp[:], rstd[:], rstd[:], ALU.mult))
    order(V.tensor_tensor(rtmp[:], rtmp[:], var[:], ALU.mult))
    order(V.tensor_scalar(rtmp[:], rtmp[:], -0.5, 1.5, ALU.mult, ALU.add))
    order(V.tensor_tensor(rstd[:], rstd[:], rtmp[:], ALU.mult))


def broadcast_rows(ap, rows, n):
    return bass.AP(tensor=ap.tensor, offset=ap.offset, ap=[[0, rows], [1, n]])


def experts(nc, name, x, gate_source, wg, bg, w1, b1, w2, b2, x_sum, normed, choices, capacity):
    tokens, D = x.shape
    E = wg.shape[1]
    F = w1.shape[2]
    T, DC, FC = tokens // P, D // P, F // P
    if capacity is None:
        NS = (choices * tokens + E * (P - 1)) // P
        NS += -NS % 2
    else:
        NS = E * capacity // P
    CHUNK = 1024
    CPE = 2 * DC * F // CHUNK
    assert DC * F == FC * D and CPE == 4 and DC == 2 and FC == 8
    GC = 2

    with ExitStack() as ctx:
        sem = ctx.enter_context(stage_semaphores(nc, name))

        def sb(n, shape, dt):
            return ctx.enter_context(nc.sbuf_tensor(f"{name}_{n}", shape, dt))

        def pb(n, shape, dt):
            return ctx.enter_context(nc.psum_tensor(f"{name}_{n}", shape, dt))


        w_hi = sb("w_hi", [P, E, CPE, CHUNK], F16)
        w_lo = sb("w_lo", [P, E, CPE, CHUNK], F16)
        staged = [sb(f"staged{c}", [P, CHUNK], F32) for c in range(CPE)]
        x_all = sb("x_all", [P, T, D], F32)
        flat = x_all[:].rearrange("p t d -> p (t d)")
        h32 = [flat[:, p * F:(p + 1) * F] for p in range(2)]
        halves = flat[:, 2 * F:4 * F].bitcast(F16)
        h_hi = [halves[:, p * F:(p + 1) * F].rearrange("p (c t) -> p c t", c=FC) for p in range(2)]
        h_lo = [halves[:, (2 + p) * F:(3 + p) * F].rearrange("p (c t) -> p c t", c=FC) for p in range(2)]
        xg = [flat[:, 4 * F + p * D:4 * F + (p + 1) * D] for p in range(2)]
        y = [flat[:, 4 * F + (2 + p) * D:4 * F + (3 + p) * D] for p in range(2)]
        xT_hi = [sb(f"xT_hi{p}", [P, DC, P], F16) for p in range(2)]
        xT_lo = [sb(f"xT_lo{p}", [P, DC, P], F16) for p in range(2)]
        gate_in = [sb(f"gate_in{p}", [P, GC, D], F32) for p in range(2)]
        gateT = [sb(f"gateT{p}", [P, DC, P], F32) for p in range(2)]
        b1_rows = sb("b1_rows", [E * FC, P], F32)
        b1T = sb("b1T", [P, E * FC], F32)
        b2_all = sb("b2_all", [P, E, D], F32)
        wg_sb = sb("wg_sb", [P, DC, E], F32)
        bg_sb = sb("bg_sb", [P, E], F32)
        ident = sb("ident", [P, P], F32)
        before = sb("before", [P, P], F16)
        ones = sb("ones", [P, P], F16)
        expert_no = sb("expert_no", [P, E], F32)
        lane_no = sb("lane_no", [P, P], F32)
        pad_row = sb("pad_row", [P, 1], F32)
        token_1 = sb("token_1", [P, T], F32)
        stats = sb("stats", [P, T, 6], F32)
        mean_var = sb("mean_var", [P, T, 2], F32)
        rstd = sb("rstd", [P, T], F32)
        rtmp = sb("rtmp", [P, T], F32)
        logits = sb("logits", [P, T, E], F32)
        work = sb("work", [P, T, E], F32)
        onehot = [sb(f"onehot{c}", [P, T, E], F32) for c in range(choices)]
        oh16 = sb("oh16", [P, T, E], F16)
        best = [sb(f"best{c}", [P, T], F32) for c in range(choices)]
        first = sb("first", [P, T], F32)
        weight = [sb(f"weight{c}", [P, T], F32) for c in range(choices)]
        total = sb("total", [P, E, T], F32)
        running = sb("running", [P, E, T], F32)
        one_t = sb("one_t", [P, T], F32)
        tiles_of = sb("tiles_of", [P, E], F32)
        start_of = sb("start_of", [P, E], F32)
        ends_of = sb("ends_of", [P, E], F32)
        slot_div = [sb(f"slot_div{c}", [P, T], F32) for c in range(choices)]
        slot_mod = [sb(f"slot_mod{c}", [P, T], F32) for c in range(choices)]
        pick_lane = [sb(f"pick_lane{p}", [P, P], F32) for p in range(2)]
        pick_tile = [sb(f"pick_tile{p}", [P, 2, NS], F32) for p in range(2)]
        row_f = sb("row_f", [P, NS], F32)
        pad_f = sb("pad_f", [P, NS], F32)
        row_of_slot = sb("row_of_slot", [P, NS], I32)
        weight_of_slot = sb("weight_of_slot", [P, NS], F32)
        expert_f = sb("expert_f", [P, NS], F32)
        expert_of_tile = sb("expert_of_tile", [P, NS], I32)
        rows_in = [sb(f"rows_in{p}", [P, 1], I32) for p in range(2)]
        rows_out = [sb(f"rows_out{p}", [P, 1], I32) for p in range(2)]

        xT_ps = [pb(f"xT_ps{p}", [P, 512], F32) for p in range(2)]
        h_ps = [pb(f"h_ps{p}", [P, 2, 512], F32) for p in range(2)]
        y_ps = [pb(f"y_ps{p}", [P, 512], F32) for p in range(2)]

        s_x = [sem(f"x_quarter{q}_loaded") for q in range(4)]; s_small = sem("small_loaded"); s_gate_in = [sem(f"gate_in{p}_loaded") for p in range(2)]
        s_staged = [sem(f"staged{c}_loaded") for c in range(CPE)]
        s_hi = sem("w_hi_done"); s_split = sem("w_split")
        s_const = sem("constants"); s_pool = sem("pool_order"); s_dve = sem("dve_order"); s_act = sem("act_order")
        s_var = sem("variances"); s_root = sem("roots"); s_normed = sem("normed"); s_stored = sem("normed_stored"); s_begun = sem("x_sum_begun")
        s_go = sem("pool_goes_on")
        s_b1 = sem("b1_transposed"); s_b1T = sem("b1T_ready")
        s_tr = [sem(f"gate_transposed{p}") for p in range(2)]; s_trc = [sem(f"gateT{p}_ready") for p in range(2)]
        s_lg = [sem(f"logits_from{p}") for p in range(2)]
        s_diff = sem("exp_in"); s_exp = sem("exp_out")
        s_oh = sem("onehots"); s_count = sem("counts")
        s_pick = [sem(f"picks{p}_ready") for p in range(2)]; s_picked = [sem(f"picks{p}_used") for p in range(2)]
        s_table = sem("tables_ready")
        s_rows_in = [sem(f"rows_in{p}_copied") for p in range(2)]; s_rows_out = [sem(f"rows_out{p}_copied") for p in range(2)]
        s_xg = [sem(f"xg{p}_gathered") for p in range(2)]; s_xt = [sem(f"xT{p}_transposed") for p in range(2)]
        s_xh = [sem(f"xT_hi{p}_ready") for p in range(2)]; s_xl = [sem(f"xT_lo{p}_ready") for p in range(2)]
        s_h = [sem(f"h{p}_banks") for p in range(2)]; s_h32 = [sem(f"h32_{p}_ready") for p in range(2)]
        s_hh = [sem(f"h_hi{p}_ready") for p in range(2)]; s_hl = [sem(f"h_lo{p}_ready") for p in range(2)]
        s_l2 = [sem(f"y_ps{p}_ready") for p in range(2)]; s_yb = [sem(f"y{p}_biased") for p in range(2)]; s_y = [sem(f"y{p}_ready") for p in range(2)]
        s_added = [sem(f"y{p}_added") for p in range(2)]

        M = NS // 2
        HEAD = 4
        block = ctx.enter_context(nc.Block())

        @block.sync
        def _(sp):
            x_tiles = x.rearrange("(t p) d -> p t d", p=P)
            for q in range(4):
                n = T // 4
                sp.dma_start(x_all[:, q * n:(q + 1) * n, :], x_tiles[:, q * n:(q + 1) * n, :]).then_inc(s_x[q], 16)
            sp.dma_start(wg_sb[:], wg.rearrange("(c p) e -> p c e", p=P)).then_inc(s_small, 16)
            if bg is not None:
                sp.dma_start(bg_sb[:], broadcast_rows(bg, P, E)).then_inc(s_small, 16)
            sp.dma_start(b1_rows[:], b1.rearrange("e (c f) -> (e c) f", f=P)).then_inc(s_small, 16)
            sp.dma_start(b2_all[:].rearrange("p e d -> p (e d)"), broadcast_rows(b2, P, E * D)).then_inc(s_small, 16)

            def load_expert(e):
                w1_e = w1[e].rearrange("(c p) f -> p c f", p=P)
                w2_e = w2[e].rearrange("(c p) d -> p c d", p=P)
                for c in range(CPE):
                    if not (isinstance(e, int) and e == 0):
                        sp.wait_ge(s_split, (e - 1) * CPE + c + 1)
                    if c < 2:
                        sp.dma_start(staged[c][:], w1_e[:, c, :]).then_inc(s_staged[c], 16)
                    else:
                        sp.dma_start(staged[c][:].rearrange("p (c d) -> p c d", d=D),
                                     w2_e[:, (c - 2) * 4:(c - 1) * 4, :]).then_inc(s_staged[c], 16)

            if gate_source is not None:
                g_tiles = gate_source.rearrange("(t p) d -> p t d", p=P)
                for p in range(2):
                    sp.dma_start(gate_in[p][:], g_tiles[:, p * GC:(p + 1) * GC, :]).then_inc(s_gate_in[p], 16)
                load_expert(0)
                with sp.Fori(1, T // GC // 2) as m:
                    for p in range(2):
                        for k in range(GC):
                            sp.wait_ge(s_tr[k], 2 * m - 1 + p)
                        sp.dma_start(gate_in[p][:], g_tiles[:, bass.ds((2 * m + p) * GC, GC), :]).then_inc(s_gate_in[p], 16)
            else:
                load_expert(0)
            sp.wait_ge(s_normed, 1)
            n_tiles = normed[0:tokens].rearrange("(t p) d -> p t d", p=P)
            sp.dma_start(n_tiles, x_all[:]).then_inc(s_stored, 16)
            sp.dma_start(normed[tokens:tokens + P], x_all[:, 0, :]).then_inc(s_stored, 16)
            with sp.Fori(1, E) as e:
                load_expert(e)
            for p in range(2):
                sp.wait_ge(s_added[p], 16 * M)

        @block.gpsimd
        def _(pool):
            order = Order(pool, s_pool)
            order(nc.gpsimd.memset(ident[:], 0.0))
            order(nc.gpsimd.memset(before[:], 1.0))
            nc.gpsimd.memset(ones[:], 1.0).then_inc(s_const, 1)
            nc.gpsimd.memset(one_t[:], 1.0).then_inc(s_const, 1)
            nc.gpsimd.affine_select(out=ident[:], in_=ident[:], compare_op=ALU.not_equal, fill=1.0, base=0,
                                    pattern=[[-1, P]], channel_multiplier=1).then_inc(s_const, 1)
            nc.gpsimd.affine_select(out=before[:], in_=before[:], compare_op=ALU.is_gt, fill=0.0, base=0,
                                    pattern=[[1, P]], channel_multiplier=-1).then_inc(s_const, 1)
            kw = dict(allow_small_or_imprecise_dtypes=True)
            nc.gpsimd.iota(expert_no[:], pattern=[[1, E]], base=0, channel_multiplier=0, **kw).then_inc(s_const, 1)
            nc.gpsimd.iota(lane_no[:], pattern=[[1, P]], base=0, channel_multiplier=0, **kw).then_inc(s_const, 1)
            nc.gpsimd.iota(pad_row[:], pattern=[[1, 1]], base=tokens + 1, channel_multiplier=1, **kw).then_inc(s_const, 1)
            nc.gpsimd.iota(token_1[:], pattern=[[P, T]], base=1, channel_multiplier=1, **kw).then_inc(s_const, 1)

            def gather(m, p, i):
                free(pool, s_xt[p], m)
                nc.gpsimd.tensor_copy(rows_in[p][:], row_of_slot[:, bass.ds(i, 1)]).then_inc(s_rows_in[p], 1)
                pool.wait_ge(s_rows_in[p], m + 1)
                pool.sem_inc(s_go)
                nc.gpsimd.indirect_dma_start(out=xg[p], out_offset=None, in_=normed,
                                             in_offset=bass.IndirectOffsetOnAxis(ap=rows_in[p][:, 0:1], axis=0)
                                             ).then_inc(s_xg[p], 16)

            def add(m, p, i):
                if p == 1:
                    pool.wait_ge(s_added[0], 16 * (m + 1))
                else:
                    free(pool, s_added[1], 16 * m)
                nc.gpsimd.tensor_copy(rows_out[p][:], row_of_slot[:, bass.ds(i, 1)]).then_inc(s_rows_out[p], 1)
                pool.wait_ge(s_rows_out[p], m + 1)
                pool.wait_ge(s_y[p], m + 1)
                pool.sem_inc(s_go)
                nc.gpsimd.indirect_dma_start(out=x_sum, out_offset=bass.IndirectOffsetOnAxis(ap=rows_out[p][:, 0:1], axis=0),
                                             in_=y[p], in_offset=None, compute_op=ALU.add).then_inc(s_added[p], 16)

            pool.wait_ge(s_table, 1)
            pool.wait_ge(s_stored, 32)
            gather(0, 0, 0)
            gather(0, 1, 1)
            gather(1, 0, 2)
            gather(1, 1, 3)
            if gate_source is not None:
                pool.wait_ge(s_begun, 32)
            add(0, 0, 0)
            with pool.Fori(2, M) as m:
                gather(m, 0, 2 * m)
                add(m - 2, 1, 2 * m - 3)
                gather(m, 1, 2 * m + 1)
                add(m - 1, 0, 2 * m - 2)
            add(M - 2, 1, NS - 3)
            add(M - 1, 0, NS - 2)
            add(M - 1, 1, NS - 1)

        def w1_at(w, e, dc, fc):
            return w[:, bass.ds(e, 1), dc, fc * P:(fc + 1) * P].rearrange("p a f -> p (a f)")

        def w2_at(w, e, fc):
            c, r = divmod(fc * D, CHUNK)
            return w[:, bass.ds(e, 1), 2 + c, r:r + D].rearrange("p a f -> p (a f)")

        @block.tensor
        def _(pe):
            pe.wait_ge(s_const, 8)
            pe.wait_ge(s_small, 48 + 16 * (bg is not None))
            nc.tensor.transpose(y_ps[0][:, 0:E * FC], b1_rows[:], ident[0:E * FC, 0:E * FC]).then_inc(s_b1, 1)
            lg = y_ps[1]
            if gate_source is None:
                pe.wait_ge(s_normed, 1)

            def gate_transpose(m, k, p):
                free(pe, s_trc[p], m * GC + k // 2)
                if gate_source is not None:
                    g = k // GC
                    if k % GC == 0:
                        pe.wait_ge(s_gate_in[g], 16 * (m + 1))
                    src = gate_in[g][:, k % GC, :]
                    for c in range(DC):
                        last = nc.tensor.transpose(xT_ps[p][:, c * P:(c + 1) * P], src[:, c * P:(c + 1) * P], ident[:])
                    last.then_inc(s_tr[p], 1)
                else:
                    for c in range(DC):
                        src = x_all[:, bass.ds(2 * GC * m + k, 1), c * P:(c + 1) * P].rearrange("p a d -> p (a d)") if not isinstance(m, int) else x_all[:, 2 * GC * m + k, c * P:(c + 1) * P]
                        last = nc.tensor.transpose(xT_ps[p][:, c * P:(c + 1) * P], src, ident[:])
                    last.then_inc(s_tr[p], 1)

            def gate_logits(m, k, p):
                pe.wait_ge(s_trc[p], m * GC + k // 2 + 1)
                t = 2 * GC * m + k
                for c in range(DC):
                    last = nc.tensor.matmul(lg[:, bass.ds(t * E, E)], gateT[p][:, c, :], wg_sb[:, c, :],
                                            start=(c == 0), stop=(c == DC - 1))
                last.then_inc(s_lg[p], 1)

            if gate_source is not None:
                def gate_tiles(m):
                    for k in range(2 * GC):
                        gate_transpose(m, k, k % 2)
                        if k % 2:
                            gate_logits(m, k - 1, 0)
                            gate_logits(m, k, 1)

                each(pe, T // GC // 2, gate_tiles)
            else:
                for m in range(T // GC // 2):
                    for k in range(2 * GC):
                        gate_transpose(m, k, k % 2)
                        if k % 2:
                            gate_logits(m, k - 1, 0)
                            gate_logits(m, k, 1)
            pe.wait_ge(s_oh, 1)
            pairs = oh16[:].rearrange("p t e -> p (t e)")
            nc.tensor.matmul(h_ps[0][:, 0, 0:T * E], before[:], pairs, start=True, stop=True)
            nc.tensor.matmul(h_ps[0][:, 1, 0:T * E], ones[:], pairs, start=True, stop=True).then_inc(s_count, 1)
            rounds = T * choices
            table = h_ps[1][:, 0, 0:2 * NS]

            def pick(m, p, start, stop):
                pe.wait_ge(s_pick[p], m + 1)
                nc.tensor.matmul(table, pick_lane[p][:], pick_tile[p][:].rearrange("p a n -> p (a n)"),
                                 start=start, stop=stop, skip_group_check=True).then_inc(s_picked[p], 1)

            pick(0, 0, True, False)
            pick(0, 1, False, False)
            with pe.Fori(1, rounds // 2 - 1) as m:
                for p in range(2):
                    pick(m, p, False, False)
            pick(rounds // 2 - 1, 0, False, False)
            pick(rounds // 2 - 1, 1, False, True)

            def transpose_in(m, p):
                pe.wait_ge(s_xg[p], 16 * (m + 1))
                if isinstance(m, int) and m == 0:
                    pe.wait_ge(s_table, 1)
                else:
                    pe.wait_ge(s_xl[p], m)
                for c in range(DC):
                    last = nc.tensor.transpose(xT_ps[p][:, c * P:(c + 1) * P], xg[p][:, c * P:(c + 1) * P], ident[:])
                last.then_inc(s_xt[p], 1)

            def layer1(m, p, i):
                e = pe.value_load(expert_of_tile[0:1, bass.ds(i, 1)], min_val=0, max_val=E - 1)
                pe.wait_ge(s_split, (e + 1) * CPE)
                pe.wait_ge(s_xl[p], m + 1)
                free(pe, s_h32[p], 2 * m)
                for b in range(2):
                    for q in range(4):
                        fc = 4 * b + q
                        out = h_ps[p][:, b, q * P:(q + 1) * P]
                        for c in range(DC):
                            hi, lo = w1_at(w_hi, e, c, fc), w1_at(w_lo, e, c, fc)
                            nc.tensor.matmul(out, hi, xT_hi[p][:, c, :], start=(c == 0), stop=False)
                            nc.tensor.matmul(out, hi, xT_lo[p][:, c, :], start=False, stop=False)
                            last = nc.tensor.matmul(out, lo, xT_hi[p][:, c, :], start=False, stop=(c == DC - 1))
                    last.then_inc(s_h[p], 1)

            def layer2(m, p, i):
                e = pe.value_load(expert_of_tile[0:1, bass.ds(i, 1)], min_val=0, max_val=E - 1)
                pe.wait_ge(s_hl[p], 2 * (m + 1))
                free(pe, s_yb[p], m)
                out = y_ps[p][:, 0:D]
                for fc in range(FC):
                    hi, lo = w2_at(w_hi, e, fc), w2_at(w_lo, e, fc)
                    nc.tensor.matmul(out, h_hi[p][:, fc, :], hi, start=(fc == 0), stop=False)
                    nc.tensor.matmul(out, h_hi[p][:, fc, :], lo, start=False, stop=False)
                    last = nc.tensor.matmul(out, h_lo[p][:, fc, :], hi, start=False, stop=(fc == FC - 1))
                last.then_inc(s_l2[p], 1)

            transpose_in(0, 0)
            transpose_in(0, 1)
            layer1(0, 0, 0)

            def pair(m):
                layer1(m, 1, 2 * m + 1)
                transpose_in(m + 1, 0)
                layer2(m, 0, 2 * m)
                layer1(m + 1, 0, 2 * m + 2)
                transpose_in(m + 1, 1)
                layer2(m, 1, 2 * m + 1)

            each(pe, M - 1, pair)
            layer1(M - 1, 1, NS - 1)
            layer2(M - 1, 0, NS - 2)
            layer2(M - 1, 1, NS - 1)

        def split_hi(act, e):
            for c in range(CPE):
                act.wait_ge(s_staged[c], 16 * (e + 1))
                nc.scalar.activation(w_hi[:, e, c, :], staged[c][:], ACT.Copy, scale=WEIGHT_SCALE).then_inc(s_hi, 1)

        @block.scalar
        def _(act):
            if gate_source is not None:
                act.dma_start(x_sum[0:tokens], x).then_inc(s_begun, 16)
                act.dma_start(x_sum[tokens:tokens + P], x[0:P]).then_inc(s_begun, 16)
            act.wait_ge(s_var, 1)
            nc.scalar.activation(rstd[:], rtmp[:], ACT.Sqrt).then_inc(s_root, 1)
            act.wait_ge(s_b1, 1)
            nc.scalar.activation(b1T[:], y_ps[0][:, 0:E * FC], ACT.Copy).then_inc(s_b1T, 1)
            split_hi(act, 0)

            def gate_copy(n, p):
                act.wait_ge(s_tr[p], n + 1)
                if not (isinstance(n, int) and n == 0):
                    act.wait_ge(s_lg[p], n)
                nc.scalar.activation(gateT[p][:].rearrange("p c t -> p (c t)"), xT_ps[p][:, 0:D], ACT.Copy).then_inc(s_trc[p], 1)

            gate_copy(0, 0)
            gate_copy(0, 1)
            with act.Fori(1, T // 2) as n:
                for p in range(2):
                    gate_copy(n, p)
            act.wait_ge(s_diff, 1)
            if choices == 2:
                nc.scalar.activation(weight[1][:], rtmp[:], ACT.Exp).then_inc(s_exp, 1)
            else:
                nc.scalar.activation(work[:], work[:], ACT.Exp).then_inc(s_exp, 1)

            def x_high(m, p):
                act.wait_ge(s_xt[p], m + 1)
                free(act, s_h[p], 2 * m)
                nc.scalar.activation(xT_hi[p][:].rearrange("p c t -> p (c t)"), xT_ps[p][:, 0:D], ACT.Copy).then_inc(s_xh[p], 1)

            def hidden(m, p, i):
                e = act.value_load(expert_of_tile[0:1, bass.ds(i, 1)], min_val=0, max_val=E - 1)
                for b in range(2):
                    act.wait_ge(s_h[p], 2 * m + b + 1)
                    free(act, s_hl[p], 2 * m)
                    for q in range(4):
                        fc = 4 * b + q
                        last = nc.scalar.activation(h32[p][:, fc * P:(fc + 1) * P], h_ps[p][:, b, q * P:(q + 1) * P],
                                                    ACT.Relu, bias=b1T[:, bass.ds(e * FC + fc, 1)], scale=1 / WEIGHT_SCALE)
                    last.then_inc(s_h32[p], 1)

            act.wait_ge(s_table, 1)
            x_high(0, 0)
            x_high(0, 1)
            hidden(0, 0, 0)
            for m in range(HEAD):
                split_hi(act, 2 * m + 1)
                hidden(m, 1, 2 * m + 1)
                x_high(m + 1, 0)
                if 2 * m + 2 < E:
                    split_hi(act, 2 * m + 2)
                hidden(m + 1, 0, 2 * m + 2)
                x_high(m + 1, 1)
            with act.Fori(HEAD, M - 1) as m:
                hidden(m, 1, 2 * m + 1)
                x_high(m + 1, 0)
                hidden(m + 1, 0, 2 * m + 2)
                x_high(m + 1, 1)
            hidden(M - 1, 1, NS - 1)

        def split_lo(dve, e):
            for c in range(CPE):
                dve.wait_ge(s_hi, e * CPE + c + 1)
                nc.vector.scalar_tensor_tensor(w_lo[:, e, c, :], staged[c][:], WEIGHT_SCALE, w_hi[:, e, c, :],
                                               ALU.mult, ALU.subtract).then_inc(s_split, 1)

        @block.vector
        def _(dve):
            V = nc.vector
            order = Order(dve, s_dve)
            for t in range(T):
                if t % (T // 4) == 0:
                    dve.wait_ge(s_x[t // (T // 4)], 16)
                order.tick(V.bn_stats(stats[:, t, :], x_all[:, t, :]))
            order.wait()
            for t in range(T):
                order.tick(V.bn_aggr(mean_var[:, t, :], stats[:, t, :]))
            order.wait()
            V.tensor_scalar(rtmp[:], mean_var[:, :, 1], EPS, None, ALU.add).then_inc(s_var, 1)
            dve.wait_ge(s_root, 1)
            order(V.reciprocal(rstd[:], rstd[:]))
            order(V.tensor_tensor(first[:], rstd[:], rstd[:], ALU.mult))
            order(V.tensor_tensor(first[:], first[:], rtmp[:], ALU.mult))
            order(V.tensor_scalar(first[:], first[:], -0.5, 1.5, ALU.mult, ALU.add))
            order(V.tensor_tensor(rstd[:], rstd[:], first[:], ALU.mult))
            for t in range(T):
                order.tick(V.tensor_scalar(x_all[:, t, :], x_all[:, t, :], mean_var[:, t, 0:1], rstd[:, t:t + 1],
                                           ALU.subtract, ALU.mult))
            order.wait()
            V.nop().then_inc(s_normed, 1)
            split_lo(dve, 0)

            def by_expert(ap):
                return ap.unsqueeze(2).to_broadcast([P, T, E])

            def of_expert(ap):
                return ap.unsqueeze(1).to_broadcast([P, T, E])

            dve.wait_ge(s_const, 8)
            for p in range(2):
                dve.wait_ge(s_lg[p], T // 2)
            lg = y_ps[1][:, 0:T * E].rearrange("p (t e) -> p t e", e=E)
            if bg is not None:
                order(V.tensor_tensor(logits[:], lg, of_expert(bg_sb[:]), ALU.add))
            else:
                order(V.tensor_copy(logits[:], lg))
            for c in range(choices):
                order(V.tensor_reduce(best[c][:], logits[:], AX_X, ALU.max))
                order(V.tensor_tensor(work[:], logits[:], by_expert(best[c][:]), ALU.is_lt))
                order(V.tensor_scalar(work[:], work[:], float(E), None, ALU.mult))
                order(V.tensor_tensor(work[:], work[:], of_expert(expert_no[:]), ALU.add))
                order(V.tensor_reduce(first[:], work[:], AX_X, ALU.min))
                order(V.tensor_tensor(onehot[c][:], of_expert(expert_no[:]), by_expert(first[:]), ALU.is_equal))
                if c + 1 < choices:
                    order(V.tensor_scalar(work[:], onehot[c][:], -3e38, None, ALU.mult))
                    order(V.tensor_tensor(logits[:], logits[:], work[:], ALU.add))
            if choices == 2:
                order(V.tensor_tensor(oh16[:], onehot[0][:], onehot[1][:], ALU.add))
                V.nop().then_inc(s_oh, 1)
                order(V.tensor_tensor(rtmp[:], best[1][:], best[0][:], ALU.subtract))
                V.nop().then_inc(s_diff, 1)
                dve.wait_ge(s_exp, 1)
                order(V.tensor_scalar(weight[0][:], weight[1][:], 1.0, None, ALU.add))
                order(V.reciprocal(weight[0][:], weight[0][:]))
                order(V.tensor_tensor(weight[1][:], weight[1][:], weight[0][:], ALU.mult))
            else:
                order(V.tensor_copy(oh16[:], onehot[0][:]))
                V.nop().then_inc(s_oh, 1)
                order(V.tensor_tensor(work[:], logits[:], by_expert(best[0][:]), ALU.subtract))
                V.nop().then_inc(s_diff, 1)
                dve.wait_ge(s_exp, 1)
                order(V.tensor_reduce(weight[0][:], work[:], AX_X, ALU.add))
                order(V.reciprocal(weight[0][:], weight[0][:]))

            dve.wait_ge(s_count, 1)
            order(V.tensor_copy(total[:].rearrange("p e t -> p t e"),
                                h_ps[0][:, 1, 0:T * E].rearrange("p (t e) -> p t e", e=E)))
            for e in range(E):
                order.tick(V.tensor_tensor_scan(running[:, e, :], one_t[:], total[:, e, :], 0.0, ALU.mult, ALU.add))
            order.wait()
            if capacity is None:
                order(V.tensor_scalar(tiles_of[:], running[:, :, T - 1], 1 / P, (P - 1) / P - 0.49609375, ALU.mult, ALU.add))
                order(V.tensor_scalar(tiles_of[:], tiles_of[:], ROUND, -ROUND, ALU.add, ALU.add))
                order(V.tensor_scalar(tiles_of[:], tiles_of[:], 1.0, None, ALU.max))
                order(V.tensor_tensor_scan(ends_of[:], one_t[:, 0:E], tiles_of[:], 0.0, ALU.mult, ALU.add))
                order(V.tensor_tensor(start_of[:], ends_of[:], tiles_of[:], ALU.subtract))
            else:
                order(V.tensor_scalar(start_of[:], expert_no[:], float(capacity // P), None, ALU.mult))
            order(V.tensor_tensor(running[:], running[:], total[:], ALU.subtract))
            order(V.tensor_tensor(work[:], running[:].rearrange("p e t -> p t e"),
                                  h_ps[0][:, 0, 0:T * E].rearrange("p (t e) -> p t e", e=E), ALU.add))
            if capacity is not None:
                order(V.tensor_scalar(logits[:], work[:], float(capacity), float(4 * tokens), ALU.is_ge, ALU.mult))
                order(V.tensor_tensor(work[:], work[:], logits[:], ALU.add))
            order(V.tensor_scalar(ends_of[:], start_of[:], float(P), None, ALU.mult))
            order(V.tensor_tensor(work[:], work[:], of_expert(ends_of[:]), ALU.add))
            for c in range(choices):
                order(V.tensor_tensor(logits[:], work[:], onehot[c][:], ALU.mult))
                order(V.tensor_reduce(first[:], logits[:], AX_X, ALU.add))
                order(V.tensor_scalar(slot_div[c][:], first[:], 1 / P, -0.49609375, ALU.mult, ALU.add))
                order(V.tensor_scalar(slot_div[c][:], slot_div[c][:], ROUND, -ROUND, ALU.add, ALU.add))
                order(V.scalar_tensor_tensor(slot_mod[c][:], slot_div[c][:], -float(P), first[:], ALU.mult, ALU.add))
            order(V.tensor_scalar(expert_f[:], lane_no[:, 0:NS], start_of[:, 1:2], None, ALU.is_ge))
            for e in range(2, E):
                order(V.scalar_tensor_tensor(expert_f[:], lane_no[:, 0:NS], start_of[:, e:e + 1], expert_f[:],
                                             ALU.is_ge, ALU.add))
            order(V.tensor_copy(expert_of_tile[:], expert_f[:]))

            def picks(m, p, c, t):
                free(dve, s_picked[p], m)
                V.tensor_scalar(pick_lane[p][:], lane_no[:], slot_mod[c][:, bass.ds(t, 1)], None, ALU.is_equal)
                V.tensor_scalar(pick_tile[p][:, 0, :], lane_no[:, 0:NS], slot_div[c][:, bass.ds(t, 1)],
                                token_1[:, bass.ds(t, 1)], ALU.is_equal, ALU.mult)
                V.tensor_scalar(pick_tile[p][:, 1, :], lane_no[:, 0:NS], slot_div[c][:, bass.ds(t, 1)],
                                weight[c][:, bass.ds(t, 1)], ALU.is_equal, ALU.mult).then_inc(s_pick[p], 1)

            if choices == 2:
                picks(0, 0, 0, 0)
                picks(0, 1, 1, 0)
                with dve.Fori(1, T) as t:
                    for c in range(2):
                        picks(t, c, c, t)
            else:
                picks(0, 0, 0, 0)
                picks(0, 1, 0, 1)
                with dve.Fori(1, T // 2) as m:
                    for p in range(2):
                        picks(m, p, 0, 2 * m + p)
            for p in range(2):
                dve.wait_ge(s_picked[p], T * choices // 2)
            table = h_ps[1][:, 0, 0:2 * NS]
            order(V.tensor_scalar(pad_f[:], table[:, 0:NS], 0.0, pad_row[:], ALU.is_equal, ALU.mult))
            order(V.scalar_tensor_tensor(row_f[:], table[:, 0:NS], -1.0, pad_f[:], ALU.add, ALU.add))
            order(V.tensor_copy(row_of_slot[:], row_f[:]))
            order(V.tensor_copy(weight_of_slot[:], table[:, NS:2 * NS]))
            V.nop().then_inc(s_table, 1)

            def x_low(m, p):
                dve.wait_ge(s_xh[p], m + 1)
                V.tensor_tensor(xT_lo[p][:].rearrange("p c t -> p (c t)"), xT_ps[p][:, 0:D],
                                xT_hi[p][:].rearrange("p c t -> p (c t)"), ALU.subtract).then_inc(s_xl[p], 1)

            def hidden_split(m, p):
                for b in range(2):
                    dve.wait_ge(s_h32[p], 2 * m + b + 1)
                    if b == 0 and not (isinstance(m, int) and m == 0):
                        dve.wait_ge(s_l2[p], m)
                    part = h32[p][:, b * 512:(b + 1) * 512]
                    hi = h_hi[p][:, 4 * b:4 * b + 4, :].rearrange("p c t -> p (c t)")
                    lo = h_lo[p][:, 4 * b:4 * b + 4, :].rearrange("p c t -> p (c t)")
                    V.tensor_copy(hi, part).then_inc(s_hh[p], 1)
                    dve.wait_ge(s_hh[p], 2 * m + b + 1)
                    V.tensor_tensor(lo, part, hi, ALU.subtract).then_inc(s_hl[p], 1)

            def result(m, p, i):
                e = dve.value_load(expert_of_tile[0:1, bass.ds(i, 1)], min_val=0, max_val=E - 1)
                dve.wait_ge(s_l2[p], m + 1)
                free(dve, s_added[p], 16 * m)
                V.scalar_tensor_tensor(y[p], y_ps[p][:, 0:D], 1 / WEIGHT_SCALE,
                                       b2_all[:, bass.ds(e, 1), :].rearrange("p a d -> p (a d)"), ALU.mult, ALU.add).then_inc(s_yb[p], 1)
                dve.wait_ge(s_yb[p], m + 1)
                V.tensor_scalar(y[p], y[p], weight_of_slot[:, bass.ds(i, 1)], None, ALU.mult).then_inc(s_y[p], 1)

            x_low(0, 0)
            x_low(0, 1)
            hidden_split(0, 0)
            for m in range(HEAD):
                split_lo(dve, 2 * m + 1)
                hidden_split(m, 1)
                x_low(m + 1, 0)
                result(m, 0, 2 * m)
                if 2 * m + 2 < E:
                    split_lo(dve, 2 * m + 2)
                hidden_split(m + 1, 0)
                x_low(m + 1, 1)
                result(m, 1, 2 * m + 1)
            with dve.Fori(HEAD, M - 1) as m:
                hidden_split(m, 1)
                x_low(m + 1, 0)
                result(m, 0, 2 * m)
                hidden_split(m + 1, 0)
                x_low(m + 1, 1)
                result(m, 1, 2 * m + 1)
            hidden_split(M - 1, 1)
            result(M - 1, 0, NS - 2)
            result(M - 1, 1, NS - 1)


def this(engine, semaphores, m, p):
    engine.wait_ge(semaphores[p], m + 1)


def last(engine, semaphores, m, p):
    free(engine, semaphores[1 - p], m + p)


def attention(nc, name, x_all, x_sum, context, mask, wq, bq, wk, bk, wv, bv, wo, bo):
    B = x_all.shape[1]
    D = x_all.shape[2]
    DC = D // P
    H = 16
    DK = D // H
    HC = H // 2
    V1 = DK + 1
    QS = WEIGHT_SCALE * float(DK) ** 0.5
    assert D == 2 * P and DK == 16

    with ExitStack() as ctx:
        sem = ctx.enter_context(stage_semaphores(nc, name))

        def sb(n, shape, dt):
            return ctx.enter_context(nc.sbuf_tensor(f"{name}_{n}", shape, dt))

        def pb(n, shape, dt):
            return ctx.enter_context(nc.psum_tensor(f"{name}_{n}", shape, dt))

        def two(n):
            return [sem(f"{n}_{p}") for p in range(2)]

        c_in = [sb(f"c_in{p}", [P, D], F32) for p in range(2)]
        w_rows = sb("w_rows", [P, 4, DC, D], F32)
        wT_hi = sb("wT_hi", [P, 4, DC, D], F16)
        wT_lo = sb("wT_lo", [P, 4, DC, D], F16)
        kvT_hi = sb("kvT_hi", [P, DC, 2 * D], F16)
        kvT_lo = sb("kvT_lo", [P, DC, 2 * D], F16)
        biases = sb("biases", [P, 4, D], F32)
        mask_sb = sb("mask_sb", [P, P], I32)
        masked = sb("masked", [P, P], I32)
        tiny = sb("tiny", [P, P], F32)
        ident = sb("ident", [P, P], F32)
        ident16 = sb("ident16", [P, P], F16)
        stats = sb("stats", [P, B, 6], F32)
        mean_var = sb("mean_var", [P, B, 2], F32)
        rstd = sb("rstd", [P, B], F32)
        var = sb("var", [P, B], F32)
        rtmp = sb("rtmp", [P, B], F32)
        xn = sb("xn", [P, D], F32)
        inT_hi = sb("inT_hi", [P, 4, P], F16)
        inT_lo = sb("inT_lo", [P, 4, P], F16)
        q32 = sb("q32", [P, D], F32)
        k32 = sb("k32", [P, D], F32)
        v32 = [sb(f"v32_{i}", [P, H, V1], F32) for i in range(4)]
        q_parts = sb("q_parts", [P, H, 4, DK], F16)
        k_parts = sb("k_parts", [P, H, 4, DK], F16)
        qT = [sb(f"qT{p}", [P, HC, P], F16) for p in range(2)]
        kT = [sb(f"kT{p}", [P, HC, P], F16) for p in range(2)]
        top = sb("top", [P, H], F32)
        prob = sb("prob", [P, H, P], F32)
        probT = sb("probT", [P, H, P], F32)
        rsum = sb("rsum", [P, H], F32)
        o32 = sb("o32", [P, D], F32)
        oT_hi = sb("oT_hi", [P, DC, P], F16)
        oT_lo = sb("oT_lo", [P, DC, P], F16)

        S = pb("S", [P, 2, HC, P], F32)
        front = [pb(f"front{i}", [P, 512], F32) for i in range(2)]
        out_ps = pb("out_ps", [P, 512], F32)
        oT_ps = pb("oT_ps", [P, 512], F32)

        s_x = sem("x_loaded"); s_c = two("context_loaded"); s_w = sem("weights_loaded")
        s_pool = sem("pool_order"); s_dve = sem("dve_order"); s_const = sem("constants")
        s_var = sem("variance"); s_root = sem("root"); s_prep = sem("dve_prepared")
        s_wt = two("weights_transposed"); s_wh = two("weights_hi"); s_wl = two("weights_lo")
        s_xn = two("xn_ready"); s_xb = two("x_biased")
        s_tp = two("inputs_transposed"); s_th = two("inT_hi_ready"); s_tl = two("inT_lo_ready")
        s_kv = two("kv_product"); s_q = two("q_product")
        s_k32 = two("k32_ready"); s_v32 = two("v32_ready"); s_q32 = two("q32_ready")
        s_qh = two("q_high"); s_kh = two("k_high"); s_ql = two("q_low"); s_kl = two("k_low")
        s_qt = two("q_transposed"); s_kt = two("k_transposed"); s_qT = two("qT_ready"); s_kT = two("kT_ready")
        s_s = [two(f"scores{r}") for r in range(2)]
        s_top = [two(f"top{r}") for r in range(2)]; s_mask = [two(f"masked{r}") for r in range(2)]
        s_sub = [two(f"shifted{r}") for r in range(2)]; s_exp = [two(f"exp{r}") for r in range(2)]
        s_pt = [two(f"prob_transposed{r}") for r in range(2)]; s_pT = [two(f"probT{r}_ready") for r in range(2)]
        s_pv = two("pv_product"); s_rs = two("rsum_ready"); s_o = two("o32_ready")
        s_ot = two("o_transposed"); s_oh = two("oT_hi_ready"); s_ol = two("oT_lo_ready")
        s_out = two("out_product"); s_done = two("batch_done")

        s_go = sem("dve_goes_on")

        M = B // 2

        def slots(engine, slot):
            def run(group, i):
                def on(step, distance, *args):
                    j = i + distance
                    if isinstance(group, int) and not 0 <= 4 * group + j < B:
                        return
                    step(2 * group + j // 2, j % 2, j % 4, *args)
                slot(on)

            first, last_ = 1, B // 4 - 1
            for i in range(4):
                run(-1, i)
            for i in range(4):
                run(0, i)
            with engine.Fori(first, last_) as group:
                for i in range(4):
                    run(group, i)
            for i in range(8):
                run(last_, i)

        block = ctx.enter_context(nc.Block())

        @block.sync
        def _(sp):
            sp.dma_start(x_all[:], x_sum.rearrange("(t p) d -> p t d", p=P)).then_inc(s_x, 16)
            for i, w in enumerate((wq, wk, wv, wo)):
                sp.dma_start(w_rows[:, i], w.rearrange("(c p) d -> p c d", p=P)).then_inc(s_w, 16)
            for i, b in enumerate((bq, bk, bv, bo)):
                sp.dma_start(biases[:, i, :], broadcast_rows(b, P, D)).then_inc(s_w, 16)
            sp.dma_start(mask_sb[:], mask.rearrange("a b q k -> (a b q) k")).then_inc(s_w, 16)

            def load(m):
                for p in range(2):
                    free(sp, s_tp[p], m)
                    sp.dma_start(c_in[p][:], context[bass.ds((2 * m + p) * P, P), :]).then_inc(s_c[p], 16)

            each(sp, M, load)

        @block.gpsimd
        def _(pool):
            order = Order(pool, s_pool)
            order(nc.gpsimd.memset(ident[:], 0.0))
            order(nc.gpsimd.memset(ident16[:], 0.0))
            for i in (ident, ident16):
                nc.gpsimd.affine_select(out=i[:], in_=i[:], compare_op=ALU.not_equal, fill=1.0, base=0,
                                        pattern=[[-1, P]], channel_multiplier=1).then_inc(s_const, 1)
            nc.gpsimd.memset(tiny[:], 1e-09).then_inc(s_const, 1)
            for i in range(4):
                nc.gpsimd.memset(v32[i][:, :, DK:V1], 1.0).then_inc(s_const, 1)
            pool.wait_ge(s_w, 16 * 9)

            def batch(m, p):
                b = 2 * m + p
                this(pool, s_xn, m, p)
                row = x_all[:, bass.ds(b, 1), :].rearrange("p a d -> p (a d)")
                nc.gpsimd.tensor_tensor(row, row, biases[:, 3, :], ALU.add).then_inc(s_xb[p], 1)
                this(pool, s_qh, m, p)
                q2 = q32[:].rearrange("p (h d) -> p h d", h=H).unsqueeze(2).to_broadcast([P, H, 2, DK])
                nc.gpsimd.tensor_tensor(q_parts[:, :, 2:4, :], q2, q_parts[:, :, 0:2, :], ALU.subtract).then_inc(s_ql[p], 1)
                this(pool, s_kh, m, p)
                k2 = k32[:].rearrange("p (h d) -> p h d", h=H).unsqueeze(2).to_broadcast([P, H, 2, DK])
                nc.gpsimd.tensor_tensor(k_parts[:, :, 1:4:2, :], k2, k_parts[:, :, 0:4:2, :], ALU.subtract).then_inc(s_kl[p], 1)

            def pair(m):
                for p in range(2):
                    batch(m, p)

            each(pool, M, pair)

        @block.tensor
        def _(pe):
            pe.wait_ge(s_const, 7)
            pe.wait_ge(s_w, 16 * 9)
            for i in range(4):
                p = i % 2
                if i >= 2:
                    pe.wait_ge(s_wl[p], i // 2)
                for r in range(DC):
                    for c in range(DC):
                        mm = nc.tensor.transpose(front[p][:, (c * DC + r) * P:(c * DC + r + 1) * P],
                                                 w_rows[:, i, r, c * P:(c + 1) * P], ident[:])
                mm.then_inc(s_wt[p], 1)
            pe.wait_ge(s_prep, 1)

            def front_in(m, p, i):
                this(pe, s_xn, m, p)
                pe.wait_ge(s_c[p], 16 * (m + 1))
                last(pe, s_qT, m, p)
                for c in range(DC):
                    nc.tensor.transpose(front[0][:, c * P:(c + 1) * P], xn[:, c * P:(c + 1) * P], ident[:])
                for c in range(DC):
                    mm = nc.tensor.transpose(front[0][:, (2 + c) * P:(3 + c) * P], c_in[p][:, c * P:(c + 1) * P], ident[:])
                mm.then_inc(s_tp[p], 1)

            def front_products(m, p, i):
                this(pe, s_tl, m, p)
                last(pe, s_kT, m, p)
                for c in range(DC):
                    a_hi, a_lo = inT_hi[:, 2 + c, :], inT_lo[:, 2 + c, :]
                    nc.tensor.matmul(front[1][:], a_hi, kvT_hi[:, c, :], start=(c == 0), stop=False)
                    nc.tensor.matmul(front[1][:], a_hi, kvT_lo[:, c, :], start=False, stop=False)
                    mm = nc.tensor.matmul(front[1][:], a_lo, kvT_hi[:, c, :], start=False, stop=(c == DC - 1))
                mm.then_inc(s_kv[p], 1)
                for c in range(DC):
                    a_hi, a_lo = inT_hi[:, c, :], inT_lo[:, c, :]
                    out = front[0][:, 0:D]
                    nc.tensor.matmul(out, a_hi, wT_hi[:, 0, c, :], start=(c == 0), stop=False)
                    nc.tensor.matmul(out, a_hi, wT_lo[:, 0, c, :], start=False, stop=False)
                    mm = nc.tensor.matmul(out, a_lo, wT_hi[:, 0, c, :], start=False, stop=(c == DC - 1))
                mm.then_inc(s_q[p], 1)

            def front_transposes(m, p, i):
                this(pe, s_ql, m, p)
                for c in range(HC):
                    mm = nc.tensor.transpose(front[0][:].bitcast(F16)[:, c * P:(c + 1) * P],
                                             q_parts[:, 2 * c:2 * c + 2].rearrange("p h k d -> p (h k d)"), ident16[:])
                mm.then_inc(s_qt[p], 1)
                this(pe, s_kl, m, p)
                this(pe, s_v32, m, p)
                for c in range(HC):
                    mm = nc.tensor.transpose(front[1][:].bitcast(F16)[:, c * P:(c + 1) * P],
                                             k_parts[:, 2 * c:2 * c + 2].rearrange("p h k d -> p (h k d)"), ident16[:])
                mm.then_inc(s_kt[p], 1)

            def scores(m, p, i, r):
                if r == 0:
                    this(pe, s_qT, m, p)
                    this(pe, s_kT, m, p)
                last(pe, s_pT[r], m, p)
                rows = slice(64 * r, 64 * r + 64)
                for c in range(HC):
                    mm = nc.tensor.matmul(S[:, r, c, :], qT[p][rows, c, :], kT[p][rows, c, :], start=True, stop=True)
                mm.then_inc(s_s[r][p], 1)

            def prob_transposes(m, p, i, r):
                this(pe, s_exp[r], m, p)
                for c in range(HC):
                    mm = nc.tensor.transpose(S[:, r, c, :], prob[:, r * HC + c, :], ident[:])
                mm.then_inc(s_pt[r][p], 1)

            def value_products(m, p, i, r):
                if r == 0:
                    last(pe, s_o, m, p)
                this(pe, s_pT[r], m, p)
                for c in range(HC):
                    h = r * HC + c
                    mm = nc.tensor.matmul(out_ps[:, h * V1:(h + 1) * V1], probT[:, h, :], v32[i][:, 2 * c + r, :],
                                          start=True, stop=True)
                if r == 1:
                    mm.then_inc(s_pv[p], 1)

            def out_transposes(m, p, i):
                this(pe, s_o, m, p)
                last(pe, s_done, m, p)
                for c in range(DC):
                    mm = nc.tensor.transpose(oT_ps[:, c * P:(c + 1) * P], o32[:, c * P:(c + 1) * P], ident[:])
                mm.then_inc(s_ot[p], 1)

            def out_product(m, p, i):
                this(pe, s_ol, m, p)
                for c in range(DC):
                    out = oT_ps[:, D:2 * D]
                    nc.tensor.matmul(out, oT_hi[:, c, :], wT_hi[:, 3, c, :], start=(c == 0), stop=False)
                    nc.tensor.matmul(out, oT_hi[:, c, :], wT_lo[:, 3, c, :], start=False, stop=False)
                    mm = nc.tensor.matmul(out, oT_lo[:, c, :], wT_hi[:, 3, c, :], start=False, stop=(c == DC - 1))
                mm.then_inc(s_out[p], 1)

            def slot(on):
                on(front_products, 1)
                on(scores, 0, 0)
                on(front_transposes, 1)
                on(prob_transposes, -1, 1)
                on(out_transposes, -2)
                on(front_in, 2)
                on(value_products, -1, 0)
                on(scores, 0, 1)
                on(out_product, -2)
                on(prob_transposes, 0, 0)
                on(value_products, -1, 1)

            slots(pe, slot)

        @block.scalar
        def _(act):
            A = nc.scalar
            act.wait_ge(s_var, 1)
            A.activation(rstd[:], var[:], ACT.Sqrt).then_inc(s_root, 1)
            for i in range(4):
                p = i % 2
                act.wait_ge(s_wt[p], i // 2 + 1)
                A.activation(wT_hi[:, i].rearrange("p c d -> p (c d)"), front[p][:], ACT.Copy, scale=WEIGHT_SCALE).then_inc(s_wh[p], 1)

            def front_in(m, p, i):
                this(act, s_tp, m, p)
                A.activation(inT_hi[:].rearrange("p c t -> p (c t)"), front[0][:], ACT.Copy).then_inc(s_th[p], 1)

            def front_high(m, p, i):
                this(act, s_k32, m, p)
                k2 = k32[:].rearrange("p (h d) -> p h d", h=H).unsqueeze(2).to_broadcast([P, H, 2, DK])
                A.activation(k_parts[:, :, 0:4:2, :], k2, ACT.Copy).then_inc(s_kh[p], 1)
                this(act, s_q32, m, p)
                q2 = q32[:].rearrange("p (h d) -> p h d", h=H).unsqueeze(2).to_broadcast([P, H, 2, DK])
                A.activation(q_parts[:, :, 0:2, :], q2, ACT.Copy).then_inc(s_qh[p], 1)

            def query_copy(m, p, i):
                this(act, s_qt, m, p)
                A.activation(qT[p][:].rearrange("p c t -> p (c t)"), front[0][:].bitcast(F16), ACT.Copy).then_inc(s_qT[p], 1)

            def key_copy(m, p, i):
                this(act, s_kt, m, p)
                A.activation(kT[p][:].rearrange("p c t -> p (c t)"), front[1][:].bitcast(F16), ACT.Copy).then_inc(s_kT[p], 1)

            def exps(m, p, i, r):
                this(act, s_sub[r], m, p)
                part = prob[:, r * HC:(r + 1) * HC, :]
                A.activation(part, part, ACT.Exp).then_inc(s_exp[r][p], 1)

            def prob_copy(m, p, i, r):
                this(act, s_pt[r], m, p)
                A.activation(probT[:, r * HC:(r + 1) * HC, :], S[:, r], ACT.Copy).then_inc(s_pT[r][p], 1)

            def out_high(m, p, i):
                this(act, s_ot, m, p)
                A.activation(oT_hi[:].rearrange("p c t -> p (c t)"), oT_ps[:, 0:D], ACT.Copy).then_inc(s_oh[p], 1)

            def slot(on):
                on(exps, -1, 1)
                on(query_copy, 1)
                on(key_copy, 1)
                on(out_high, -2)
                on(prob_copy, -1, 1)
                on(front_in, 2)
                on(exps, 0, 0)
                on(prob_copy, 0, 0)
                on(front_high, 2)

            slots(act, slot)

        @block.vector
        def _(dve):
            V = nc.vector
            order = Order(dve, s_dve)
            dve.wait_ge(s_x, 16)
            layernorm_scales(dve, order, x_all, stats, mean_var, var, rstd, rtmp, s_var, s_root)
            dve.wait_ge(s_w, 16 * 9)
            for i in range(4):
                p = i % 2
                dve.wait_ge(s_wh[p], i // 2 + 1)
                V.scalar_tensor_tensor(wT_lo[:, i].rearrange("p c d -> p (c d)"), front[p][:], WEIGHT_SCALE,
                                       wT_hi[:, i].rearrange("p c d -> p (c d)"), ALU.mult, ALU.subtract).then_inc(s_wl[p], 1)
            for p in range(2):
                dve.wait_ge(s_wl[p], 2)
            for src, dst in ((wT_hi, kvT_hi), (wT_lo, kvT_lo)):
                for i in range(2):
                    order.tick(V.tensor_copy(dst[:, :, i * D:(i + 1) * D], src[:, 1 + i]))
            order.tick(V.tensor_scalar(biases[:, 0, :], biases[:, 0, :], 1 / float(DK) ** 0.5, None, ALU.mult))
            order(V.tensor_scalar(masked[:], mask_sb[:], 0, None, ALU.is_equal))
            V.nop().then_inc(s_prep, 1)
            dve.wait_ge(s_const, 7)

            def normalise(m, p, i):
                b = 2 * m + p
                last(dve, s_tp, m, p)
                V.tensor_scalar(xn[:], x_all[:, bass.ds(b, 1), :].rearrange("p a d -> p (a d)"),
                                mean_var[:, bass.ds(b, 1), 0], rstd[:, bass.ds(b, 1)], ALU.subtract, ALU.mult).then_inc(s_xn[p], 1)

            def front_low(m, p, i):
                this(dve, s_th, m, p)
                V.tensor_tensor(inT_lo[:].rearrange("p c t -> p (c t)"), front[0][:],
                                inT_hi[:].rearrange("p c t -> p (c t)"), ALU.subtract).then_inc(s_tl[p], 1)

            def front_bias(m, p, i):
                this(dve, s_kv, m, p)
                last(dve, s_kl, m, p)
                last(dve, s_ql, m, p)
                V.scalar_tensor_tensor(k32[:], front[1][:, 0:D], 1 / WEIGHT_SCALE, biases[:, 1, :], ALU.mult, ALU.add).then_inc(s_k32[p], 1)
                this(dve, s_q, m, p)
                V.scalar_tensor_tensor(q32[:], front[0][:, 0:D], 1 / QS, biases[:, 0, :], ALU.mult, ALU.add).then_inc(s_q32[p], 1)
                V.scalar_tensor_tensor(v32[i][:, :, 0:DK], front[1][:, D:2 * D].rearrange("p (h d) -> p h d", h=H), 1 / WEIGHT_SCALE,
                                       biases[:, 2, :].rearrange("p (h d) -> p h d", h=H), ALU.mult, ALU.add).then_inc(s_v32[p], 1)

            def softmax_shift(m, p, i, r):
                this(dve, s_s[r], m, p)
                wide = [P, HC, P]
                dve.sem_inc(s_go)
                V.copy_predicated(S[:, r], masked[:].unsqueeze(1).to_broadcast(wide),
                                  tiny[:].unsqueeze(1).to_broadcast(wide)).then_inc(s_mask[r][p], 1)
                this(dve, s_mask[r], m, p)
                tops = top[:, r * HC:(r + 1) * HC]
                V.tensor_reduce(tops, S[:, r], AX_X, ALU.max).then_inc(s_top[r][p], 1)
                this(dve, s_top[r], m, p)
                last(dve, s_pt[r], m, p)
                V.tensor_tensor(prob[:, r * HC:(r + 1) * HC, :], S[:, r], tops.unsqueeze(2).to_broadcast(wide),
                                ALU.subtract).then_inc(s_sub[r][p], 1)

            def divide(m, p, i):
                this(dve, s_pv, m, p)
                o = out_ps[:, 0:H * V1].rearrange("p (r c v) -> p r c v", r=2, v=V1)
                V.reciprocal(rsum[:].rearrange("p (r c) -> p r c", r=2), o[:, :, :, DK]).then_inc(s_rs[p], 1)
                this(dve, s_rs, m, p)
                last(dve, s_ot, m, p)
                V.tensor_tensor(o32[:].rearrange("p (c r d) -> p r c d", r=2, d=DK), o[:, :, :, 0:DK],
                                rsum[:].rearrange("p (r c) -> p r c", r=2).unsqueeze(3).to_broadcast([P, 2, HC, DK]),
                                ALU.mult).then_inc(s_o[p], 1)

            def out_low(m, p, i):
                this(dve, s_oh, m, p)
                V.tensor_tensor(oT_lo[:].rearrange("p c t -> p (c t)"), oT_ps[:, 0:D],
                                oT_hi[:].rearrange("p c t -> p (c t)"), ALU.subtract).then_inc(s_ol[p], 1)

            def finish(m, p, i):
                b = 2 * m + p
                this(dve, s_out, m, p)
                this(dve, s_xb, m, p)
                row = x_all[:, bass.ds(b, 1), :].rearrange("p a d -> p (a d)")
                V.scalar_tensor_tensor(row, oT_ps[:, D:2 * D], 1 / WEIGHT_SCALE, row, ALU.mult, ALU.add).then_inc(s_done[p], 1)

            def slot(on):
                on(softmax_shift, 0, 0)
                on(out_low, -2)
                on(front_low, 2)
                on(normalise, 3)
                on(softmax_shift, 0, 1)
                on(finish, -2)
                on(divide, -1)
                on(front_bias, 2)

            slots(dve, slot)
            for p in range(2):
                dve.wait_ge(s_done[p], M)


def gated_ffn(nc, name, x_all, w_gate, w_up, w_down, up_raw, out):
    T, D = x_all.shape[1], x_all.shape[2]
    tokens = T * P
    I = w_gate.shape[0]
    DC, IC = D // P, I // P
    BLOCK = 32
    WQMAX = 7.0
    QMAX = 2.0**15 - 1
    N = 512
    TG = tokens // N
    COLS = IC * tokens
    CB = 1024
    STEPS = COLS // CB
    NP = 2 * IC
    BANKS = 4

    with ExitStack() as ctx:
        sem = ctx.enter_context(stage_semaphores(nc, name))

        def sb(n, shape, dt):
            return ctx.enter_context(nc.sbuf_tensor(f"{name}_{n}", shape, dt))

        def pb(n, shape, dt):
            return ctx.enter_context(nc.psum_tensor(f"{name}_{n}", shape, dt))

        def two(n):
            return [sem(f"{n}_{p}") for p in range(2)]

        act_all = sb("act_all", [P, IC, tokens], F32)
        flat = act_all[:].rearrange("p c t -> p (c t)")
        y_all = flat[:, 0:T * D].rearrange("p (t d) -> p t d", d=D)
        W = IC * D
        rows = [flat[:, T * D + i * W:T * D + (i + 1) * W] for i in range(3)]
        scaled = [flat[:, T * D + (3 + i) * W:T * D + (4 + i) * W] for i in range(3)]
        yT_hi = sb("yT_hi", [P, DC, tokens], F16)
        yT_lo = sb("yT_lo", [P, DC, tokens], F16)
        guT_hi = sb("guT_hi", [P, 2, DC, I], F16)
        guT_lo = sb("guT_lo", [P, 2, DC, I], F16)
        dT_hi = sb("dT_hi", [P, IC, D], F16)
        dT_lo = sb("dT_lo", [P, IC, D], F16)
        ident = sb("ident", [P, P], F32)
        round_c = sb("round_c", [P, 1], F32)
        round_u = sb("round_u", [P, 1], F32)
        stats = sb("stats", [P, T, 6], F32)
        mean_var = sb("mean_var", [P, T, 2], F32)
        rstd = sb("rstd", [P, T], F32)
        var = sb("var", [P, T], F32)
        rtmp = sb("rtmp", [P, T], F32)
        NB = W // BLOCK
        b_scale = sb("b_scale", [P, 3, NB], F32)
        b_inv = sb("b_inv", [P, 3, NB], F32)
        maxes = sb("maxes", [P, NP, TG], F32)
        step_max = sb("step_max", [P, max(STEPS, T)], F32)
        largest = sb("largest", [P, 4, 2], F32)
        reduced = sb("reduced", [P, 4, 2], F32)
        scale = sb("scale", [P, 5], F32)
        to_int = sb("to_int", [P, 5], F32)
        tmp = sb("tmp", [P, 5], F32)
        unit = sb("unit", [P, 3], F32)
        u_out = [sb(f"u_out{p}", [P, N], F32) for p in range(2)]
        work = [[sb(f"work{i}{p}", [P, CB], F32) for p in range(2)] for i in range(2)]
        later = yT_hi[:].rearrange("p c t -> p (c t)").bitcast(F32)
        o_parts = yT_lo[:].rearrange("p c t -> p (c t)")

        ps = [pb(f"ps{i}", [P, N], F32) for i in range(8)]

        s_w = [sem(f"rows{i}_loaded") for i in range(3)]
        s_const = sem("constants"); s_pool = sem("pool_order"); s_dve = sem("dve_order")
        s_var = sem("variance"); s_root = sem("root")
        s_deq = sem("weights_dequantised"); s_wt = two("weights_transposed"); s_wh = two("weights_hi"); s_wl = two("weights_lo")
        s_big = sem("largest_ready"); s_red = sem("largest_reduced"); s_scale = sem("scales_ready")
        s_t = two("x_rounded"); s_q = two("x_quantised"); s_qt = two("x_transposed"); s_qh = two("yT_hi_ready"); s_ql = two("yT_lo_ready")
        s_pr = [sem(f"product_in_bank{i}") for i in range(BANKS)]; s_ev = [sem(f"bank{i}_copied") for i in range(BANKS)]
        s_mx = [sem(f"bank{i}_max_taken") for i in range(BANKS)]
        s_us = two("up_stored")
        s_2 = {k: two("sig_" + k) for k in ("t", "int", "sigmoid", "shift", "sig", "product", "max")}
        s_3 = {k: two("up_" + k) for k in ("loaded", "t", "int", "tu", "product", "max")}
        s_4 = {k: two("down_" + k) for k in ("t", "int", "hi", "lo", "product", "out", "stored")}

        def weight_groups(i):
            if i < 2:
                return [[c * D + d * P for c in range(c0, c0 + 2) for d in range(DC)] for c0 in range(0, IC, 2)]
            return [[r * I + c * P for c in range(c0, c0 + 2) for r in range(DC)] for c0 in range(0, IC, 2)]

        def weight_parts(i, j, w, d):
            if i < 2:
                return w[:, i, :, 2 * j * P:2 * (j + 1) * P].rearrange("p r (c q) -> p c r q", q=P)
            return d[:, 2 * j:2 * j + 2, :].rearrange("p c (r q) -> p c r q", q=P)

        def down_parts(p):
            n = IC * P
            return [o_parts[:, (2 * h + p) * n:(2 * h + p + 1) * n].rearrange("p (c t) -> p c t", c=IC) for h in range(2)]

        s_go = sem("act_goes_on")

        block = ctx.enter_context(nc.Block())

        @block.sync
        def _(sp):
            for i, w in enumerate((w_gate, w_up)):
                sp.dma_start(rows[i].rearrange("p (c d) -> p c d", d=D), w.rearrange("(c p) d -> p c d", p=P)).then_inc(s_w[i], 16)
            sp.dma_start(rows[2].rearrange("p (c i) -> p c i", i=I), w_down.rearrange("(c p) i -> p c i", p=P)).then_inc(s_w[2], 16)


            def up_out(g):
                for c in range(IC):
                    k = IC + c
                    sp.wait_ge(s_ev[k % BANKS], (NP // BANKS) * g + k // BANKS + 1)
                    sp.dma_start(up_raw[:, c, bass.ds(g * N, N)], u_out[c % 2][:]).then_inc(s_us[c % 2], 16)

            each(sp, TG, up_out)
            for p in range(2):
                sp.wait_ge(s_us[p], 16 * TG * IC // 2)
            up_flat = up_raw.rearrange("p c t -> p (c t)")

            def up_in(m):
                for p in range(2):
                    free(sp, s_3["tu"][p], m)
                    sp.dma_start(later[:, (2 + p) * CB:(3 + p) * CB], up_flat[:, bass.ds((2 * m + p) * CB, CB)]).then_inc(s_3["loaded"][p], 16)

            each(sp, STEPS // 2, up_in)

            def result_out(m):
                for p in range(2):
                    sp.wait_ge(s_4["out"][p], m + 1)
                    sp.dma_start(out[bass.ds((2 * m + p) * P, P), :], u_out[p][:, 0:D]).then_inc(s_4["stored"][p], 16)

            each(sp, T // 2, result_out)
            for p in range(2):
                sp.wait_ge(s_4["stored"][p], 16 * T // 2)

        @block.gpsimd
        def _(pool):
            order = Order(pool, s_pool)
            order(nc.gpsimd.memset(ident[:], 0.0))
            nc.gpsimd.affine_select(out=ident[:], in_=ident[:], compare_op=ALU.not_equal, fill=1.0, base=0,
                                    pattern=[[-1, P]], channel_multiplier=1).then_inc(s_const, 1)
            nc.gpsimd.memset(round_c[:], ROUND).then_inc(s_const, 1)
            nc.gpsimd.memset(round_u[:], 2.0**23).then_inc(s_const, 1)

            def all_max(n):
                pool.wait_ge(s_big, n + 1)
                nc.gpsimd.partition_all_reduce(reduced[:, n, :], largest[:, n, :], P, bass.bass_isa.ReduceOp.max).then_inc(s_red, 1)

            all_max(0)
            all_max(1)

            def multiply_sigmoid(m):
                for p in range(2):
                    this(pool, s_2["sig"], m, p)
                    part = flat[:, bass.ds((2 * m + p) * CB, CB)]
                    nc.gpsimd.tensor_tensor(part, part, work[1][p][:], ALU.mult).then_inc(s_2["product"][p], 1)

            each(pool, STEPS // 2, multiply_sigmoid)
            all_max(2)
            all_max(3)

        @block.tensor
        def _(pe):
            pe.wait_ge(s_const, 3)

            def weights(i, n, parts):
                p = n % 2
                if n >= 2:
                    pe.wait_ge(s_wl[p], n // 2)
                for j, part in enumerate(parts):
                    mm = nc.tensor.transpose(ps[p][:, j * P:(j + 1) * P], part, ident[:])
                mm.then_inc(s_wt[p], 1)

            n = 0
            for i in range(3):
                pe.wait_ge(s_deq, i + 1)
                for group in weight_groups(i):
                    weights(i, n, [scaled[i][:, a:a + P] for a in group])
                    n += 1

            def tokens_in(m, p):
                this(pe, s_q, m, p)
                free(pe, s_ql[p], m)
                for t in range(2):
                    for c in range(DC):
                        mm = nc.tensor.transpose(ps[2 + p][:, (2 * c + t) * P:(2 * c + t + 1) * P],
                                                 work[0][p][:, t * D + c * P:t * D + (c + 1) * P], ident[:])
                mm.then_inc(s_qt[p], 1)

            def tokens_group(m):
                for p in range(2):
                    tokens_in(m, p)

            each(pe, T // 4, tokens_group)
            for p in range(2):
                pe.wait_ge(s_ql[p], T // 4)
                pe.wait_ge(s_wl[p], (n + 1 - p) // 2)

            def products(g):
                y_at = [[y[:, c, bass.ds(g * N, N)] for c in range(DC)] for y in (yT_hi, yT_lo)]
                for k in range(NP):
                    b = k % BANKS
                    free(pe, s_ev[b], (NP // BANKS) * g + k // BANKS)
                    i, c0 = divmod(k, IC)
                    for c in range(DC):
                        hi, lo = (w[:, i, c, c0 * P:(c0 + 1) * P] for w in (guT_hi, guT_lo))
                        nc.tensor.matmul(ps[4 + b][:], hi, y_at[0][c], start=(c == 0), stop=False)
                        nc.tensor.matmul(ps[4 + b][:], hi, y_at[1][c], start=False, stop=False)
                        mm = nc.tensor.matmul(ps[4 + b][:], lo, y_at[0][c], start=False, stop=(c == DC - 1))
                    mm.then_inc(s_pr[b], 1)

            each(pe, TG, products)

            def down_products(m):
                for p in range(2):
                    this(pe, s_4["lo"], m, p)
                    free(pe, s_4["out"][p], m)
                    hi, lo = down_parts(p)
                    for c in range(IC):
                        nc.tensor.matmul(ps[p][:, 0:D], hi[:, c, :], dT_hi[:, c, :], start=(c == 0), stop=False)
                        nc.tensor.matmul(ps[p][:, 0:D], hi[:, c, :], dT_lo[:, c, :], start=False, stop=False)
                        mm = nc.tensor.matmul(ps[p][:, 0:D], lo[:, c, :], dT_hi[:, c, :], start=False, stop=(c == IC - 1))
                    mm.then_inc(s_4["product"][p], 1)

            each(pe, T // 2, down_products)

        @block.scalar
        def _(act):
            A = nc.scalar
            act.wait_ge(s_var, 1)
            A.activation(rstd[:], var[:], ACT.Sqrt).then_inc(s_root, 1)
            n = 0
            for i in range(3):
                for j in range(IC // 2):
                    p = n % 2
                    act.wait_ge(s_wt[p], n // 2 + 1)
                    bank = ps[p][:].rearrange("p (c r q) -> p c r q", c=2, r=DC)
                    A.activation(weight_parts(i, j, guT_hi, dT_hi), bank, ACT.Copy, scale=WEIGHT_SCALE).then_inc(s_wh[p], 1)
                    n += 1
            act.wait_ge(s_const, 3)
            act.wait_ge(s_scale, 1)

            def round_input(m, p):
                free(act, s_qt[p], m)
                act.sem_inc(s_go)
                A.activation(work[0][p][:, 0:2 * D], flat[:, bass.ds((2 * m + p) * 2 * D, 2 * D)], ACT.Identity,
                             bias=round_c[:], scale=to_int[:, 0:1]).then_inc(s_t[p], 1)

            def input_high(m, p):
                this(act, s_qt, m, p)
                act.sem_inc(s_go)
                t0 = (2 * m + p) * 2 * P
                A.activation(yT_hi[:, :, bass.ds(t0, 2 * P)], ps[2 + p][:].rearrange("p (c t) -> p c t", c=DC),
                             ACT.Copy).then_inc(s_qh[p], 1)

            staggered(act, T // 2, (round_input, 1), (input_high, 0))

            def copy_products(g):
                for k in range(NP):
                    b = k % BANKS
                    act.wait_ge(s_pr[b], (NP // BANKS) * g + k // BANKS + 1)
                    if k < IC:
                        dst = act_all[:, k, bass.ds(g * N, N)]
                    else:
                        c = k - IC
                        free(act, s_us[c % 2], 16 * ((IC // 2) * g + c // 2))
                        if c >= 2:
                            act.wait_ge(s_mx[(k - 2) % BANKS], (NP // BANKS) * g + (k - 2) // BANKS + 1)
                        else:
                            k2 = NP - 2 + c
                            free(act, s_mx[k2 % BANKS], (NP // BANKS) * (g - 1) + k2 // BANKS + 1)
                        dst = u_out[c % 2][:]
                    A.activation(dst, ps[4 + b][:], ACT.Copy).then_inc(s_ev[b], 1)

            each(act, TG, copy_products)

            act.wait_ge(s_scale, 2)

            def round_gate(m, p):
                free(act, s_2["sig"][p], m)
                act.sem_inc(s_go)
                part = flat[:, bass.ds((2 * m + p) * CB, CB)]
                A.activation(work[0][p][:], part, ACT.Identity, bias=round_c[:], scale=to_int[:, 1:2]).then_inc(s_2["t"][p], 1)

            def sigmoid(m, p):
                this(act, s_2["int"], m, p)
                free(act, s_2["product"][p], m)
                act.sem_inc(s_go)
                part = flat[:, bass.ds((2 * m + p) * CB, CB)]
                A.activation(work[1][p][:], part, ACT.Sigmoid, scale=scale[:, 1:2]).then_inc(s_2["sigmoid"][p], 1)
                this(act, s_2["sigmoid"], m, p)
                A.activation(work[0][p][:], work[1][p][:], ACT.Identity, bias=round_u[:], scale=2.0**16).then_inc(s_2["shift"][p], 1)

            staggered(act, STEPS, (round_gate, 1), (sigmoid, 0))

            act.wait_ge(s_scale, 3)

            def scale_up_steps(m):
                for p in range(2):
                    part = flat[:, bass.ds((2 * m + p) * CB, CB)]
                    free(act, s_3["int"][p], m)
                    act.sem_inc(s_go)
                    A.activation(work[0][p][:], part, ACT.Identity, bias=round_c[:], scale=to_int[:, 3:4]).then_inc(s_3["t"][p], 1)
                    free(act, s_3["product"][p], m)
                    act.wait_ge(s_3["loaded"][p], 16 * (m + 1))
                    A.activation(work[1][p][:], later[:, (2 + p) * CB:(3 + p) * CB], ACT.Identity, bias=round_c[:],
                                 scale=to_int[:, 2:3]).then_inc(s_3["tu"][p], 1)

            each(act, STEPS // 2, scale_up_steps)

            act.wait_ge(s_scale, 4)

            def round_product(m, p):
                free(act, s_4["int"][p], m)
                act.sem_inc(s_go)
                A.activation(work[0][p][:, 0:IC * P].rearrange("p (c t) -> p c t", c=IC), act_all[:, :, bass.ds((2 * m + p) * P, P)],
                             ACT.Identity, bias=round_c[:], scale=to_int[:, 4:5]).then_inc(s_4["t"][p], 1)

            def product_high(m, p):
                this(act, s_4["int"], m, p)
                free(act, s_4["product"][p], m)
                A.activation(down_parts(p)[0].rearrange("p c t -> p (c t)"), work[1][p][:, 0:IC * P], ACT.Copy).then_inc(s_4["hi"][p], 1)

            staggered(act, T, (round_product, 1), (product_high, 0))

        @block.vector
        def _(dve):
            V = nc.vector
            order = Order(dve, s_dve)
            layernorm_scales(dve, order, x_all, stats, mean_var, var, rstd, rtmp, s_var, s_root)
            for t in range(T):
                order.tick(V.tensor_scalar(y_all[:, t, :], x_all[:, t, :], mean_var[:, t, 0:1], rstd[:, t:t + 1],
                                           ALU.subtract, ALU.mult))
            order.tick(V.memset(largest[:], 0.0))
            order.wait()
            order(V.tensor_reduce(step_max[:, 0:T], y_all, AX_X, ALU.max, apply_absolute_value=True))
            V.tensor_reduce(largest[:, 0, 0:1], step_max[:, 0:T], AX_X, ALU.max).then_inc(s_big, 1)

            for i in range(3):
                dve.wait_ge(s_w[i], 16)
                blocks = rows[i].rearrange("p (b k) -> p b k", k=BLOCK)
                to = scaled[i].rearrange("p (b k) -> p b k", k=BLOCK)
                s, inv = b_scale[:, i, :], b_inv[:, i, :]
                order(V.tensor_reduce(s, blocks, AX_X, ALU.max, apply_absolute_value=True))
                order(V.tensor_scalar(s, s, 1 / WQMAX, 1e-12, ALU.mult, ALU.max))
                order(V.reciprocal(inv, s))
                order(V.tensor_tensor(to, blocks, inv.unsqueeze(2).to_broadcast([P, NB, BLOCK]), ALU.mult))
                order(V.tensor_scalar(to, to, ROUND, -ROUND, ALU.add, ALU.add))
                V.tensor_tensor(to, to, s.unsqueeze(2).to_broadcast([P, NB, BLOCK]), ALU.mult).then_inc(s_deq, 1)
            n = 0
            for i in range(3):
                for j in range(IC // 2):
                    p = n % 2
                    dve.wait_ge(s_wh[p], n // 2 + 1)
                    bank = ps[p][:].rearrange("p (c r q) -> p c r q", c=2, r=DC)
                    for c in range(2):
                        ins = V.scalar_tensor_tensor(weight_parts(i, j, guT_lo, dT_lo)[:, c], bank[:, c], WEIGHT_SCALE,
                                                     weight_parts(i, j, guT_hi, dT_hi)[:, c], ALU.mult, ALU.subtract)
                    ins.then_inc(s_wl[p], 1)
                    n += 1

            def new_scale(n, col, unit):
                big = reduced[:, n, col:col + 1]
                c = {0: 0, 1: 1 + col, 2: 3, 3: 4}[n]
                if unit is not None:
                    order(V.tensor_scalar(tmp[:, c:c + 1], big, unit, None, ALU.mult))
                    big = tmp[:, c:c + 1]
                order(V.tensor_scalar(scale[:, c:c + 1], big, 1 / QMAX, 1e-12, ALU.mult, ALU.max))
                order(V.reciprocal(to_int[:, c:c + 1], scale[:, c:c + 1]))
                if unit is not None:
                    order(V.tensor_scalar(to_int[:, c:c + 1], to_int[:, c:c + 1], unit, None, ALU.mult))

            dve.wait_ge(s_red, 1)
            new_scale(0, 0, None)
            V.nop().then_inc(s_scale, 1)

            def input_integers(m, p):
                this(dve, s_t, m, p)
                V.tensor_scalar(work[0][p][:, 0:2 * D], work[0][p][:, 0:2 * D], -ROUND, None, ALU.add).then_inc(s_q[p], 1)

            def input_low(m, p):
                this(dve, s_qh, m, p)
                t0 = (2 * m + p) * 2 * P
                V.tensor_tensor(yT_lo[:, :, bass.ds(t0, 2 * P)], ps[2 + p][:].rearrange("p (c t) -> p c t", c=DC),
                                yT_hi[:, :, bass.ds(t0, 2 * P)], ALU.subtract).then_inc(s_ql[p], 1)

            staggered(dve, T // 2, (input_integers, 1), (input_low, 0))

            def product_maxima(g):
                for k in range(NP):
                    b = k % BANKS
                    dve.wait_ge(s_ev[b], (NP // BANKS) * g + k // BANKS + 1)
                    src = act_all[:, k, bass.ds(g * N, N)] if k < IC else u_out[k % 2][:]
                    V.tensor_reduce(maxes[:, k, bass.ds(g, 1)], src, AX_X, ALU.max, apply_absolute_value=True).then_inc(s_mx[b], 1)

            each(dve, TG, product_maxima)
            for b in range(BANKS):
                dve.wait_ge(s_mx[b], TG * NP // BANKS)
            order(V.tensor_scalar(unit[:, 0:1], scale[:, 0:1], 1 / WEIGHT_SCALE, None, ALU.mult))
            V.tensor_reduce(largest[:, 1, :], maxes[:].rearrange("p (i c) g -> p i (c g)", i=2), AX_X, ALU.max).then_inc(s_big, 1)
            dve.wait_ge(s_red, 2)
            new_scale(1, 0, unit[:, 0:1])
            new_scale(1, 1, unit[:, 0:1])
            V.nop().then_inc(s_scale, 1)

            def gate_integers(m, p):
                this(dve, s_2["t"], m, p)
                V.tensor_scalar(flat[:, bass.ds((2 * m + p) * CB, CB)], work[0][p][:], -ROUND, None, ALU.add).then_inc(s_2["int"][p], 1)

            def sigmoid_integers(m, p):
                this(dve, s_2["shift"], m, p)
                V.tensor_scalar(work[1][p][:], work[0][p][:], 2.0**23 + 65535.0, -2.0**23, ALU.min, ALU.add).then_inc(s_2["sig"][p], 1)

            def gate_maximum(m, p):
                this(dve, s_2["product"], m, p)
                V.tensor_reduce(step_max[:, bass.ds(2 * m + p, 1)], flat[:, bass.ds((2 * m + p) * CB, CB)], AX_X, ALU.max,
                                apply_absolute_value=True).then_inc(s_2["max"][p], 1)

            staggered(dve, STEPS, (gate_integers, 1), (sigmoid_integers, 0), (gate_maximum, -1))
            for p in range(2):
                dve.wait_ge(s_2["max"][p], STEPS // 2)
            order(V.tensor_scalar(unit[:, 1:2], scale[:, 1:2], 2.0**-16, None, ALU.mult))
            V.tensor_reduce(largest[:, 2, 0:1], step_max[:, 0:STEPS], AX_X, ALU.max).then_inc(s_big, 1)
            dve.wait_ge(s_red, 3)
            new_scale(2, 0, unit[:, 1:2])
            V.nop().then_inc(s_scale, 1)

            def part(m, p):
                return flat[:, bass.ds((2 * m + p) * CB, CB)]

            def gated_integers(m, p):
                this(dve, s_3["t"], m, p)
                V.tensor_scalar(part(m, p), work[0][p][:], -ROUND, None, ALU.add).then_inc(s_3["int"][p], 1)

            def multiply_up(m, p):
                this(dve, s_3["tu"], m, p)
                this(dve, s_3["int"], m, p)
                V.scalar_tensor_tensor(part(m, p), work[1][p][:], -ROUND, part(m, p), ALU.add, ALU.mult).then_inc(s_3["product"][p], 1)

            def product_maximum(m, p):
                this(dve, s_3["product"], m, p)
                V.tensor_reduce(step_max[:, bass.ds(2 * m + p, 1)], part(m, p), AX_X, ALU.max, apply_absolute_value=True).then_inc(s_3["max"][p], 1)

            staggered(dve, STEPS, (gated_integers, 1), (multiply_up, 0), (product_maximum, -1))
            for p in range(2):
                dve.wait_ge(s_3["max"][p], STEPS // 2)
            order(V.tensor_tensor(unit[:, 2:3], scale[:, 2:3], scale[:, 3:4], ALU.mult))
            V.tensor_reduce(largest[:, 3, 0:1], step_max[:, 0:STEPS], AX_X, ALU.max).then_inc(s_big, 1)
            dve.wait_ge(s_red, 4)
            new_scale(3, 0, unit[:, 2:3])
            order(V.tensor_scalar(tmp[:, 4:5], scale[:, 4:5], 1 / WEIGHT_SCALE, None, ALU.mult))
            V.nop().then_inc(s_scale, 1)

            def product_integers(m, p):
                this(dve, s_4["t"], m, p)
                free(dve, s_4["lo"][p], m)
                V.tensor_scalar(work[1][p][:, 0:IC * P], work[0][p][:, 0:IC * P], -ROUND, None, ALU.add).then_inc(s_4["int"][p], 1)

            def product_low(m, p):
                this(dve, s_4["hi"], m, p)
                V.tensor_tensor(down_parts(p)[1].rearrange("p c t -> p (c t)"), work[1][p][:, 0:IC * P],
                                down_parts(p)[0].rearrange("p c t -> p (c t)"), ALU.subtract).then_inc(s_4["lo"][p], 1)

            def add_to_x(m, p):
                this(dve, s_4["product"], m, p)
                free(dve, s_4["stored"][p], 16 * m)
                V.scalar_tensor_tensor(u_out[p][:, 0:D], ps[p][:, 0:D], tmp[:, 4:5],
                                       x_all[:, bass.ds(2 * m + p, 1), :].rearrange("p a d -> p (a d)"), ALU.mult, ALU.add).then_inc(s_4["out"][p], 1)

            staggered(dve, T, (product_integers, 1), (product_low, 0), (add_to_x, -1))


def two_layers(nc, x, context, mask, e2, e1, attn, ffn, out):
    tokens, D = x.shape
    E = e1["wg"].shape[1]
    I = ffn["w_gate"].shape[0]
    x_sum = nc.dram_tensor("x_sum", (tokens + P, D), F32, kind="Internal").ap()
    normed = nc.dram_tensor("normed", (tokens + P, D), F32, kind="Internal").ap()
    up_raw = nc.dram_tensor("up_raw", (P, I // P, tokens), F32, kind="Internal").ap()
    experts(nc, "top2", x, context, e2["wg"], e2["bg"], e2["w1"], e2["b1"], e2["w2"], e2["b2"], x_sum, normed, 2, None)
    experts(nc, "top1", x_sum[0:tokens], None, e1["wg"], None, e1["w1"], e1["b1"], e1["w2"], e1["b2"], x_sum, normed, 1,
            tokens // E)
    with nc.sbuf_tensor("x_held", [P, tokens // P, D], F32) as x_held:
        attention(nc, "attn", x_held, x_sum[0:tokens], context, mask, **attn)
        gated_ffn(nc, "ffn", x_held, ffn["w_gate"], ffn["w_up"], ffn["w_down"], up_raw, out)


NAMES = ["x", "ctx_1024", "mask_1x1xSxS2_ik1",
         "L0_xattn_Wg", "L0_xattn_bg", "L0_xattn_W1", "L0_xattn_b1", "L0_xattn_W2", "L0_xattn_b2",
         "L0_ffn_wg", "L0_ffn_w1", "L0_ffn_b1", "L0_ffn_w2", "L0_ffn_b2",
         "L1_xattn_wq_w", "L1_xattn_wq_b", "L1_xattn_wk_w", "L1_xattn_wk_b",
         "L1_xattn_wv_w", "L1_xattn_wv_b", "L1_xattn_wo_w", "L1_xattn_wo_b",
         "L1_ffn_w_gate", "L1_ffn_w_up", "L1_ffn_w_down"]


def kernel(**inputs):
    import numpy as np
    import concourse.bacc as bacc
    from concourse.bass_utils import run_bass_kernel_spmd

    nc = bacc.Bacc("TRN2", target_bir_lowering=False, num_devices=1)
    arrays, a = {}, {}
    for name in NAMES:
        array = np.ascontiguousarray(inputs[name])
        arrays[f"in_{name}"] = array
        a[name] = nc.dram_tensor(f"in_{name}", array.shape, mybir.dt.from_np(array.dtype), kind="ExternalInput").ap()
    shape = inputs["x"].shape
    out = nc.dram_tensor("out", shape, F32, kind="ExternalOutput").ap()
    rows = [t.rearrange("b s d -> (b s) d") for t in (a["x"], a["ctx_1024"], out)]
    two_layers(nc, rows[0], rows[1], a["mask_1x1xSxS2_ik1"],
               {k.lower(): a[f"L0_xattn_{k}"] for k in ("Wg", "bg", "W1", "b1", "W2", "b2")},
               {k: a[f"L0_ffn_{k}"] for k in ("wg", "w1", "b1", "w2", "b2")},
               {k[0:2] if k[3] == "w" else "b" + k[1]: a[f"L1_xattn_{k}"]
                for k in ("wq_w", "wq_b", "wk_w", "wk_b", "wv_w", "wv_b", "wo_w", "wo_b")},
               {k: a[f"L1_ffn_{k}"] for k in ("w_gate", "w_up", "w_down")},
               rows[2])
    result = run_bass_kernel_spmd(nc, [arrays], core_ids=[0])
    return result.results[0]["out"]
```

```python
import concourse.bass as bass
from concourse import mybir
from contextlib import ExitStack, contextmanager

F32 = mybir.dt.float32
F16 = mybir.dt.float16
I32 = mybir.dt.int32
ALU = mybir.AluOpType
ACT = mybir.ActivationFunctionType
AX_X = mybir.AxisListType.X
P = 128
WEIGHT_SCALE = 64.0
ROUND = 1.5 * 2.0**23
EPS = 1e-05


@contextmanager
def stage_semaphores(nc, name):
    held = []

    def sem(n):
        held.append(nc.alloc_semaphore(name=f"{name}_{n}"))
        return held[-1]

    yield sem
    nc.clear_and_free_semaphores(held)
    nc.all_engine_barrier()


class Order:

    def __init__(self, engine, semaphore):
        self.engine, self.semaphore, self.count = engine, semaphore, 0

    def __call__(self, instruction):
        instruction.then_inc(self.semaphore, 1)
        self.count = self.count + 1
        self.engine.wait_ge(self.semaphore, self.count)

    def tick(self, instruction):
        instruction.then_inc(self.semaphore, 1)
        self.count = self.count + 1

    def wait(self):
        self.engine.wait_ge(self.semaphore, self.count)


def free(engine, semaphore, value):
    if not (isinstance(value, int) and value <= 0):
        engine.wait_ge(semaphore, value)


def each(engine, n, body):
    body(0)
    with engine.Fori(1, n) as m:
        body(m)


def staggered(engine, count, *steps):
    ahead, behind = max(d for _, d in steps), -min(d for _, d in steps)

    def pair(m):
        for p in range(2):
            for step, distance in steps:
                j = p + distance
                if not isinstance(m, int) or 0 <= 2 * m + j < count:
                    step(m + j // 2, j % 2)

    start, end = 1 + (behind + 1) // 2, (count - ahead) // 2
    for m in range(-((ahead + 1) // 2), start):
        pair(m)
    with engine.Fori(start, end) as m:
        pair(m)
    for m in range(end, (count + behind + 1) // 2):
        pair(m)


def layernorm_scales(dve, order, x_all, stats, mean_var, var, rstd, rtmp, s_var, s_root):
    V = dve
    T = x_all.shape[1]
    for t in range(T):
        order.tick(V.bn_stats(stats[:, t, :], x_all[:, t, :]))
    order.wait()
    for t in range(T):
        order.tick(V.bn_aggr(mean_var[:, t, :], stats[:, t, :]))
    order.wait()
    V.tensor_scalar(var[:], mean_var[:, :, 1], EPS, None, ALU.add).then_inc(s_var, 1)
    dve.wait_ge(s_root, 1)
    order(V.reciprocal(rstd[:], rstd[:]))
    order(V.tensor_tensor(rtmp[:], rstd[:], rstd[:], ALU.mult))
    order(V.tensor_tensor(rtmp[:], rtmp[:], var[:], ALU.mult))
    order(V.tensor_scalar(rtmp[:], rtmp[:], -0.5, 1.5, ALU.mult, ALU.add))
    order(V.tensor_tensor(rstd[:], rstd[:], rtmp[:], ALU.mult))


def broadcast_rows(ap, rows, n):
    return bass.AP(tensor=ap.tensor, offset=ap.offset, ap=[[0, rows], [1, n]])


def experts(nc, name, x, gate_source, wg, bg, w1, b1, w2, b2, x_sum, normed, choices, capacity):
    tokens, D = x.shape
    E = wg.shape[1]
    F = w1.shape[2]
    T, DC, FC = tokens // P, D // P, F // P
    R = 2 * P
    if capacity is None:
        NT = (choices * tokens + E * (R - 1)) // R
        NT += NT % 2
    else:
        NT = E * capacity // R
    NS = 2 * NT
    CHUNK = 1024
    CPE = 2 * DC * F // CHUNK
    assert DC * F == FC * D and CPE == 4 and DC == 2 and FC == 8
    GC = 2

    with ExitStack() as ctx:
        sem = ctx.enter_context(stage_semaphores(nc, name))

        def sb(n, shape, dt):
            return ctx.enter_context(nc.sbuf_tensor(f"{name}_{n}", shape, dt))

        def pb(n, shape, dt):
            return ctx.enter_context(nc.psum_tensor(f"{name}_{n}", shape, dt))


        w_hi = sb("w_hi", [P, E, CPE, CHUNK], F16)
        w_lo = sb("w_lo", [P, E, CPE, CHUNK], F16)
        staged = [sb(f"staged{c}", [P, CHUNK], F32) for c in range(CPE)]
        x_all = sb("x_all", [P, T, D], F32)
        flat = x_all[:].rearrange("p t d -> p (t d)")
        h32 = flat[:, 0:FC * R]
        at = FC * R
        parts = flat[:, at:at + 2 * FC * R].bitcast(F16)
        h_hi, h_lo = ([parts[:, (2 * i + p) * FC * R:(2 * i + p + 1) * FC * R].rearrange("p (c t) -> p c t", c=FC)
                       for p in range(2)] for i in range(2))
        at += 2 * FC * R
        xg, y = ([flat[:, at + (2 * i + p) * 2 * D:at + (2 * i + p + 1) * 2 * D].rearrange("p (k d) -> p k d", k=2)
                  for p in range(2)] for i in range(2))
        xT_hi = [sb(f"xT_hi{p}", [P, DC, R], F16) for p in range(2)]
        xT_lo = [sb(f"xT_lo{p}", [P, DC, R], F16) for p in range(2)]
        gate_in = [sb(f"gate_in{p}", [P, GC, D], F32) for p in range(2)]
        gateT = [xT_hi[p][:].rearrange("p c t -> p (c t)").bitcast(F32).rearrange("p (c t) -> p c t", c=DC) for p in range(2)]
        b1_rows = sb("b1_rows", [E * FC, P], F32)
        b1T = sb("b1T", [P, E * FC], F32)
        b2_all = sb("b2_all", [P, E, D], F32)
        wg_sb = sb("wg_sb", [P, DC, E], F32)
        bg_sb = sb("bg_sb", [P, E], F32)
        ident = sb("ident", [P, P], F32)
        before = sb("before", [P, P], F16)
        ones = sb("ones", [P, P], F16)
        expert_no = sb("expert_no", [P, E], F32)
        lane_no = sb("lane_no", [P, P], F32)
        pad_row = sb("pad_row", [P, 1], F32)
        token_1 = sb("token_1", [P, T], F32)
        stats = sb("stats", [P, T, 6], F32)
        mean_var = sb("mean_var", [P, T, 2], F32)
        rstd = sb("rstd", [P, T], F32)
        rtmp = sb("rtmp", [P, T], F32)
        logits = sb("logits", [P, T, E], F32)
        work = sb("work", [P, T, E], F32)
        onehot = [sb(f"onehot{c}", [P, T, E], F32) for c in range(choices)]
        oh16 = sb("oh16", [P, T, E], F16)
        best = [sb(f"best{c}", [P, T], F32) for c in range(choices)]
        first = sb("first", [P, T], F32)
        weight = [sb(f"weight{c}", [P, T], F32) for c in range(choices)]
        total = sb("total", [P, E, T], F32)
        running = sb("running", [P, E, T], F32)
        one_t = sb("one_t", [P, T], F32)
        tiles_of = sb("tiles_of", [P, E], F32)
        start_of = sb("start_of", [P, E], F32)
        ends_of = sb("ends_of", [P, E], F32)
        slot_div = [sb(f"slot_div{c}", [P, T], F32) for c in range(choices)]
        slot_mod = [sb(f"slot_mod{c}", [P, T], F32) for c in range(choices)]
        pick_lane = [sb(f"pick_lane{p}", [P, P], F32) for p in range(2)]
        pick_tile = [sb(f"pick_tile{p}", [P, 2, NS], F32) for p in range(2)]
        row_f = sb("row_f", [P, NS], F32)
        pad_f = sb("pad_f", [P, NS], F32)
        row_of_slot = sb("row_of_slot", [P, NS], I32)
        weight_of_slot = sb("weight_of_slot", [P, NS], F32)
        expert_f = sb("expert_f", [P, NT], F32)
        expert_of_tile = sb("expert_of_tile", [P, NT], I32)
        rows_in = [[sb(f"rows_in{p}{k}", [P, 1], I32) for k in range(2)] for p in range(2)]
        rows_out = [sb(f"rows_out{p}", [P, 1], I32) for p in range(2)]

        xT_ps = [pb(f"xT_ps{p}", [P, 512], F32) for p in range(2)]
        h_ps = pb("h_ps", [P, 4, 512], F32)
        y_ps = [pb(f"y_ps{p}", [P, 512], F32) for p in range(2)]

        s_x = [sem(f"x_quarter{q}_loaded") for q in range(4)]; s_small = sem("small_loaded"); s_gate_in = [sem(f"gate_in{p}_loaded") for p in range(2)]
        s_staged = [sem(f"staged{c}_loaded") for c in range(CPE)]
        s_hi = sem("w_hi_done"); s_split = sem("w_split")
        s_const = sem("constants"); s_pool = sem("pool_order"); s_dve = sem("dve_order"); s_act = sem("act_order")
        s_var = sem("variances"); s_root = sem("roots"); s_normed = sem("normed"); s_stored = sem("normed_stored"); s_begun = sem("x_sum_begun")
        s_go = sem("pool_goes_on")
        s_b1 = sem("b1_transposed"); s_b1T = sem("b1T_ready")
        s_tr = [sem(f"gate_transposed{p}") for p in range(2)]; s_trc = [sem(f"gateT{p}_ready") for p in range(2)]
        s_lg = [sem(f"logits_from{p}") for p in range(2)]
        s_diff = sem("exp_in"); s_exp = sem("exp_out")
        s_oh = sem("onehots"); s_count = sem("counts")
        s_pick = [sem(f"picks{p}_ready") for p in range(2)]; s_picked = [sem(f"picks{p}_used") for p in range(2)]
        s_table = sem("tables_ready")
        s_rows_in = [sem(f"rows_in{p}_copied") for p in range(2)]; s_rows_out = [sem(f"rows_out{p}_copied") for p in range(2)]
        s_xg = [sem(f"xg{p}_gathered") for p in range(2)]; s_xt = [sem(f"xT{p}_transposed") for p in range(2)]
        s_xh = [sem(f"xT_hi{p}_ready") for p in range(2)]; s_xl = [sem(f"xT_lo{p}_ready") for p in range(2)]
        s_h = [sem(f"h{p}_banks") for p in range(2)]; s_h32 = [sem(f"h32_{p}_ready") for p in range(2)]
        s_hh = [sem(f"h_hi{p}_ready") for p in range(2)]; s_hl = [sem(f"h_lo{p}_ready") for p in range(2)]
        s_l2 = [sem(f"y_ps{p}_ready") for p in range(2)]; s_yb = [sem(f"y{p}_biased") for p in range(2)]; s_y = [sem(f"y{p}_ready") for p in range(2)]
        s_added = [sem(f"y{p}_added") for p in range(2)]

        M = NT // 2
        HEAD = 4
        block = ctx.enter_context(nc.Block())

        @block.sync
        def _(sp):
            x_tiles = x.rearrange("(t p) d -> p t d", p=P)
            for q in range(4):
                n = T // 4
                sp.dma_start(x_all[:, q * n:(q + 1) * n, :], x_tiles[:, q * n:(q + 1) * n, :]).then_inc(s_x[q], 16)
            sp.dma_start(wg_sb[:], wg.rearrange("(c p) e -> p c e", p=P)).then_inc(s_small, 16)
            if bg is not None:
                sp.dma_start(bg_sb[:], broadcast_rows(bg, P, E)).then_inc(s_small, 16)
            sp.dma_start(b1_rows[:], b1.rearrange("e (c f) -> (e c) f", f=P)).then_inc(s_small, 16)
            sp.dma_start(b2_all[:].rearrange("p e d -> p (e d)"), broadcast_rows(b2, P, E * D)).then_inc(s_small, 16)

            def load_expert(e):
                w1_e = w1[e].rearrange("(c p) f -> p c f", p=P)
                w2_e = w2[e].rearrange("(c p) d -> p c d", p=P)
                for c in range(CPE):
                    if not (isinstance(e, int) and e == 0):
                        sp.wait_ge(s_split, (e - 1) * CPE + c + 1)
                    if c < 2:
                        sp.dma_start(staged[c][:], w1_e[:, c, :]).then_inc(s_staged[c], 16)
                    else:
                        sp.dma_start(staged[c][:].rearrange("p (c d) -> p c d", d=D),
                                     w2_e[:, (c - 2) * 4:(c - 1) * 4, :]).then_inc(s_staged[c], 16)

            if gate_source is not None:
                g_tiles = gate_source.rearrange("(t p) d -> p t d", p=P)
                for p in range(2):
                    sp.dma_start(gate_in[p][:], g_tiles[:, p * GC:(p + 1) * GC, :]).then_inc(s_gate_in[p], 16)
                load_expert(0)
                with sp.Fori(1, T // GC // 2) as m:
                    for p in range(2):
                        for k in range(GC):
                            sp.wait_ge(s_tr[k], 2 * m - 1 + p)
                        sp.dma_start(gate_in[p][:], g_tiles[:, bass.ds((2 * m + p) * GC, GC), :]).then_inc(s_gate_in[p], 16)
            else:
                load_expert(0)
            sp.wait_ge(s_normed, 1)
            n_tiles = normed[0:tokens].rearrange("(t p) d -> p t d", p=P)
            sp.dma_start(n_tiles, x_all[:]).then_inc(s_stored, 16)
            sp.dma_start(normed[tokens:tokens + P], x_all[:, 0, :]).then_inc(s_stored, 16)
            with sp.Fori(1, E) as e:
                load_expert(e)
            for k in range(2):
                sp.wait_ge(s_added[k], 16 * NT)

        @block.gpsimd
        def _(pool):
            order = Order(pool, s_pool)
            order(nc.gpsimd.memset(ident[:], 0.0))
            order(nc.gpsimd.memset(before[:], 1.0))
            nc.gpsimd.memset(ones[:], 1.0).then_inc(s_const, 1)
            nc.gpsimd.memset(one_t[:], 1.0).then_inc(s_const, 1)
            nc.gpsimd.affine_select(out=ident[:], in_=ident[:], compare_op=ALU.not_equal, fill=1.0, base=0,
                                    pattern=[[-1, P]], channel_multiplier=1).then_inc(s_const, 1)
            nc.gpsimd.affine_select(out=before[:], in_=before[:], compare_op=ALU.is_gt, fill=0.0, base=0,
                                    pattern=[[1, P]], channel_multiplier=-1).then_inc(s_const, 1)
            kw = dict(allow_small_or_imprecise_dtypes=True)
            nc.gpsimd.iota(expert_no[:], pattern=[[1, E]], base=0, channel_multiplier=0, **kw).then_inc(s_const, 1)
            nc.gpsimd.iota(lane_no[:], pattern=[[1, P]], base=0, channel_multiplier=0, **kw).then_inc(s_const, 1)
            nc.gpsimd.iota(pad_row[:], pattern=[[1, 1]], base=tokens + 1, channel_multiplier=1, **kw).then_inc(s_const, 1)
            nc.gpsimd.iota(token_1[:], pattern=[[P, T]], base=1, channel_multiplier=1, **kw).then_inc(s_const, 1)

            def gather(m, p):
                free(pool, s_xt[p], m)
                for k in range(2):
                    rows = rows_in[p][k]
                    nc.gpsimd.tensor_copy(rows[:], row_of_slot[:, bass.ds(4 * m + 2 * p + k, 1)]).then_inc(s_rows_in[p], 1)
                    pool.wait_ge(s_rows_in[p], 2 * m + k + 1)
                    pool.sem_inc(s_go)
                    nc.gpsimd.indirect_dma_start(out=xg[p][:, k, :], out_offset=None, in_=normed,
                                                 in_offset=bass.IndirectOffsetOnAxis(ap=rows[:, 0:1], axis=0)
                                                 ).then_inc(s_xg[p], 16)

            def add(m, p):
                for k in range(2):
                    free(pool, s_added[1 - k], 16 * (2 * m + p + k))
                    nc.gpsimd.tensor_copy(rows_out[k][:], row_of_slot[:, bass.ds(4 * m + 2 * p + k, 1)]).then_inc(s_rows_out[k], 1)
                    pool.wait_ge(s_rows_out[k], 2 * m + p + 1)
                    pool.wait_ge(s_y[p], m + 1)
                    pool.sem_inc(s_go)
                    nc.gpsimd.indirect_dma_start(out=x_sum, out_offset=bass.IndirectOffsetOnAxis(ap=rows_out[k][:, 0:1], axis=0),
                                                 in_=y[p][:, k, :], in_offset=None, compute_op=ALU.add).then_inc(s_added[k], 16)

            pool.wait_ge(s_table, 1)
            pool.wait_ge(s_stored, 32)
            for m in range(2):
                for p in range(2):
                    gather(m, p)
            if gate_source is not None:
                pool.wait_ge(s_begun, 32)
            with pool.Fori(2, M) as m:
                for p in range(2):
                    gather(m, p)
                    add(m - 2, p)
            for m in range(M - 2, M):
                for p in range(2):
                    add(m, p)

        def w1_at(w, e, dc, fc):
            return w[:, bass.ds(e, 1), dc, fc * P:(fc + 1) * P].rearrange("p a f -> p (a f)")

        def w2_at(w, e, fc):
            c, r = divmod(fc * D, CHUNK)
            return w[:, bass.ds(e, 1), 2 + c, r:r + D].rearrange("p a f -> p (a f)")

        @block.tensor
        def _(pe):
            pe.wait_ge(s_const, 8)
            pe.wait_ge(s_small, 48 + 16 * (bg is not None))
            nc.tensor.transpose(y_ps[0][:, 0:E * FC], b1_rows[:], ident[0:E * FC, 0:E * FC]).then_inc(s_b1, 1)
            lg = y_ps[1]
            if gate_source is None:
                pe.wait_ge(s_normed, 1)

            def gate_transpose(m, k, p):
                free(pe, s_trc[p], m * GC + k // 2)
                if gate_source is not None:
                    g = k // GC
                    if k % GC == 0:
                        pe.wait_ge(s_gate_in[g], 16 * (m + 1))
                    src = gate_in[g][:, k % GC, :]
                    for c in range(DC):
                        last = nc.tensor.transpose(xT_ps[p][:, c * P:(c + 1) * P], src[:, c * P:(c + 1) * P], ident[:])
                    last.then_inc(s_tr[p], 1)
                else:
                    for c in range(DC):
                        src = x_all[:, bass.ds(2 * GC * m + k, 1), c * P:(c + 1) * P].rearrange("p a d -> p (a d)") if not isinstance(m, int) else x_all[:, 2 * GC * m + k, c * P:(c + 1) * P]
                        last = nc.tensor.transpose(xT_ps[p][:, c * P:(c + 1) * P], src, ident[:])
                    last.then_inc(s_tr[p], 1)

            def gate_logits(m, k, p):
                pe.wait_ge(s_trc[p], m * GC + k // 2 + 1)
                t = 2 * GC * m + k
                for c in range(DC):
                    last = nc.tensor.matmul(lg[:, bass.ds(t * E, E)], gateT[p][:, c, :], wg_sb[:, c, :],
                                            start=(c == 0), stop=(c == DC - 1))
                last.then_inc(s_lg[p], 1)

            if gate_source is not None:
                def gate_tiles(m):
                    for k in range(2 * GC):
                        gate_transpose(m, k, k % 2)
                        if k % 2:
                            gate_logits(m, k - 1, 0)
                            gate_logits(m, k, 1)

                each(pe, T // GC // 2, gate_tiles)
            else:
                for m in range(T // GC // 2):
                    for k in range(2 * GC):
                        gate_transpose(m, k, k % 2)
                        if k % 2:
                            gate_logits(m, k - 1, 0)
                            gate_logits(m, k, 1)
            pe.wait_ge(s_oh, 1)
            pairs = oh16[:].rearrange("p t e -> p (t e)")
            nc.tensor.matmul(h_ps[:, 0, 0:T * E], before[:], pairs, start=True, stop=True)
            nc.tensor.matmul(h_ps[:, 1, 0:T * E], ones[:], pairs, start=True, stop=True).then_inc(s_count, 1)
            rounds = T * choices
            table = h_ps[:, 2, 0:2 * NS]

            def pick(m, p, start, stop):
                pe.wait_ge(s_pick[p], m + 1)
                nc.tensor.matmul(table, pick_lane[p][:], pick_tile[p][:].rearrange("p a n -> p (a n)"),
                                 start=start, stop=stop, skip_group_check=True).then_inc(s_picked[p], 1)

            pick(0, 0, True, False)
            pick(0, 1, False, False)
            with pe.Fori(1, rounds // 2 - 1) as m:
                for p in range(2):
                    pick(m, p, False, False)
            pick(rounds // 2 - 1, 0, False, False)
            pick(rounds // 2 - 1, 1, False, True)

            def transpose_in(m, p):
                pe.wait_ge(s_xg[p], 32 * (m + 1))
                if isinstance(m, int) and m == 0:
                    pe.wait_ge(s_table, 1)
                else:
                    pe.wait_ge(s_xl[p], m)
                for c in range(DC):
                    for k in range(2):
                        last = nc.tensor.transpose(xT_ps[p][:, c * R + k * P:c * R + (k + 1) * P],
                                                   xg[p][:, k, c * P:(c + 1) * P], ident[:])
                last.then_inc(s_xt[p], 1)

            def expert(i):
                return pe.value_load(expert_of_tile[0:1, bass.ds(i, 1)], min_val=0, max_val=E - 1)

            def layer1(m, p, e, fc):
                b, q = divmod(fc, 2)
                if fc == 0:
                    pe.wait_ge(s_xl[p], m + 1)
                if q == 0:
                    free(pe, s_h32[1 - p], 4 * (m - 1 + p) + b + 1)
                out = h_ps[:, b, q * R:(q + 1) * R]
                for c in range(DC):
                    hi, lo = w1_at(w_hi, e, c, fc), w1_at(w_lo, e, c, fc)
                    nc.tensor.matmul(out, hi, xT_hi[p][:, c, :], start=(c == 0), stop=False)
                    nc.tensor.matmul(out, hi, xT_lo[p][:, c, :], start=False, stop=False)
                    last = nc.tensor.matmul(out, lo, xT_hi[p][:, c, :], start=False, stop=(c == DC - 1))
                if q == 1:
                    last.then_inc(s_h[p], 1)

            def layer2(m, p, e, fc):
                if fc % 2 == 0:
                    pe.wait_ge(s_hl[p], 4 * m + 1 + fc // 2)
                if fc == 0:
                    free(pe, s_yb[p], m)
                hi, lo = w2_at(w_hi, e, fc), w2_at(w_lo, e, fc)
                for k in range(2):
                    out = y_ps[p][:, k * D:(k + 1) * D]
                    rows = slice(k * P, (k + 1) * P)
                    nc.tensor.matmul(out, h_hi[p][:, fc, rows], hi, start=(fc == 0 and k == 0), stop=False, skip_group_check=True)
                    nc.tensor.matmul(out, h_hi[p][:, fc, rows], lo, start=False, stop=False, skip_group_check=True)
                    last = nc.tensor.matmul(out, h_lo[p][:, fc, rows], hi, start=False, stop=(fc == FC - 1), skip_group_check=True)
                if fc == FC - 1:
                    last.then_inc(s_l2[p], 1)

            def tiles(m, experts_split, more=True):
                first_tile = isinstance(m, int) and m == 0
                e_before = None if first_tile else expert(2 * m - 1)
                for p in range(2):
                    e = expert(2 * m + p)
                    if more or p == 0:
                        transpose_in(m + p, 1 - p)
                    if not experts_split:
                        pe.wait_ge(s_split, (e + 1) * CPE)
                    for fc in range(FC):
                        layer1(m, p, e, fc)
                        if e_before is not None:
                            layer2(m - 1 + p, 1 - p, e_before, fc)
                    e_before = e
                return e_before

            transpose_in(0, 0)
            for m in range(HEAD):
                tiles(m, False)
            pe.wait_ge(s_split, E * CPE)
            with pe.Fori(HEAD, M - 1) as m:
                tiles(m, True)
            e = tiles(M - 1, True, more=False)
            for fc in range(FC):
                layer2(M - 1, 1, e, fc)

        def split_hi(act, e):
            for c in range(CPE):
                act.wait_ge(s_staged[c], 16 * (e + 1))
                nc.scalar.activation(w_hi[:, e, c, :], staged[c][:], ACT.Copy, scale=WEIGHT_SCALE).then_inc(s_hi, 1)

        @block.scalar
        def _(act):
            if gate_source is not None:
                act.dma_start(x_sum[0:tokens], x).then_inc(s_begun, 16)
                act.dma_start(x_sum[tokens:tokens + P], x[0:P]).then_inc(s_begun, 16)
            act.wait_ge(s_var, 1)
            nc.scalar.activation(rstd[:], rtmp[:], ACT.Sqrt).then_inc(s_root, 1)
            act.wait_ge(s_b1, 1)
            nc.scalar.activation(b1T[:], y_ps[0][:, 0:E * FC], ACT.Copy).then_inc(s_b1T, 1)
            split_hi(act, 0)

            def gate_copy(n, p):
                act.wait_ge(s_tr[p], n + 1)
                if not (isinstance(n, int) and n == 0):
                    act.wait_ge(s_lg[p], n)
                nc.scalar.activation(gateT[p].rearrange("p c t -> p (c t)"), xT_ps[p][:, 0:D], ACT.Copy).then_inc(s_trc[p], 1)

            gate_copy(0, 0)
            gate_copy(0, 1)
            with act.Fori(1, T // 2) as n:
                for p in range(2):
                    gate_copy(n, p)
            act.wait_ge(s_diff, 1)
            if choices == 2:
                nc.scalar.activation(weight[1][:], rtmp[:], ACT.Exp).then_inc(s_exp, 1)
            else:
                nc.scalar.activation(work[:], work[:], ACT.Exp).then_inc(s_exp, 1)

            def x_high(m, p):
                act.wait_ge(s_xt[p], m + 1)
                free(act, s_h[p], 4 * m)
                nc.scalar.activation(xT_hi[p][:].rearrange("p c t -> p (c t)"), xT_ps[p][:], ACT.Copy).then_inc(s_xh[p], 1)

            def hidden(m, p, i):
                e = act.value_load(expert_of_tile[0:1, bass.ds(i, 1)], min_val=0, max_val=E - 1)
                for b in range(4):
                    act.wait_ge(s_h[p], 4 * m + b + 1)
                    free(act, s_hl[1 - p], 4 * (m - 1 + p) + b + 1)
                    for q in range(2):
                        fc = 2 * b + q
                        last = nc.scalar.activation(h32[:, fc * R:(fc + 1) * R], h_ps[:, b, q * R:(q + 1) * R],
                                                    ACT.Relu, bias=b1T[:, bass.ds(e * FC + fc, 1)], scale=1 / WEIGHT_SCALE)
                    last.then_inc(s_h32[p], 1)

            act.wait_ge(s_table, 1)
            x_high(0, 0)
            for m in range(HEAD):
                for p in range(2):
                    if 0 < 2 * m + p < E:
                        split_hi(act, 2 * m + p)
                    x_high(m + p, 1 - p)
                    hidden(m, p, 2 * m + p)
            with act.Fori(HEAD, M - 1) as m:
                for p in range(2):
                    x_high(m + p, 1 - p)
                    hidden(m, p, 2 * m + p)
            x_high(M - 1, 1)
            hidden(M - 1, 0, NT - 2)
            hidden(M - 1, 1, NT - 1)

        def split_lo(dve, e):
            for c in range(CPE):
                dve.wait_ge(s_hi, e * CPE + c + 1)
                nc.vector.scalar_tensor_tensor(w_lo[:, e, c, :], staged[c][:], WEIGHT_SCALE, w_hi[:, e, c, :],
                                               ALU.mult, ALU.subtract).then_inc(s_split, 1)

        @block.vector
        def _(dve):
            V = nc.vector
            order = Order(dve, s_dve)
            for t in range(T):
                if t % (T // 4) == 0:
                    dve.wait_ge(s_x[t // (T // 4)], 16)
                order.tick(V.bn_stats(stats[:, t, :], x_all[:, t, :]))
            order.wait()
            for t in range(T):
                order.tick(V.bn_aggr(mean_var[:, t, :], stats[:, t, :]))
            order.wait()
            V.tensor_scalar(rtmp[:], mean_var[:, :, 1], EPS, None, ALU.add).then_inc(s_var, 1)
            dve.wait_ge(s_root, 1)
            order(V.reciprocal(rstd[:], rstd[:]))
            order(V.tensor_tensor(first[:], rstd[:], rstd[:], ALU.mult))
            order(V.tensor_tensor(first[:], first[:], rtmp[:], ALU.mult))
            order(V.tensor_scalar(first[:], first[:], -0.5, 1.5, ALU.mult, ALU.add))
            order(V.tensor_tensor(rstd[:], rstd[:], first[:], ALU.mult))
            for t in range(T):
                order.tick(V.tensor_scalar(x_all[:, t, :], x_all[:, t, :], mean_var[:, t, 0:1], rstd[:, t:t + 1],
                                           ALU.subtract, ALU.mult))
            order.wait()
            V.nop().then_inc(s_normed, 1)
            split_lo(dve, 0)

            def by_expert(ap):
                return ap.unsqueeze(2).to_broadcast([P, T, E])

            def of_expert(ap):
                return ap.unsqueeze(1).to_broadcast([P, T, E])

            dve.wait_ge(s_const, 8)
            for p in range(2):
                dve.wait_ge(s_lg[p], T // 2)
            lg = y_ps[1][:, 0:T * E].rearrange("p (t e) -> p t e", e=E)
            if bg is not None:
                order(V.tensor_tensor(logits[:], lg, of_expert(bg_sb[:]), ALU.add))
            else:
                order(V.tensor_copy(logits[:], lg))
            for c in range(choices):
                order(V.tensor_reduce(best[c][:], logits[:], AX_X, ALU.max))
                order(V.tensor_tensor(work[:], logits[:], by_expert(best[c][:]), ALU.is_lt))
                order(V.tensor_scalar(work[:], work[:], float(E), None, ALU.mult))
                order(V.tensor_tensor(work[:], work[:], of_expert(expert_no[:]), ALU.add))
                order(V.tensor_reduce(first[:], work[:], AX_X, ALU.min))
                order(V.tensor_tensor(onehot[c][:], of_expert(expert_no[:]), by_expert(first[:]), ALU.is_equal))
                if c + 1 < choices:
                    order(V.tensor_scalar(work[:], onehot[c][:], -3e38, None, ALU.mult))
                    order(V.tensor_tensor(logits[:], logits[:], work[:], ALU.add))
            if choices == 2:
                order(V.tensor_tensor(oh16[:], onehot[0][:], onehot[1][:], ALU.add))
                V.nop().then_inc(s_oh, 1)
                order(V.tensor_tensor(rtmp[:], best[1][:], best[0][:], ALU.subtract))
                V.nop().then_inc(s_diff, 1)
                dve.wait_ge(s_exp, 1)
                order(V.tensor_scalar(weight[0][:], weight[1][:], 1.0, None, ALU.add))
                order(V.reciprocal(weight[0][:], weight[0][:]))
                order(V.tensor_tensor(weight[1][:], weight[1][:], weight[0][:], ALU.mult))
            else:
                order(V.tensor_copy(oh16[:], onehot[0][:]))
                V.nop().then_inc(s_oh, 1)
                order(V.tensor_tensor(work[:], logits[:], by_expert(best[0][:]), ALU.subtract))
                V.nop().then_inc(s_diff, 1)
                dve.wait_ge(s_exp, 1)
                order(V.tensor_reduce(weight[0][:], work[:], AX_X, ALU.add))
                order(V.reciprocal(weight[0][:], weight[0][:]))

            dve.wait_ge(s_count, 1)
            order(V.tensor_copy(total[:].rearrange("p e t -> p t e"),
                                h_ps[:, 1, 0:T * E].rearrange("p (t e) -> p t e", e=E)))
            for e in range(E):
                order.tick(V.tensor_tensor_scan(running[:, e, :], one_t[:], total[:, e, :], 0.0, ALU.mult, ALU.add))
            order.wait()
            if capacity is None:
                order(V.tensor_scalar(tiles_of[:], running[:, :, T - 1], 1 / R, (R - 1) / R - (0.5 - 0.5 / R), ALU.mult, ALU.add))
                order(V.tensor_scalar(tiles_of[:], tiles_of[:], ROUND, -ROUND, ALU.add, ALU.add))
                order(V.tensor_scalar(tiles_of[:], tiles_of[:], 1.0, None, ALU.max))
                order(V.tensor_tensor_scan(ends_of[:], one_t[:, 0:E], tiles_of[:], 0.0, ALU.mult, ALU.add))
                order(V.tensor_tensor(start_of[:], ends_of[:], tiles_of[:], ALU.subtract))
            else:
                order(V.tensor_scalar(start_of[:], expert_no[:], float(capacity // R), None, ALU.mult))
            order(V.tensor_tensor(running[:], running[:], total[:], ALU.subtract))
            order(V.tensor_tensor(work[:], running[:].rearrange("p e t -> p t e"),
                                  h_ps[:, 0, 0:T * E].rearrange("p (t e) -> p t e", e=E), ALU.add))
            if capacity is not None:
                order(V.tensor_scalar(logits[:], work[:], float(capacity), float(4 * tokens), ALU.is_ge, ALU.mult))
                order(V.tensor_tensor(work[:], work[:], logits[:], ALU.add))
            order(V.tensor_scalar(ends_of[:], start_of[:], float(R), None, ALU.mult))
            order(V.tensor_tensor(work[:], work[:], of_expert(ends_of[:]), ALU.add))
            for c in range(choices):
                order(V.tensor_tensor(logits[:], work[:], onehot[c][:], ALU.mult))
                order(V.tensor_reduce(first[:], logits[:], AX_X, ALU.add))
                order(V.tensor_scalar(slot_div[c][:], first[:], 1 / P, -0.49609375, ALU.mult, ALU.add))
                order(V.tensor_scalar(slot_div[c][:], slot_div[c][:], ROUND, -ROUND, ALU.add, ALU.add))
                order(V.scalar_tensor_tensor(slot_mod[c][:], slot_div[c][:], -float(P), first[:], ALU.mult, ALU.add))
            order(V.tensor_scalar(expert_f[:], lane_no[:, 0:NT], start_of[:, 1:2], None, ALU.is_ge))
            for e in range(2, E):
                order(V.scalar_tensor_tensor(expert_f[:], lane_no[:, 0:NT], start_of[:, e:e + 1], expert_f[:],
                                             ALU.is_ge, ALU.add))
            order(V.tensor_copy(expert_of_tile[:], expert_f[:]))

            def picks(m, p, c, t):
                free(dve, s_picked[p], m)
                V.tensor_scalar(pick_lane[p][:], lane_no[:], slot_mod[c][:, bass.ds(t, 1)], None, ALU.is_equal)
                V.tensor_scalar(pick_tile[p][:, 0, :], lane_no[:, 0:NS], slot_div[c][:, bass.ds(t, 1)],
                                token_1[:, bass.ds(t, 1)], ALU.is_equal, ALU.mult)
                V.tensor_scalar(pick_tile[p][:, 1, :], lane_no[:, 0:NS], slot_div[c][:, bass.ds(t, 1)],
                                weight[c][:, bass.ds(t, 1)], ALU.is_equal, ALU.mult).then_inc(s_pick[p], 1)

            if choices == 2:
                picks(0, 0, 0, 0)
                picks(0, 1, 1, 0)
                with dve.Fori(1, T) as t:
                    for c in range(2):
                        picks(t, c, c, t)
            else:
                picks(0, 0, 0, 0)
                picks(0, 1, 0, 1)
                with dve.Fori(1, T // 2) as m:
                    for p in range(2):
                        picks(m, p, 0, 2 * m + p)
            for p in range(2):
                dve.wait_ge(s_picked[p], T * choices // 2)
            table = h_ps[:, 2, 0:2 * NS]
            order(V.tensor_scalar(pad_f[:], table[:, 0:NS], 0.0, pad_row[:], ALU.is_equal, ALU.mult))
            order(V.scalar_tensor_tensor(row_f[:], table[:, 0:NS], -1.0, pad_f[:], ALU.add, ALU.add))
            order(V.tensor_copy(row_of_slot[:], row_f[:]))
            order(V.tensor_copy(weight_of_slot[:], table[:, NS:2 * NS]))
            V.nop().then_inc(s_table, 1)

            def x_low(m, p):
                dve.wait_ge(s_xh[p], m + 1)
                V.tensor_tensor(xT_lo[p][:].rearrange("p c t -> p (c t)"), xT_ps[p][:],
                                xT_hi[p][:].rearrange("p c t -> p (c t)"), ALU.subtract).then_inc(s_xl[p], 1)

            def hidden_split(m, p):
                for b in range(4):
                    dve.wait_ge(s_h32[p], 4 * m + b + 1)
                    if b == 0:
                        free(dve, s_l2[p], m)
                    part = h32[:, b * 2 * R:(b + 1) * 2 * R]
                    hi, lo = (h[p][:, 2 * b:2 * b + 2, :].rearrange("p c t -> p (c t)") for h in (h_hi, h_lo))
                    V.tensor_copy(hi, part).then_inc(s_hh[p], 1)
                    dve.wait_ge(s_hh[p], 4 * m + b + 1)
                    V.tensor_tensor(lo, part, hi, ALU.subtract).then_inc(s_hl[p], 1)

            def result(m, p, i):
                e = dve.value_load(expert_of_tile[0:1, bass.ds(i, 1)], min_val=0, max_val=E - 1)
                dve.wait_ge(s_l2[p], m + 1)
                free(dve, s_added[1], 16 * (2 * m + p - 1))
                V.scalar_tensor_tensor(y[p], y_ps[p][:].rearrange("p (k d) -> p k d", k=2), 1 / WEIGHT_SCALE,
                                       b2_all[:, bass.ds(e, 1), :].to_broadcast([P, 2, D]), ALU.mult, ALU.add).then_inc(s_yb[p], 1)
                dve.wait_ge(s_yb[p], m + 1)
                for k in range(2):
                    last = V.tensor_scalar(y[p][:, k, :], y[p][:, k, :], weight_of_slot[:, bass.ds(2 * i + k, 1)], None, ALU.mult)
                last.then_inc(s_y[p], 1)

            x_low(0, 0)
            for m in range(HEAD):
                for p in range(2):
                    if 0 < 2 * m + p < E:
                        split_lo(dve, 2 * m + p)
                    x_low(m + p, 1 - p)
                    hidden_split(m, p)
                    if m + p > 0:
                        result(m - 1 + p, 1 - p, 2 * m + p - 1)
            with dve.Fori(HEAD, M - 1) as m:
                for p in range(2):
                    x_low(m + p, 1 - p)
                    hidden_split(m, p)
                    result(m - 1 + p, 1 - p, 2 * m + p - 1)
            x_low(M - 1, 1)
            hidden_split(M - 1, 0)
            result(M - 2, 1, NT - 3)
            hidden_split(M - 1, 1)
            result(M - 1, 0, NT - 2)
            result(M - 1, 1, NT - 1)


def this(engine, semaphores, m, p):
    engine.wait_ge(semaphores[p], m + 1)


def last(engine, semaphores, m, p):
    free(engine, semaphores[1 - p], m + p)


def attention(nc, name, x_all, x_sum, context, mask, wq, bq, wk, bk, wv, bv, wo, bo):
    B = x_all.shape[1]
    D = x_all.shape[2]
    DC = D // P
    H = 16
    DK = D // H
    HC = H // 2
    V1 = DK + 1
    QS = WEIGHT_SCALE * float(DK) ** 0.5
    assert D == 2 * P and DK == 16

    with ExitStack() as ctx:
        sem = ctx.enter_context(stage_semaphores(nc, name))

        def sb(n, shape, dt):
            return ctx.enter_context(nc.sbuf_tensor(f"{name}_{n}", shape, dt))

        def pb(n, shape, dt):
            return ctx.enter_context(nc.psum_tensor(f"{name}_{n}", shape, dt))

        def two(n):
            return [sem(f"{n}_{p}") for p in range(2)]

        c_in = [sb(f"c_in{p}", [P, D], F32) for p in range(2)]
        w_rows = sb("w_rows", [P, 4, DC, D], F32)
        wT_hi = sb("wT_hi", [P, 4, DC, D], F16)
        wT_lo = sb("wT_lo", [P, 4, DC, D], F16)
        kvT_hi = sb("kvT_hi", [P, DC, 2 * D], F16)
        kvT_lo = sb("kvT_lo", [P, DC, 2 * D], F16)
        biases = sb("biases", [P, 4, D], F32)
        mask_sb = sb("mask_sb", [P, P], I32)
        masked = sb("masked", [P, P], I32)
        tiny = sb("tiny", [P, P], F32)
        ident = sb("ident", [P, P], F32)
        ident16 = sb("ident16", [P, P], F16)
        stats = sb("stats", [P, B, 6], F32)
        mean_var = sb("mean_var", [P, B, 2], F32)
        rstd = sb("rstd", [P, B], F32)
        var = sb("var", [P, B], F32)
        rtmp = sb("rtmp", [P, B], F32)
        xn = sb("xn", [P, D], F32)
        inT_hi = sb("inT_hi", [P, 4, P], F16)
        inT_lo = sb("inT_lo", [P, 4, P], F16)
        q32 = sb("q32", [P, D], F32)
        k32 = sb("k32", [P, D], F32)
        v32 = [sb(f"v32_{i}", [P, H, V1], F32) for i in range(4)]
        q_parts = sb("q_parts", [P, H, 4, DK], F16)
        k_parts = sb("k_parts", [P, H, 4, DK], F16)
        qT = [sb(f"qT{p}", [P, HC, P], F16) for p in range(2)]
        kT = [sb(f"kT{p}", [P, HC, P], F16) for p in range(2)]
        top = sb("top", [P, H], F32)
        prob = sb("prob", [P, H, P], F32)
        probT = sb("probT", [P, H, P], F32)
        rsum = sb("rsum", [P, H], F32)
        o32 = sb("o32", [P, D], F32)
        oT_hi = sb("oT_hi", [P, DC, P], F16)
        oT_lo = sb("oT_lo", [P, DC, P], F16)

        S = pb("S", [P, 2, HC, P], F32)
        front = [pb(f"front{i}", [P, 512], F32) for i in range(2)]
        out_ps = pb("out_ps", [P, 512], F32)
        oT_ps = pb("oT_ps", [P, 512], F32)

        s_x = sem("x_loaded"); s_c = two("context_loaded"); s_w = sem("weights_loaded")
        s_pool = sem("pool_order"); s_dve = sem("dve_order"); s_const = sem("constants")
        s_var = sem("variance"); s_root = sem("root"); s_prep = sem("dve_prepared")
        s_wt = two("weights_transposed"); s_wh = two("weights_hi"); s_wl = two("weights_lo")
        s_xn = two("xn_ready"); s_xb = two("x_biased")
        s_tp = two("inputs_transposed"); s_th = two("inT_hi_ready"); s_tl = two("inT_lo_ready")
        s_kv = two("kv_product"); s_q = two("q_product")
        s_k32 = two("k32_ready"); s_v32 = two("v32_ready"); s_q32 = two("q32_ready")
        s_qh = two("q_high"); s_kh = two("k_high"); s_ql = two("q_low"); s_kl = two("k_low")
        s_qt = two("q_transposed"); s_kt = two("k_transposed"); s_qT = two("qT_ready"); s_kT = two("kT_ready")
        s_s = [two(f"scores{r}") for r in range(2)]
        s_top = [two(f"top{r}") for r in range(2)]; s_mask = [two(f"masked{r}") for r in range(2)]
        s_sub = [two(f"shifted{r}") for r in range(2)]; s_exp = [two(f"exp{r}") for r in range(2)]
        s_pt = [two(f"prob_transposed{r}") for r in range(2)]; s_pT = [two(f"probT{r}_ready") for r in range(2)]
        s_pv = two("pv_product"); s_rs = two("rsum_ready"); s_o = two("o32_ready")
        s_ot = two("o_transposed"); s_oh = two("oT_hi_ready"); s_ol = two("oT_lo_ready")
        s_out = two("out_product"); s_done = two("batch_done")

        s_go = sem("dve_goes_on")

        M = B // 2

        def slots(engine, slot):
            def run(group, i):
                def on(step, distance, *args):
                    j = i + distance
                    if isinstance(group, int) and not 0 <= 4 * group + j < B:
                        return
                    step(2 * group + j // 2, j % 2, j % 4, *args)
                slot(on)

            first, last_ = 1, B // 4 - 1
            for i in range(4):
                run(-1, i)
            for i in range(4):
                run(0, i)
            with engine.Fori(first, last_) as group:
                for i in range(4):
                    run(group, i)
            for i in range(8):
                run(last_, i)

        block = ctx.enter_context(nc.Block())

        @block.sync
        def _(sp):
            sp.dma_start(x_all[:], x_sum.rearrange("(t p) d -> p t d", p=P)).then_inc(s_x, 16)
            for i, w in enumerate((wq, wk, wv, wo)):
                sp.dma_start(w_rows[:, i], w.rearrange("(c p) d -> p c d", p=P)).then_inc(s_w, 16)
            for i, b in enumerate((bq, bk, bv, bo)):
                sp.dma_start(biases[:, i, :], broadcast_rows(b, P, D)).then_inc(s_w, 16)
            sp.dma_start(mask_sb[:], mask.rearrange("a b q k -> (a b q) k")).then_inc(s_w, 16)

            def load(m):
                for p in range(2):
                    free(sp, s_tp[p], m)
                    sp.dma_start(c_in[p][:], context[bass.ds((2 * m + p) * P, P), :]).then_inc(s_c[p], 16)

            each(sp, M, load)

        @block.gpsimd
        def _(pool):
            order = Order(pool, s_pool)
            order(nc.gpsimd.memset(ident[:], 0.0))
            order(nc.gpsimd.memset(ident16[:], 0.0))
            for i in (ident, ident16):
                nc.gpsimd.affine_select(out=i[:], in_=i[:], compare_op=ALU.not_equal, fill=1.0, base=0,
                                        pattern=[[-1, P]], channel_multiplier=1).then_inc(s_const, 1)
            nc.gpsimd.memset(tiny[:], 1e-09).then_inc(s_const, 1)
            for i in range(4):
                nc.gpsimd.memset(v32[i][:, :, DK:V1], 1.0).then_inc(s_const, 1)
            pool.wait_ge(s_w, 16 * 9)

            def batch(m, p):
                b = 2 * m + p
                this(pool, s_xn, m, p)
                row = x_all[:, bass.ds(b, 1), :].rearrange("p a d -> p (a d)")
                nc.gpsimd.tensor_tensor(row, row, biases[:, 3, :], ALU.add).then_inc(s_xb[p], 1)
                this(pool, s_qh, m, p)
                q2 = q32[:].rearrange("p (h d) -> p h d", h=H).unsqueeze(2).to_broadcast([P, H, 2, DK])
                nc.gpsimd.tensor_tensor(q_parts[:, :, 2:4, :], q2, q_parts[:, :, 0:2, :], ALU.subtract).then_inc(s_ql[p], 1)
                this(pool, s_kh, m, p)
                k2 = k32[:].rearrange("p (h d) -> p h d", h=H).unsqueeze(2).to_broadcast([P, H, 2, DK])
                nc.gpsimd.tensor_tensor(k_parts[:, :, 1:4:2, :], k2, k_parts[:, :, 0:4:2, :], ALU.subtract).then_inc(s_kl[p], 1)

            def pair(m):
                for p in range(2):
                    batch(m, p)

            each(pool, M, pair)

        @block.tensor
        def _(pe):
            pe.wait_ge(s_const, 7)
            pe.wait_ge(s_w, 16 * 9)
            for i in range(4):
                p = i % 2
                if i >= 2:
                    pe.wait_ge(s_wl[p], i // 2)
                for r in range(DC):
                    for c in range(DC):
                        mm = nc.tensor.transpose(front[p][:, (c * DC + r) * P:(c * DC + r + 1) * P],
                                                 w_rows[:, i, r, c * P:(c + 1) * P], ident[:])
                mm.then_inc(s_wt[p], 1)
            pe.wait_ge(s_prep, 1)

            def front_in(m, p, i):
                this(pe, s_xn, m, p)
                pe.wait_ge(s_c[p], 16 * (m + 1))
                last(pe, s_qT, m, p)
                for c in range(DC):
                    nc.tensor.transpose(front[0][:, c * P:(c + 1) * P], xn[:, c * P:(c + 1) * P], ident[:])
                for c in range(DC):
                    mm = nc.tensor.transpose(front[0][:, (2 + c) * P:(3 + c) * P], c_in[p][:, c * P:(c + 1) * P], ident[:])
                mm.then_inc(s_tp[p], 1)

            def front_products(m, p, i):
                this(pe, s_tl, m, p)
                last(pe, s_kT, m, p)
                for c in range(DC):
                    a_hi, a_lo = inT_hi[:, 2 + c, :], inT_lo[:, 2 + c, :]
                    nc.tensor.matmul(front[1][:], a_hi, kvT_hi[:, c, :], start=(c == 0), stop=False)
                    nc.tensor.matmul(front[1][:], a_hi, kvT_lo[:, c, :], start=False, stop=False)
                    mm = nc.tensor.matmul(front[1][:], a_lo, kvT_hi[:, c, :], start=False, stop=(c == DC - 1))
                mm.then_inc(s_kv[p], 1)
                for c in range(DC):
                    a_hi, a_lo = inT_hi[:, c, :], inT_lo[:, c, :]
                    out = front[0][:, 0:D]
                    nc.tensor.matmul(out, a_hi, wT_hi[:, 0, c, :], start=(c == 0), stop=False)
                    nc.tensor.matmul(out, a_hi, wT_lo[:, 0, c, :], start=False, stop=False)
                    mm = nc.tensor.matmul(out, a_lo, wT_hi[:, 0, c, :], start=False, stop=(c == DC - 1))
                mm.then_inc(s_q[p], 1)

            def front_transposes(m, p, i):
                this(pe, s_ql, m, p)
                for c in range(HC):
                    mm = nc.tensor.transpose(front[0][:].bitcast(F16)[:, c * P:(c + 1) * P],
                                             q_parts[:, 2 * c:2 * c + 2].rearrange("p h k d -> p (h k d)"), ident16[:])
                mm.then_inc(s_qt[p], 1)
                this(pe, s_kl, m, p)
                this(pe, s_v32, m, p)
                for c in range(HC):
                    mm = nc.tensor.transpose(front[1][:].bitcast(F16)[:, c * P:(c + 1) * P],
                                             k_parts[:, 2 * c:2 * c + 2].rearrange("p h k d -> p (h k d)"), ident16[:])
                mm.then_inc(s_kt[p], 1)

            def scores(m, p, i, r):
                if r == 0:
                    this(pe, s_qT, m, p)
                    this(pe, s_kT, m, p)
                last(pe, s_pT[r], m, p)
                rows = slice(64 * r, 64 * r + 64)
                for c in range(HC):
                    mm = nc.tensor.matmul(S[:, r, c, :], qT[p][rows, c, :], kT[p][rows, c, :], start=True, stop=True)
                mm.then_inc(s_s[r][p], 1)

            def prob_transposes(m, p, i, r):
                this(pe, s_exp[r], m, p)
                for c in range(HC):
                    mm = nc.tensor.transpose(S[:, r, c, :], prob[:, r * HC + c, :], ident[:])
                mm.then_inc(s_pt[r][p], 1)

            def value_products(m, p, i, r):
                if r == 0:
                    last(pe, s_o, m, p)
                this(pe, s_pT[r], m, p)
                for c in range(HC):
                    h = r * HC + c
                    mm = nc.tensor.matmul(out_ps[:, h * V1:(h + 1) * V1], probT[:, h, :], v32[i][:, 2 * c + r, :],
                                          start=True, stop=True)
                if r == 1:
                    mm.then_inc(s_pv[p], 1)

            def out_transposes(m, p, i):
                this(pe, s_o, m, p)
                last(pe, s_done, m, p)
                for c in range(DC):
                    mm = nc.tensor.transpose(oT_ps[:, c * P:(c + 1) * P], o32[:, c * P:(c + 1) * P], ident[:])
                mm.then_inc(s_ot[p], 1)

            def out_product(m, p, i):
                this(pe, s_ol, m, p)
                for c in range(DC):
                    out = oT_ps[:, D:2 * D]
                    nc.tensor.matmul(out, oT_hi[:, c, :], wT_hi[:, 3, c, :], start=(c == 0), stop=False)
                    nc.tensor.matmul(out, oT_hi[:, c, :], wT_lo[:, 3, c, :], start=False, stop=False)
                    mm = nc.tensor.matmul(out, oT_lo[:, c, :], wT_hi[:, 3, c, :], start=False, stop=(c == DC - 1))
                mm.then_inc(s_out[p], 1)

            def slot(on):
                on(front_products, 1)
                on(scores, 0, 0)
                on(front_transposes, 1)
                on(prob_transposes, -1, 1)
                on(out_transposes, -2)
                on(front_in, 2)
                on(value_products, -1, 0)
                on(scores, 0, 1)
                on(out_product, -2)
                on(prob_transposes, 0, 0)
                on(value_products, -1, 1)

            slots(pe, slot)

        @block.scalar
        def _(act):
            A = nc.scalar
            act.wait_ge(s_var, 1)
            A.activation(rstd[:], var[:], ACT.Sqrt).then_inc(s_root, 1)
            for i in range(4):
                p = i % 2
                act.wait_ge(s_wt[p], i // 2 + 1)
                A.activation(wT_hi[:, i].rearrange("p c d -> p (c d)"), front[p][:], ACT.Copy, scale=WEIGHT_SCALE).then_inc(s_wh[p], 1)

            def front_in(m, p, i):
                this(act, s_tp, m, p)
                A.activation(inT_hi[:].rearrange("p c t -> p (c t)"), front[0][:], ACT.Copy).then_inc(s_th[p], 1)

            def front_high(m, p, i):
                this(act, s_k32, m, p)
                k2 = k32[:].rearrange("p (h d) -> p h d", h=H).unsqueeze(2).to_broadcast([P, H, 2, DK])
                A.activation(k_parts[:, :, 0:4:2, :], k2, ACT.Copy).then_inc(s_kh[p], 1)
                this(act, s_q32, m, p)
                q2 = q32[:].rearrange("p (h d) -> p h d", h=H).unsqueeze(2).to_broadcast([P, H, 2, DK])
                A.activation(q_parts[:, :, 0:2, :], q2, ACT.Copy).then_inc(s_qh[p], 1)

            def query_copy(m, p, i):
                this(act, s_qt, m, p)
                A.activation(qT[p][:].rearrange("p c t -> p (c t)"), front[0][:].bitcast(F16), ACT.Copy).then_inc(s_qT[p], 1)

            def key_copy(m, p, i):
                this(act, s_kt, m, p)
                A.activation(kT[p][:].rearrange("p c t -> p (c t)"), front[1][:].bitcast(F16), ACT.Copy).then_inc(s_kT[p], 1)

            def exps(m, p, i, r):
                this(act, s_sub[r], m, p)
                part = prob[:, r * HC:(r + 1) * HC, :]
                A.activation(part, part, ACT.Exp).then_inc(s_exp[r][p], 1)

            def prob_copy(m, p, i, r):
                this(act, s_pt[r], m, p)
                A.activation(probT[:, r * HC:(r + 1) * HC, :], S[:, r], ACT.Copy).then_inc(s_pT[r][p], 1)

            def out_high(m, p, i):
                this(act, s_ot, m, p)
                A.activation(oT_hi[:].rearrange("p c t -> p (c t)"), oT_ps[:, 0:D], ACT.Copy).then_inc(s_oh[p], 1)

            def slot(on):
                on(exps, -1, 1)
                on(query_copy, 1)
                on(key_copy, 1)
                on(out_high, -2)
                on(prob_copy, -1, 1)
                on(front_in, 2)
                on(exps, 0, 0)
                on(prob_copy, 0, 0)
                on(front_high, 2)

            slots(act, slot)

        @block.vector
        def _(dve):
            V = nc.vector
            order = Order(dve, s_dve)
            dve.wait_ge(s_x, 16)
            layernorm_scales(dve, order, x_all, stats, mean_var, var, rstd, rtmp, s_var, s_root)
            dve.wait_ge(s_w, 16 * 9)
            for i in range(4):
                p = i % 2
                dve.wait_ge(s_wh[p], i // 2 + 1)
                V.scalar_tensor_tensor(wT_lo[:, i].rearrange("p c d -> p (c d)"), front[p][:], WEIGHT_SCALE,
                                       wT_hi[:, i].rearrange("p c d -> p (c d)"), ALU.mult, ALU.subtract).then_inc(s_wl[p], 1)
            for p in range(2):
                dve.wait_ge(s_wl[p], 2)
            for src, dst in ((wT_hi, kvT_hi), (wT_lo, kvT_lo)):
                for i in range(2):
                    order.tick(V.tensor_copy(dst[:, :, i * D:(i + 1) * D], src[:, 1 + i]))
            order.tick(V.tensor_scalar(biases[:, 0, :], biases[:, 0, :], 1 / float(DK) ** 0.5, None, ALU.mult))
            order(V.tensor_scalar(masked[:], mask_sb[:], 0, None, ALU.is_equal))
            V.nop().then_inc(s_prep, 1)
            dve.wait_ge(s_const, 7)

            def normalise(m, p, i):
                b = 2 * m + p
                last(dve, s_tp, m, p)
                V.tensor_scalar(xn[:], x_all[:, bass.ds(b, 1), :].rearrange("p a d -> p (a d)"),
                                mean_var[:, bass.ds(b, 1), 0], rstd[:, bass.ds(b, 1)], ALU.subtract, ALU.mult).then_inc(s_xn[p], 1)

            def front_low(m, p, i):
                this(dve, s_th, m, p)
                V.tensor_tensor(inT_lo[:].rearrange("p c t -> p (c t)"), front[0][:],
                                inT_hi[:].rearrange("p c t -> p (c t)"), ALU.subtract).then_inc(s_tl[p], 1)

            def front_bias(m, p, i):
                this(dve, s_kv, m, p)
                last(dve, s_kl, m, p)
                last(dve, s_ql, m, p)
                V.scalar_tensor_tensor(k32[:], front[1][:, 0:D], 1 / WEIGHT_SCALE, biases[:, 1, :], ALU.mult, ALU.add).then_inc(s_k32[p], 1)
                this(dve, s_q, m, p)
                V.scalar_tensor_tensor(q32[:], front[0][:, 0:D], 1 / QS, biases[:, 0, :], ALU.mult, ALU.add).then_inc(s_q32[p], 1)
                V.scalar_tensor_tensor(v32[i][:, :, 0:DK], front[1][:, D:2 * D].rearrange("p (h d) -> p h d", h=H), 1 / WEIGHT_SCALE,
                                       biases[:, 2, :].rearrange("p (h d) -> p h d", h=H), ALU.mult, ALU.add).then_inc(s_v32[p], 1)

            def softmax_shift(m, p, i, r):
                this(dve, s_s[r], m, p)
                wide = [P, HC, P]
                dve.sem_inc(s_go)
                V.copy_predicated(S[:, r], masked[:].unsqueeze(1).to_broadcast(wide),
                                  tiny[:].unsqueeze(1).to_broadcast(wide)).then_inc(s_mask[r][p], 1)
                this(dve, s_mask[r], m, p)
                tops = top[:, r * HC:(r + 1) * HC]
                V.tensor_reduce(tops, S[:, r], AX_X, ALU.max).then_inc(s_top[r][p], 1)
                this(dve, s_top[r], m, p)
                last(dve, s_pt[r], m, p)
                V.tensor_tensor(prob[:, r * HC:(r + 1) * HC, :], S[:, r], tops.unsqueeze(2).to_broadcast(wide),
                                ALU.subtract).then_inc(s_sub[r][p], 1)

            def divide(m, p, i):
                this(dve, s_pv, m, p)
                o = out_ps[:, 0:H * V1].rearrange("p (r c v) -> p r c v", r=2, v=V1)
                V.reciprocal(rsum[:].rearrange("p (r c) -> p r c", r=2), o[:, :, :, DK]).then_inc(s_rs[p], 1)
                this(dve, s_rs, m, p)
                last(dve, s_ot, m, p)
                V.tensor_tensor(o32[:].rearrange("p (c r d) -> p r c d", r=2, d=DK), o[:, :, :, 0:DK],
                                rsum[:].rearrange("p (r c) -> p r c", r=2).unsqueeze(3).to_broadcast([P, 2, HC, DK]),
                                ALU.mult).then_inc(s_o[p], 1)

            def out_low(m, p, i):
                this(dve, s_oh, m, p)
                V.tensor_tensor(oT_lo[:].rearrange("p c t -> p (c t)"), oT_ps[:, 0:D],
                                oT_hi[:].rearrange("p c t -> p (c t)"), ALU.subtract).then_inc(s_ol[p], 1)

            def finish(m, p, i):
                b = 2 * m + p
                this(dve, s_out, m, p)
                this(dve, s_xb, m, p)
                row = x_all[:, bass.ds(b, 1), :].rearrange("p a d -> p (a d)")
                V.scalar_tensor_tensor(row, oT_ps[:, D:2 * D], 1 / WEIGHT_SCALE, row, ALU.mult, ALU.add).then_inc(s_done[p], 1)

            def slot(on):
                on(softmax_shift, 0, 0)
                on(out_low, -2)
                on(front_low, 2)
                on(normalise, 3)
                on(softmax_shift, 0, 1)
                on(finish, -2)
                on(divide, -1)
                on(front_bias, 2)

            slots(dve, slot)
            for p in range(2):
                dve.wait_ge(s_done[p], M)


def gated_ffn(nc, name, x_all, w_gate, w_up, w_down, up_raw, out):
    T, D = x_all.shape[1], x_all.shape[2]
    tokens = T * P
    I = w_gate.shape[0]
    DC, IC = D // P, I // P
    BLOCK = 32
    WQMAX = 7.0
    QMAX = 2.0**15 - 1
    N = 512
    TG = tokens // N
    COLS = IC * tokens
    CB = 1024
    STEPS = COLS // CB
    NP = 2 * IC
    BANKS = 4

    with ExitStack() as ctx:
        sem = ctx.enter_context(stage_semaphores(nc, name))

        def sb(n, shape, dt):
            return ctx.enter_context(nc.sbuf_tensor(f"{name}_{n}", shape, dt))

        def pb(n, shape, dt):
            return ctx.enter_context(nc.psum_tensor(f"{name}_{n}", shape, dt))

        def two(n):
            return [sem(f"{n}_{p}") for p in range(2)]

        act_all = sb("act_all", [P, IC, tokens], F32)
        flat = act_all[:].rearrange("p c t -> p (c t)")
        y_all = flat[:, 0:T * D].rearrange("p (t d) -> p t d", d=D)
        W = IC * D
        rows = [flat[:, T * D + i * W:T * D + (i + 1) * W] for i in range(3)]
        scaled = [flat[:, T * D + (3 + i) * W:T * D + (4 + i) * W] for i in range(3)]
        yT_hi = sb("yT_hi", [P, DC, tokens], F16)
        yT_lo = sb("yT_lo", [P, DC, tokens], F16)
        guT_hi = sb("guT_hi", [P, 2, DC, I], F16)
        guT_lo = sb("guT_lo", [P, 2, DC, I], F16)
        dT_hi = sb("dT_hi", [P, IC, D], F16)
        dT_lo = sb("dT_lo", [P, IC, D], F16)
        ident = sb("ident", [P, P], F32)
        round_c = sb("round_c", [P, 1], F32)
        round_u = sb("round_u", [P, 1], F32)
        stats = sb("stats", [P, T, 6], F32)
        mean_var = sb("mean_var", [P, T, 2], F32)
        rstd = sb("rstd", [P, T], F32)
        var = sb("var", [P, T], F32)
        rtmp = sb("rtmp", [P, T], F32)
        NB = W // BLOCK
        b_scale = sb("b_scale", [P, 3, NB], F32)
        b_inv = sb("b_inv", [P, 3, NB], F32)
        maxes = sb("maxes", [P, NP, TG], F32)
        step_max = sb("step_max", [P, max(STEPS, T)], F32)
        largest = sb("largest", [P, 4, 2], F32)
        reduced = sb("reduced", [P, 4, 2], F32)
        scale = sb("scale", [P, 5], F32)
        to_int = sb("to_int", [P, 5], F32)
        tmp = sb("tmp", [P, 5], F32)
        unit = sb("unit", [P, 3], F32)
        u_out = [sb(f"u_out{p}", [P, N], F32) for p in range(2)]
        work = [[sb(f"work{i}{p}", [P, CB], F32) for p in range(2)] for i in range(2)]
        later = yT_hi[:].rearrange("p c t -> p (c t)").bitcast(F32)
        o_parts = yT_lo[:].rearrange("p c t -> p (c t)")

        ps = [pb(f"ps{i}", [P, N], F32) for i in range(8)]

        s_w = [sem(f"rows{i}_loaded") for i in range(3)]
        s_const = sem("constants"); s_pool = sem("pool_order"); s_dve = sem("dve_order")
        s_var = sem("variance"); s_root = sem("root")
        s_deq = sem("weights_dequantised"); s_wt = two("weights_transposed"); s_wh = two("weights_hi"); s_wl = two("weights_lo")
        s_big = sem("largest_ready"); s_red = sem("largest_reduced"); s_scale = sem("scales_ready")
        s_t = two("x_rounded"); s_q = two("x_quantised"); s_qt = two("x_transposed"); s_qh = two("yT_hi_ready"); s_ql = two("yT_lo_ready")
        s_pr = [sem(f"product_in_bank{i}") for i in range(BANKS)]; s_ev = [sem(f"bank{i}_copied") for i in range(BANKS)]
        s_mx = [sem(f"bank{i}_max_taken") for i in range(BANKS)]
        s_us = two("up_stored")
        s_2 = {k: two("sig_" + k) for k in ("t", "int", "sigmoid", "shift", "sig", "product", "max")}
        s_3 = {k: two("up_" + k) for k in ("loaded", "t", "int", "tu", "product", "max")}
        s_4 = {k: two("down_" + k) for k in ("t", "int", "hi", "lo", "product", "out", "stored")}

        def weight_groups(i):
            if i < 2:
                return [[c * D + d * P for c in range(c0, c0 + 2) for d in range(DC)] for c0 in range(0, IC, 2)]
            return [[r * I + c * P for c in range(c0, c0 + 2) for r in range(DC)] for c0 in range(0, IC, 2)]

        def weight_parts(i, j, w, d):
            if i < 2:
                return w[:, i, :, 2 * j * P:2 * (j + 1) * P].rearrange("p r (c q) -> p c r q", q=P)
            return d[:, 2 * j:2 * j + 2, :].rearrange("p c (r q) -> p c r q", q=P)

        def down_parts(p):
            n = IC * P
            return [o_parts[:, (2 * h + p) * n:(2 * h + p + 1) * n].rearrange("p (c t) -> p c t", c=IC) for h in range(2)]

        s_go = sem("act_goes_on")

        block = ctx.enter_context(nc.Block())

        @block.sync
        def _(sp):
            for i, w in enumerate((w_gate, w_up)):
                sp.dma_start(rows[i].rearrange("p (c d) -> p c d", d=D), w.rearrange("(c p) d -> p c d", p=P)).then_inc(s_w[i], 16)
            sp.dma_start(rows[2].rearrange("p (c i) -> p c i", i=I), w_down.rearrange("(c p) i -> p c i", p=P)).then_inc(s_w[2], 16)


            def up_out(g):
                for c in range(IC):
                    k = IC + c
                    sp.wait_ge(s_ev[k % BANKS], (NP // BANKS) * g + k // BANKS + 1)
                    sp.dma_start(up_raw[:, c, bass.ds(g * N, N)], u_out[c % 2][:]).then_inc(s_us[c % 2], 16)

            each(sp, TG, up_out)
            for p in range(2):
                sp.wait_ge(s_us[p], 16 * TG * IC // 2)
            up_flat = up_raw.rearrange("p c t -> p (c t)")

            def up_in(m):
                for p in range(2):
                    free(sp, s_3["tu"][p], m)
                    sp.dma_start(later[:, (2 + p) * CB:(3 + p) * CB], up_flat[:, bass.ds((2 * m + p) * CB, CB)]).then_inc(s_3["loaded"][p], 16)

            each(sp, STEPS // 2, up_in)

            def result_out(m):
                for p in range(2):
                    sp.wait_ge(s_4["out"][p], m + 1)
                    sp.dma_start(out[bass.ds((2 * m + p) * P, P), :], u_out[p][:, 0:D]).then_inc(s_4["stored"][p], 16)

            each(sp, T // 2, result_out)
            for p in range(2):
                sp.wait_ge(s_4["stored"][p], 16 * T // 2)

        @block.gpsimd
        def _(pool):
            order = Order(pool, s_pool)
            order(nc.gpsimd.memset(ident[:], 0.0))
            nc.gpsimd.affine_select(out=ident[:], in_=ident[:], compare_op=ALU.not_equal, fill=1.0, base=0,
                                    pattern=[[-1, P]], channel_multiplier=1).then_inc(s_const, 1)
            nc.gpsimd.memset(round_c[:], ROUND).then_inc(s_const, 1)
            nc.gpsimd.memset(round_u[:], 2.0**23).then_inc(s_const, 1)

            def all_max(n):
                pool.wait_ge(s_big, n + 1)
                nc.gpsimd.partition_all_reduce(reduced[:, n, :], largest[:, n, :], P, bass.bass_isa.ReduceOp.max).then_inc(s_red, 1)

            all_max(0)
            all_max(1)

            def multiply_sigmoid(m):
                for p in range(2):
                    this(pool, s_2["sig"], m, p)
                    part = flat[:, bass.ds((2 * m + p) * CB, CB)]
                    nc.gpsimd.tensor_tensor(part, part, work[1][p][:], ALU.mult).then_inc(s_2["product"][p], 1)

            each(pool, STEPS // 2, multiply_sigmoid)
            all_max(2)
            all_max(3)

        @block.tensor
        def _(pe):
            pe.wait_ge(s_const, 3)

            def weights(i, n, parts):
                p = n % 2
                if n >= 2:
                    pe.wait_ge(s_wl[p], n // 2)
                for j, part in enumerate(parts):
                    mm = nc.tensor.transpose(ps[p][:, j * P:(j + 1) * P], part, ident[:])
                mm.then_inc(s_wt[p], 1)

            n = 0
            for i in range(3):
                pe.wait_ge(s_deq, i + 1)
                for group in weight_groups(i):
                    weights(i, n, [scaled[i][:, a:a + P] for a in group])
                    n += 1

            def tokens_in(m, p):
                this(pe, s_q, m, p)
                free(pe, s_ql[p], m)
                for t in range(2):
                    for c in range(DC):
                        mm = nc.tensor.transpose(ps[2 + p][:, (2 * c + t) * P:(2 * c + t + 1) * P],
                                                 work[0][p][:, t * D + c * P:t * D + (c + 1) * P], ident[:])
                mm.then_inc(s_qt[p], 1)

            def tokens_group(m):
                for p in range(2):
                    tokens_in(m, p)

            each(pe, T // 4, tokens_group)
            for p in range(2):
                pe.wait_ge(s_ql[p], T // 4)
                pe.wait_ge(s_wl[p], (n + 1 - p) // 2)

            def products(g):
                y_at = [[y[:, c, bass.ds(g * N, N)] for c in range(DC)] for y in (yT_hi, yT_lo)]
                for k in range(NP):
                    b = k % BANKS
                    free(pe, s_ev[b], (NP // BANKS) * g + k // BANKS)
                    i, c0 = divmod(k, IC)
                    for c in range(DC):
                        hi, lo = (w[:, i, c, c0 * P:(c0 + 1) * P] for w in (guT_hi, guT_lo))
                        nc.tensor.matmul(ps[4 + b][:], hi, y_at[0][c], start=(c == 0), stop=False)
                        nc.tensor.matmul(ps[4 + b][:], hi, y_at[1][c], start=False, stop=False)
                        mm = nc.tensor.matmul(ps[4 + b][:], lo, y_at[0][c], start=False, stop=(c == DC - 1))
                    mm.then_inc(s_pr[b], 1)

            each(pe, TG, products)

            def down_products(m):
                for p in range(2):
                    this(pe, s_4["lo"], m, p)
                    free(pe, s_4["out"][p], m)
                    hi, lo = down_parts(p)
                    for c in range(IC):
                        nc.tensor.matmul(ps[p][:, 0:D], hi[:, c, :], dT_hi[:, c, :], start=(c == 0), stop=False)
                        nc.tensor.matmul(ps[p][:, 0:D], hi[:, c, :], dT_lo[:, c, :], start=False, stop=False)
                        mm = nc.tensor.matmul(ps[p][:, 0:D], lo[:, c, :], dT_hi[:, c, :], start=False, stop=(c == IC - 1))
                    mm.then_inc(s_4["product"][p], 1)

            each(pe, T // 2, down_products)

        @block.scalar
        def _(act):
            A = nc.scalar
            act.wait_ge(s_var, 1)
            A.activation(rstd[:], var[:], ACT.Sqrt).then_inc(s_root, 1)
            n = 0
            for i in range(3):
                for j in range(IC // 2):
                    p = n % 2
                    act.wait_ge(s_wt[p], n // 2 + 1)
                    bank = ps[p][:].rearrange("p (c r q) -> p c r q", c=2, r=DC)
                    A.activation(weight_parts(i, j, guT_hi, dT_hi), bank, ACT.Copy, scale=WEIGHT_SCALE).then_inc(s_wh[p], 1)
                    n += 1
            act.wait_ge(s_const, 3)
            act.wait_ge(s_scale, 1)

            def round_input(m, p):
                free(act, s_qt[p], m)
                act.sem_inc(s_go)
                A.activation(work[0][p][:, 0:2 * D], flat[:, bass.ds((2 * m + p) * 2 * D, 2 * D)], ACT.Identity,
                             bias=round_c[:], scale=to_int[:, 0:1]).then_inc(s_t[p], 1)

            def input_high(m, p):
                this(act, s_qt, m, p)
                act.sem_inc(s_go)
                t0 = (2 * m + p) * 2 * P
                A.activation(yT_hi[:, :, bass.ds(t0, 2 * P)], ps[2 + p][:].rearrange("p (c t) -> p c t", c=DC),
                             ACT.Copy).then_inc(s_qh[p], 1)

            staggered(act, T // 2, (round_input, 1), (input_high, 0))

            def copy_products(g):
                for k in range(NP):
                    b = k % BANKS
                    act.wait_ge(s_pr[b], (NP // BANKS) * g + k // BANKS + 1)
                    if k < IC:
                        dst = act_all[:, k, bass.ds(g * N, N)]
                    else:
                        c = k - IC
                        free(act, s_us[c % 2], 16 * ((IC // 2) * g + c // 2))
                        if c >= 2:
                            act.wait_ge(s_mx[(k - 2) % BANKS], (NP // BANKS) * g + (k - 2) // BANKS + 1)
                        else:
                            k2 = NP - 2 + c
                            free(act, s_mx[k2 % BANKS], (NP // BANKS) * (g - 1) + k2 // BANKS + 1)
                        dst = u_out[c % 2][:]
                    A.activation(dst, ps[4 + b][:], ACT.Copy).then_inc(s_ev[b], 1)

            each(act, TG, copy_products)

            act.wait_ge(s_scale, 2)

            def round_gate(m, p):
                free(act, s_2["sig"][p], m)
                act.sem_inc(s_go)
                part = flat[:, bass.ds((2 * m + p) * CB, CB)]
                A.activation(work[0][p][:], part, ACT.Identity, bias=round_c[:], scale=to_int[:, 1:2]).then_inc(s_2["t"][p], 1)

            def sigmoid(m, p):
                this(act, s_2["int"], m, p)
                free(act, s_2["product"][p], m)
                act.sem_inc(s_go)
                part = flat[:, bass.ds((2 * m + p) * CB, CB)]
                A.activation(work[1][p][:], part, ACT.Sigmoid, scale=scale[:, 1:2]).then_inc(s_2["sigmoid"][p], 1)
                this(act, s_2["sigmoid"], m, p)
                A.activation(work[0][p][:], work[1][p][:], ACT.Identity, bias=round_u[:], scale=2.0**16).then_inc(s_2["shift"][p], 1)

            staggered(act, STEPS, (round_gate, 1), (sigmoid, 0))

            act.wait_ge(s_scale, 3)

            def scale_up_steps(m):
                for p in range(2):
                    part = flat[:, bass.ds((2 * m + p) * CB, CB)]
                    free(act, s_3["int"][p], m)
                    act.sem_inc(s_go)
                    A.activation(work[0][p][:], part, ACT.Identity, bias=round_c[:], scale=to_int[:, 3:4]).then_inc(s_3["t"][p], 1)
                    free(act, s_3["product"][p], m)
                    act.wait_ge(s_3["loaded"][p], 16 * (m + 1))
                    A.activation(work[1][p][:], later[:, (2 + p) * CB:(3 + p) * CB], ACT.Identity, bias=round_c[:],
                                 scale=to_int[:, 2:3]).then_inc(s_3["tu"][p], 1)

            each(act, STEPS // 2, scale_up_steps)

            act.wait_ge(s_scale, 4)

            def round_product(m, p):
                free(act, s_4["int"][p], m)
                act.sem_inc(s_go)
                A.activation(work[0][p][:, 0:IC * P].rearrange("p (c t) -> p c t", c=IC), act_all[:, :, bass.ds((2 * m + p) * P, P)],
                             ACT.Identity, bias=round_c[:], scale=to_int[:, 4:5]).then_inc(s_4["t"][p], 1)

            def product_high(m, p):
                this(act, s_4["int"], m, p)
                free(act, s_4["product"][p], m)
                A.activation(down_parts(p)[0].rearrange("p c t -> p (c t)"), work[1][p][:, 0:IC * P], ACT.Copy).then_inc(s_4["hi"][p], 1)

            staggered(act, T, (round_product, 1), (product_high, 0))

        @block.vector
        def _(dve):
            V = nc.vector
            order = Order(dve, s_dve)
            layernorm_scales(dve, order, x_all, stats, mean_var, var, rstd, rtmp, s_var, s_root)
            for t in range(T):
                order.tick(V.tensor_scalar(y_all[:, t, :], x_all[:, t, :], mean_var[:, t, 0:1], rstd[:, t:t + 1],
                                           ALU.subtract, ALU.mult))
            order.tick(V.memset(largest[:], 0.0))
            order.wait()
            order(V.tensor_reduce(step_max[:, 0:T], y_all, AX_X, ALU.max, apply_absolute_value=True))
            V.tensor_reduce(largest[:, 0, 0:1], step_max[:, 0:T], AX_X, ALU.max).then_inc(s_big, 1)

            for i in range(3):
                dve.wait_ge(s_w[i], 16)
                blocks = rows[i].rearrange("p (b k) -> p b k", k=BLOCK)
                to = scaled[i].rearrange("p (b k) -> p b k", k=BLOCK)
                s, inv = b_scale[:, i, :], b_inv[:, i, :]
                order(V.tensor_reduce(s, blocks, AX_X, ALU.max, apply_absolute_value=True))
                order(V.tensor_scalar(s, s, 1 / WQMAX, 1e-12, ALU.mult, ALU.max))
                order(V.reciprocal(inv, s))
                order(V.tensor_tensor(to, blocks, inv.unsqueeze(2).to_broadcast([P, NB, BLOCK]), ALU.mult))
                order(V.tensor_scalar(to, to, ROUND, -ROUND, ALU.add, ALU.add))
                V.tensor_tensor(to, to, s.unsqueeze(2).to_broadcast([P, NB, BLOCK]), ALU.mult).then_inc(s_deq, 1)
            n = 0
            for i in range(3):
                for j in range(IC // 2):
                    p = n % 2
                    dve.wait_ge(s_wh[p], n // 2 + 1)
                    bank = ps[p][:].rearrange("p (c r q) -> p c r q", c=2, r=DC)
                    for c in range(2):
                        ins = V.scalar_tensor_tensor(weight_parts(i, j, guT_lo, dT_lo)[:, c], bank[:, c], WEIGHT_SCALE,
                                                     weight_parts(i, j, guT_hi, dT_hi)[:, c], ALU.mult, ALU.subtract)
                    ins.then_inc(s_wl[p], 1)
                    n += 1

            def new_scale(n, col, unit):
                big = reduced[:, n, col:col + 1]
                c = {0: 0, 1: 1 + col, 2: 3, 3: 4}[n]
                if unit is not None:
                    order(V.tensor_scalar(tmp[:, c:c + 1], big, unit, None, ALU.mult))
                    big = tmp[:, c:c + 1]
                order(V.tensor_scalar(scale[:, c:c + 1], big, 1 / QMAX, 1e-12, ALU.mult, ALU.max))
                order(V.reciprocal(to_int[:, c:c + 1], scale[:, c:c + 1]))
                if unit is not None:
                    order(V.tensor_scalar(to_int[:, c:c + 1], to_int[:, c:c + 1], unit, None, ALU.mult))

            dve.wait_ge(s_red, 1)
            new_scale(0, 0, None)
            V.nop().then_inc(s_scale, 1)

            def input_integers(m, p):
                this(dve, s_t, m, p)
                V.tensor_scalar(work[0][p][:, 0:2 * D], work[0][p][:, 0:2 * D], -ROUND, None, ALU.add).then_inc(s_q[p], 1)

            def input_low(m, p):
                this(dve, s_qh, m, p)
                t0 = (2 * m + p) * 2 * P
                V.tensor_tensor(yT_lo[:, :, bass.ds(t0, 2 * P)], ps[2 + p][:].rearrange("p (c t) -> p c t", c=DC),
                                yT_hi[:, :, bass.ds(t0, 2 * P)], ALU.subtract).then_inc(s_ql[p], 1)

            staggered(dve, T // 2, (input_integers, 1), (input_low, 0))

            def product_maxima(g):
                for k in range(NP):
                    b = k % BANKS
                    dve.wait_ge(s_ev[b], (NP // BANKS) * g + k // BANKS + 1)
                    src = act_all[:, k, bass.ds(g * N, N)] if k < IC else u_out[k % 2][:]
                    V.tensor_reduce(maxes[:, k, bass.ds(g, 1)], src, AX_X, ALU.max, apply_absolute_value=True).then_inc(s_mx[b], 1)

            each(dve, TG, product_maxima)
            for b in range(BANKS):
                dve.wait_ge(s_mx[b], TG * NP // BANKS)
            order(V.tensor_scalar(unit[:, 0:1], scale[:, 0:1], 1 / WEIGHT_SCALE, None, ALU.mult))
            V.tensor_reduce(largest[:, 1, :], maxes[:].rearrange("p (i c) g -> p i (c g)", i=2), AX_X, ALU.max).then_inc(s_big, 1)
            dve.wait_ge(s_red, 2)
            new_scale(1, 0, unit[:, 0:1])
            new_scale(1, 1, unit[:, 0:1])
            V.nop().then_inc(s_scale, 1)

            def gate_integers(m, p):
                this(dve, s_2["t"], m, p)
                V.tensor_scalar(flat[:, bass.ds((2 * m + p) * CB, CB)], work[0][p][:], -ROUND, None, ALU.add).then_inc(s_2["int"][p], 1)

            def sigmoid_integers(m, p):
                this(dve, s_2["shift"], m, p)
                V.tensor_scalar(work[1][p][:], work[0][p][:], 2.0**23 + 65535.0, -2.0**23, ALU.min, ALU.add).then_inc(s_2["sig"][p], 1)

            def gate_maximum(m, p):
                this(dve, s_2["product"], m, p)
                V.tensor_reduce(step_max[:, bass.ds(2 * m + p, 1)], flat[:, bass.ds((2 * m + p) * CB, CB)], AX_X, ALU.max,
                                apply_absolute_value=True).then_inc(s_2["max"][p], 1)

            staggered(dve, STEPS, (gate_integers, 1), (sigmoid_integers, 0), (gate_maximum, -1))
            for p in range(2):
                dve.wait_ge(s_2["max"][p], STEPS // 2)
            order(V.tensor_scalar(unit[:, 1:2], scale[:, 1:2], 2.0**-16, None, ALU.mult))
            V.tensor_reduce(largest[:, 2, 0:1], step_max[:, 0:STEPS], AX_X, ALU.max).then_inc(s_big, 1)
            dve.wait_ge(s_red, 3)
            new_scale(2, 0, unit[:, 1:2])
            V.nop().then_inc(s_scale, 1)

            def part(m, p):
                return flat[:, bass.ds((2 * m + p) * CB, CB)]

            def gated_integers(m, p):
                this(dve, s_3["t"], m, p)
                V.tensor_scalar(part(m, p), work[0][p][:], -ROUND, None, ALU.add).then_inc(s_3["int"][p], 1)

            def multiply_up(m, p):
                this(dve, s_3["tu"], m, p)
                this(dve, s_3["int"], m, p)
                V.scalar_tensor_tensor(part(m, p), work[1][p][:], -ROUND, part(m, p), ALU.add, ALU.mult).then_inc(s_3["product"][p], 1)

            def product_maximum(m, p):
                this(dve, s_3["product"], m, p)
                V.tensor_reduce(step_max[:, bass.ds(2 * m + p, 1)], part(m, p), AX_X, ALU.max, apply_absolute_value=True).then_inc(s_3["max"][p], 1)

            staggered(dve, STEPS, (gated_integers, 1), (multiply_up, 0), (product_maximum, -1))
            for p in range(2):
                dve.wait_ge(s_3["max"][p], STEPS // 2)
            order(V.tensor_tensor(unit[:, 2:3], scale[:, 2:3], scale[:, 3:4], ALU.mult))
            V.tensor_reduce(largest[:, 3, 0:1], step_max[:, 0:STEPS], AX_X, ALU.max).then_inc(s_big, 1)
            dve.wait_ge(s_red, 4)
            new_scale(3, 0, unit[:, 2:3])
            order(V.tensor_scalar(tmp[:, 4:5], scale[:, 4:5], 1 / WEIGHT_SCALE, None, ALU.mult))
            V.nop().then_inc(s_scale, 1)

            def product_integers(m, p):
                this(dve, s_4["t"], m, p)
                free(dve, s_4["lo"][p], m)
                V.tensor_scalar(work[1][p][:, 0:IC * P], work[0][p][:, 0:IC * P], -ROUND, None, ALU.add).then_inc(s_4["int"][p], 1)

            def product_low(m, p):
                this(dve, s_4["hi"], m, p)
                V.tensor_tensor(down_parts(p)[1].rearrange("p c t -> p (c t)"), work[1][p][:, 0:IC * P],
                                down_parts(p)[0].rearrange("p c t -> p (c t)"), ALU.subtract).then_inc(s_4["lo"][p], 1)

            def add_to_x(m, p):
                this(dve, s_4["product"], m, p)
                free(dve, s_4["stored"][p], 16 * m)
                V.scalar_tensor_tensor(u_out[p][:, 0:D], ps[p][:, 0:D], tmp[:, 4:5],
                                       x_all[:, bass.ds(2 * m + p, 1), :].rearrange("p a d -> p (a d)"), ALU.mult, ALU.add).then_inc(s_4["out"][p], 1)

            staggered(dve, T, (product_integers, 1), (product_low, 0), (add_to_x, -1))


def two_layers(nc, x, context, mask, e2, e1, attn, ffn, out):
    tokens, D = x.shape
    E = e1["wg"].shape[1]
    I = ffn["w_gate"].shape[0]
    x_sum = nc.dram_tensor("x_sum", (tokens + P, D), F32, kind="Internal").ap()
    normed = nc.dram_tensor("normed", (tokens + P, D), F32, kind="Internal").ap()
    up_raw = nc.dram_tensor("up_raw", (P, I // P, tokens), F32, kind="Internal").ap()
    experts(nc, "top2", x, context, e2["wg"], e2["bg"], e2["w1"], e2["b1"], e2["w2"], e2["b2"], x_sum, normed, 2, None)
    experts(nc, "top1", x_sum[0:tokens], None, e1["wg"], None, e1["w1"], e1["b1"], e1["w2"], e1["b2"], x_sum, normed, 1,
            tokens // E)
    with nc.sbuf_tensor("x_held", [P, tokens // P, D], F32) as x_held:
        attention(nc, "attn", x_held, x_sum[0:tokens], context, mask, **attn)
        gated_ffn(nc, "ffn", x_held, ffn["w_gate"], ffn["w_up"], ffn["w_down"], up_raw, out)


NAMES = ["x", "ctx_1024", "mask_1x1xSxS2_ik1",
         "L0_xattn_Wg", "L0_xattn_bg", "L0_xattn_W1", "L0_xattn_b1", "L0_xattn_W2", "L0_xattn_b2",
         "L0_ffn_wg", "L0_ffn_w1", "L0_ffn_b1", "L0_ffn_w2", "L0_ffn_b2",
         "L1_xattn_wq_w", "L1_xattn_wq_b", "L1_xattn_wk_w", "L1_xattn_wk_b",
         "L1_xattn_wv_w", "L1_xattn_wv_b", "L1_xattn_wo_w", "L1_xattn_wo_b",
         "L1_ffn_w_gate", "L1_ffn_w_up", "L1_ffn_w_down"]


def kernel(**inputs):
    import numpy as np
    import concourse.bacc as bacc
    from concourse.bass_utils import run_bass_kernel_spmd

    nc = bacc.Bacc("TRN2", target_bir_lowering=False, num_devices=1)
    arrays, a = {}, {}
    for name in NAMES:
        array = np.ascontiguousarray(inputs[name])
        arrays[f"in_{name}"] = array
        a[name] = nc.dram_tensor(f"in_{name}", array.shape, mybir.dt.from_np(array.dtype), kind="ExternalInput").ap()
    shape = inputs["x"].shape
    out = nc.dram_tensor("out", shape, F32, kind="ExternalOutput").ap()
    rows = [t.rearrange("b s d -> (b s) d") for t in (a["x"], a["ctx_1024"], out)]
    two_layers(nc, rows[0], rows[1], a["mask_1x1xSxS2_ik1"],
               {k.lower(): a[f"L0_xattn_{k}"] for k in ("Wg", "bg", "W1", "b1", "W2", "b2")},
               {k: a[f"L0_ffn_{k}"] for k in ("wg", "w1", "b1", "w2", "b2")},
               {k[0:2] if k[3] == "w" else "b" + k[1]: a[f"L1_xattn_{k}"]
                for k in ("wq_w", "wq_b", "wk_w", "wk_b", "wv_w", "wv_b", "wo_w", "wo_b")},
               {k: a[f"L1_ffn_{k}"] for k in ("w_gate", "w_up", "w_down")},
               rows[2])
    result = run_bass_kernel_spmd(nc, [arrays], core_ids=[0])
    return result.results[0]["out"]
```
